# Optimizing a Trainium2 kernel written in Bass

```python
import numpy as np
import jax
import jax.numpy as jnp

def _softmax(x, axis=-1):
    return jax.nn.softmax(x, axis=axis)

def _gelu(x):
    return jax.nn.gelu(x, approximate=True)

def _silu(x):
    return jax.nn.silu(x)

def _sigmoid(x):
    return jax.nn.sigmoid(x)

def _layernorm(x, axis=-1, eps=1e-05):
    m = jnp.mean(x, axis=axis, keepdims=True)
    v = jnp.var(x, axis=axis, keepdims=True)
    return (x - m) / jnp.sqrt(v + eps)

def _scatter_add(tgt, idx, src, axis=0):
    return tgt.at[idx].add(src)

def _segment_sum(src, seg, n):
    return jax.ops.segment_sum(src, seg, n)
kernel_name = 'mk_decoder_preln_d2_seqx_r8_6fa470'

def setup_inputs(seed: int=0):
    np.random.seed(seed)
    _w = jnp.asarray

    def _rec_inputs():
        import jax
        import jax.numpy as jnp
        _rk = jax.random.key(seed)
        x = -0.0003929 + 0.9999 * jax.random.normal(jax.random.fold_in(_rk, 1), (16, 64, 128), jnp.float32)
        _lenS = 64 - jax.random.randint(jax.random.fold_in(_rk, 7), (16,), 0, max(1, 64 // 4) + 1, jnp.int32)
        _lenS2 = 64 - jax.random.randint(jax.random.fold_in(_rk, 8), (16,), 0, max(1, 64 // 4) + 1, jnp.int32)
        _ctx_768P = jax.random.normal(jax.random.fold_in(_rk, 11), (16, 16, 96), jnp.float32)
        _ctx_768c = jax.random.dirichlet(jax.random.fold_in(_rk, 511), 0.3 * jnp.ones((16,), jnp.float32), (16, 64))
        _ctx_768t = jnp.einsum('bsk,bkd->bsd', _ctx_768c, _ctx_768P)
        _ctx_768t = _ctx_768t * jax.lax.rsqrt(jnp.mean(jnp.square(_ctx_768t)) + 1e-12) * 0.953939
        ctx_768 = -7.36909e-05 + 0.999899 * (_ctx_768t + 0.3 * jax.random.normal(jax.random.fold_in(_rk, 611), (16, 64, 96), jnp.float32))
        _validS = jnp.arange(64)[None, :] < _lenS[:, None]
        _validS2 = jnp.arange(64)[None, :] < _lenS2[:, None]
        _causal = jnp.tril(jnp.ones((64, 64), dtype=bool))
        mask_BxS2_bk0 = jnp.logical_not(jnp.broadcast_to(_validS2[:, :], (16, 64)))
        return (x, ctx_768, mask_BxS2_bk0)
    x, ctx_768, mask_BxS2_bk0 = _rec_inputs()

    def _L0_attn_setup():
        import jax, jax.numpy as jnp
        import numpy as np
        B, S, E, H = (2, 256, 128, 16)
        key = jax.random.key(seed)
        k1, k2 = jax.random.split(key)
        inputs = jax.random.normal(k1, (B, S, E), dtype=jnp.float32)
        qkv_kernel = jax.random.normal(k2, (E, 3 * E), dtype=jnp.float32) * (1.0 / np.sqrt(E))
        qkv_bias = jnp.zeros((1, 3 * E), dtype=jnp.float32)
        return {'inputs': inputs, 'qkv_kernel': qkv_kernel, 'qkv_bias': qkv_bias}
    _L0_attn_all = _L0_attn_setup()
    _L0_attn_in = {k: v for k, v in _L0_attn_all.items() if k in ('qkv_kernel', 'qkv_bias')}
    del _L0_attn_all

    def _L0_xattn_setup():
        import jax, jax.numpy as jnp
        import numpy as np
        IMG_DIM, TXT_DIM, HID = (128, 96, 128)
        B, LQ, LK = (8, 256, 256)
        key = jax.random.key(seed)
        ks = jax.random.split(key, 8)
        s_img = 1.0 / np.sqrt(IMG_DIM)
        s_txt = 1.0 / np.sqrt(TXT_DIM)
        return {'image_features': jax.random.normal(ks[0], (B, LQ, IMG_DIM), jnp.float32), 'text_features': jax.random.normal(ks[1], (B, LK, TXT_DIM), jnp.float32), 'Wq': jax.random.uniform(ks[2], (IMG_DIM, HID), jnp.float32, -s_img, s_img), 'bq': jax.random.uniform(ks[3], (HID,), jnp.float32, -s_img, s_img), 'Wk': jax.random.uniform(ks[4], (TXT_DIM, HID), jnp.float32, -s_txt, s_txt), 'bk': jax.random.uniform(ks[5], (HID,), jnp.float32, -s_txt, s_txt), 'Wv': jax.random.uniform(ks[6], (TXT_DIM, HID), jnp.float32, -s_txt, s_txt), 'bv': jax.random.uniform(ks[7], (HID,), jnp.float32, -s_txt, s_txt)}
    _L0_xattn_all = _L0_xattn_setup()
    _L0_xattn_in = {k: v for k, v in _L0_xattn_all.items() if k in ('Wq', 'bq', 'Wk', 'bk', 'Wv', 'bv')}
    del _L0_xattn_all

    def _L0_ffn_setup():
        import jax, jax.numpy as jnp
        import numpy as np
        from jax import lax
        D_MODEL = 128
        INTER = 128
        N_EXPERTS = 8
        TOP_K = 2
        ROUTE_SCALE = 1.0
        B, S = (2, 512)
        key = jax.random.key(seed)
        ks = jax.random.split(key, 16)
        sc_d = 1.0 / np.sqrt(D_MODEL)
        sc_f = 1.0 / np.sqrt(INTER)
        inp = {'x': jax.random.normal(ks[0], (B, S, D_MODEL), dtype=jnp.float32), 'gate_w': jax.random.normal(ks[1], (N_EXPERTS, D_MODEL), dtype=jnp.float32) * sc_d, 'w1': jax.random.normal(ks[2], (N_EXPERTS, D_MODEL, INTER), dtype=jnp.float32) * sc_d, 'b1': jnp.zeros((N_EXPERTS, INTER), dtype=jnp.float32), 'w2': jax.random.normal(ks[3], (N_EXPERTS, INTER, D_MODEL), dtype=jnp.float32) * sc_f, 'b2': jnp.zeros((N_EXPERTS, D_MODEL), dtype=jnp.float32), 'w3': jax.random.normal(ks[4], (N_EXPERTS, D_MODEL, INTER), dtype=jnp.float32) * sc_d, 'b3': jnp.zeros((N_EXPERTS, INTER), dtype=jnp.float32), 'sw1': jax.random.normal(ks[5], (D_MODEL, INTER), dtype=jnp.float32) * sc_d, 'sb1': jnp.zeros((INTER,), dtype=jnp.float32), 'sw2': jax.random.normal(ks[6], (INTER, D_MODEL), dtype=jnp.float32) * sc_f, 'sb2': jnp.zeros((D_MODEL,), dtype=jnp.float32), 'sw3': jax.random.normal(ks[7], (D_MODEL, INTER), dtype=jnp.float32) * sc_d, 'sb3': jnp.zeros((INTER,), dtype=jnp.float32)}
        return inp
    _L0_ffn_all = _L0_ffn_setup()
    _L0_ffn_in = {k: v for k, v in _L0_ffn_all.items() if k in ('gate_w', 'w1', 'b1', 'w2', 'b2', 'w3', 'b3', 'sw1', 'sb1', 'sw2', 'sb2', 'sw3', 'sb3')}
    del _L0_ffn_all

    def _L1_attn_setup():
        import jax, jax.numpy as jnp
        import numpy as np
        LN_EPS = 1e-05
        CLAMP = 1000000.0
        key = jax.random.key(seed)
        k0, k1, k2, k3 = jax.random.split(key, 4)
        Bsz, L, D, N = (8, 256, 128, 32)
        x = jax.random.normal(k0, (Bsz, L, D), dtype=jnp.float32)
        A = jax.random.normal(k1, (N, N), dtype=jnp.float32) * 0.01
        B = jax.random.normal(k2, (N, D), dtype=jnp.float32) * 0.01
        C = jax.random.normal(k3, (D, N), dtype=jnp.float32) * 0.01
        gamma = jnp.ones((D,), dtype=jnp.float32)
        beta = jnp.zeros((D,), dtype=jnp.float32)
        return {'x': x, 'A': A, 'B': B, 'C': C, 'gamma': gamma, 'beta': beta}
    _L1_attn_all = _L1_attn_setup()
    _L1_attn_in = {k: v for k, v in _L1_attn_all.items() if k in ('A', 'B', 'C', 'gamma', 'beta')}
    del _L1_attn_all

    def _L1_xattn_setup():
        import jax, jax.numpy as jnp
        import numpy as np
        HEADS = 8
        DIM_HEAD = 64
        QUERY_DIM = 128
        CONTEXT_DIM = 96
        INNER = HEADS * DIM_HEAD
        key = jax.random.key(seed)
        ks = jax.random.split(key, 8)
        b, n, j = (4, 256, 256)
        x = jax.random.normal(ks[0], (b, n, QUERY_DIM), dtype=jnp.float32)
        context = jax.random.normal(ks[1], (b, j, CONTEXT_DIM), dtype=jnp.float32)
        mask = jax.random.randint(ks[2], (b, j), 0, 2).astype(jnp.bool_)
        W_q = jax.random.normal(ks[3], (QUERY_DIM, INNER), dtype=jnp.float32) / np.sqrt(QUERY_DIM)
        W_k = jax.random.normal(ks[4], (CONTEXT_DIM, INNER), dtype=jnp.float32) / np.sqrt(CONTEXT_DIM)
        W_v = jax.random.normal(ks[5], (CONTEXT_DIM, INNER), dtype=jnp.float32) / np.sqrt(CONTEXT_DIM)
        W_o = jax.random.normal(ks[6], (INNER, QUERY_DIM), dtype=jnp.float32) / np.sqrt(INNER)
        b_o = jax.random.normal(ks[7], (QUERY_DIM,), dtype=jnp.float32) * 0.01
        return {'x': x, 'context': context, 'mask': mask, 'W_q': W_q, 'W_k': W_k, 'W_v': W_v, 'W_o': W_o, 'b_o': b_o}
    _L1_xattn_all = _L1_xattn_setup()
    _L1_xattn_in = {k: v for k, v in _L1_xattn_all.items() if k in ('W_q', 'W_k', 'W_v', 'W_o', 'b_o')}
    del _L1_xattn_all

    def _L1_ffn_setup():
        import jax, jax.numpy as jnp
        import numpy as np
        key = jax.random.key(seed)
        k0, k1, k2, k3 = jax.random.split(key, 4)
        B, S, D, F, E = (8, 256, 128, 256, 8)
        x = jax.random.normal(k0, (B, S, D), dtype=jnp.float32)
        Wg = jax.random.normal(k1, (D, E), dtype=jnp.float32) * 0.02
        W1 = jax.random.normal(k2, (E, D, F), dtype=jnp.float32) * 0.02
        W2 = jax.random.normal(k3, (E, F, D), dtype=jnp.float32) * 0.02
        return {'x': x, 'Wg': Wg, 'W1': W1, 'W2': W2}
    _L1_ffn_all = _L1_ffn_setup()
    _L1_ffn_in = {k: v for k, v in _L1_ffn_all.items() if k in ('Wg', 'W1', 'W2')}
    del _L1_ffn_all
    return {'x': x, 'ctx_768': ctx_768, 'mask_BxS2_bk0': mask_BxS2_bk0, 'L0_attn_qkv_kernel': _L0_attn_in['qkv_kernel'], 'L0_attn_qkv_bias': _L0_attn_in['qkv_bias'], 'L0_xattn_Wq': _L0_xattn_in['Wq'], 'L0_xattn_bq': _L0_xattn_in['bq'], 'L0_xattn_Wk': _L0_xattn_in['Wk'], 'L0_xattn_bk': _L0_xattn_in['bk'], 'L0_xattn_Wv': _L0_xattn_in['Wv'], 'L0_xattn_bv': _L0_xattn_in['bv'], 'L0_ffn_gate_w': _L0_ffn_in['gate_w'], 'L0_ffn_w1': _L0_ffn_in['w1'], 'L0_ffn_b1': _L0_ffn_in['b1'], 'L0_ffn_w2': _L0_ffn_in['w2'], 'L0_ffn_b2': _L0_ffn_in['b2'], 'L0_ffn_w3': _L0_ffn_in['w3'], 'L0_ffn_b3': _L0_ffn_in['b3'], 'L0_ffn_sw1': _L0_ffn_in['sw1'], 'L0_ffn_sb1': _L0_ffn_in['sb1'], 'L0_ffn_sw2': _L0_ffn_in['sw2'], 'L0_ffn_sb2': _L0_ffn_in['sb2'], 'L0_ffn_sw3': _L0_ffn_in['sw3'], 'L0_ffn_sb3': _L0_ffn_in['sb3'], 'L1_attn_A': _L1_attn_in['A'], 'L1_attn_B': _L1_attn_in['B'], 'L1_attn_C': _L1_attn_in['C'], 'L1_attn_gamma': _L1_attn_in['gamma'], 'L1_attn_beta': _L1_attn_in['beta'], 'L1_xattn_W_q': _L1_xattn_in['W_q'], 'L1_xattn_W_k': _L1_xattn_in['W_k'], 'L1_xattn_W_v': _L1_xattn_in['W_v'], 'L1_xattn_W_o': _L1_xattn_in['W_o'], 'L1_xattn_b_o': _L1_xattn_in['b_o'], 'L1_ffn_Wg': _L1_ffn_in['Wg'], 'L1_ffn_W1': _L1_ffn_in['W1'], 'L1_ffn_W2': _L1_ffn_in['W2']}

def reference(x, ctx_768, mask_BxS2_bk0, L0_attn_qkv_kernel, L0_attn_qkv_bias, L0_xattn_Wq, L0_xattn_bq, L0_xattn_Wk, L0_xattn_bk, L0_xattn_Wv, L0_xattn_bv, L0_ffn_gate_w, L0_ffn_w1, L0_ffn_b1, L0_ffn_w2, L0_ffn_b2, L0_ffn_w3, L0_ffn_b3, L0_ffn_sw1, L0_ffn_sb1, L0_ffn_sw2, L0_ffn_sb2, L0_ffn_sw3, L0_ffn_sb3, L1_attn_A, L1_attn_B, L1_attn_C, L1_attn_gamma, L1_attn_beta, L1_xattn_W_q, L1_xattn_W_k, L1_xattn_W_v, L1_xattn_W_o, L1_xattn_b_o, L1_ffn_Wg, L1_ffn_W1, L1_ffn_W2):
    import jax
    import jax.numpy as jnp

    def _L0_attn_ref(inputs, qkv_kernel, qkv_bias):
        import jax, jax.numpy as jnp
        import numpy as np
        B, S, E, H = (2, 256, 128, 16)
        b, s, e = inputs.shape
        hidden, heads = (E, H)
        qkv = jnp.einsum('bse,ef->bsf', inputs, qkv_kernel) + qkv_bias
        qkv_heads = qkv.reshape(b, heads, s, -1)
        q, k, v = jnp.split(qkv_heads, 3, axis=-1)
        scale = 1.0 / np.sqrt(2.0 * hidden)
        qk = jnp.einsum('bhse,bhte->bhst', q, k) * scale
        mask = jnp.triu(jnp.full((s, s), -jnp.inf, dtype=jnp.float32), k=1)
        attn = jax.nn.softmax(qk + mask, axis=-1)
        out = jnp.einsum('bhst,bhte->bhse', attn, v).reshape(b, s, e)
        return out

    def _L0_xattn_ref(image_features, text_features, Wq, bq, Wk, bk, Wv, bv):
        import jax, jax.numpy as jnp
        import numpy as np
        IMG_DIM, TXT_DIM, HID = (128, 96, 128)
        B, LQ, LK = (8, 256, 256)
        query = jnp.einsum('bqi,ih->bqh', image_features, Wq) + bq
        key = jnp.einsum('bkt,th->bkh', text_features, Wk) + bk
        value = jnp.einsum('bkt,th->bkh', text_features, Wv) + bv
        scale = 1.0 / jnp.sqrt(jnp.asarray(HID, query.dtype))
        scores = jnp.einsum('bqh,bkh->bqk', query, key) * scale
        weights = jax.nn.softmax(scores, axis=-1)
        attended = jnp.einsum('bqk,bkh->bqh', weights, value)
        return attended

    def _L0_ffn_ref(x, gate_w, w1, b1, w2, b2, w3, b3, sw1, sb1, sw2, sb2, sw3, sb3):
        import jax, jax.numpy as jnp
        import numpy as np
        from jax import lax
        D_MODEL = 128
        INTER = 128
        N_EXPERTS = 8
        TOP_K = 2
        ROUTE_SCALE = 1.0
        B, S = (2, 512)
        Bx, Sx, D = x.shape
        xt = x.reshape(-1, D)
        scores = jax.nn.softmax((xt @ gate_w.T).astype(jnp.float32), axis=-1)
        top_vals, top_idx = lax.top_k(scores, TOP_K)
        weights = (top_vals * ROUTE_SCALE).astype(x.dtype)
        combine = jnp.sum(jax.nn.one_hot(top_idx, N_EXPERTS, dtype=x.dtype) * weights[..., None], axis=1)

        def body(acc, p):
            W1, B1, W2, B2, W3, B3, c = p
            h = jax.nn.silu(xt @ W1 + B1) * (xt @ W3 + B3)
            return (acc + c[:, None] * (h @ W2 + B2), None)
        y, _ = lax.scan(body, jnp.zeros_like(xt), (w1, b1, w2, b2, w3, b3, combine.T))
        z = jax.nn.silu(xt @ sw1 + sb1) * (xt @ sw3 + sb3) @ sw2 + sb2
        return (y + z).reshape(Bx, Sx, D)

    def _L1_attn_ref(x, A, B, C, gamma, beta):
        import jax, jax.numpy as jnp
        import numpy as np
        LN_EPS = 1e-05
        CLAMP = 1000000.0
        Bsz = x.shape[0]
        N = A.shape[0]
        uB = jnp.einsum('bld,nd->lbn', x, B)

        def step(state, u_t):
            s = state @ A.T + u_t
            return (s, s)
        init = jnp.zeros((Bsz, N), dtype=x.dtype)
        _, states = jax.lax.scan(step, init, uB)
        y = jnp.einsum('lbn,dn->bld', states, C)
        act = jax.nn.gelu(y, approximate=False)
        mean = jnp.mean(act, axis=-1, keepdims=True)
        var = jnp.var(act, axis=-1, keepdims=True)
        norm = (act - mean) / jnp.sqrt(var + LN_EPS) * gamma + beta
        return jnp.nan_to_num(norm, nan=0.0, posinf=CLAMP, neginf=-CLAMP)

    def _L1_xattn_ref(x, context, mask, W_q, W_k, W_v, W_o, b_o):
        import jax, jax.numpy as jnp
        import numpy as np
        HEADS = 8
        DIM_HEAD = 64
        QUERY_DIM = 128
        CONTEXT_DIM = 96
        INNER = HEADS * DIM_HEAD
        b, n, _ = x.shape
        j = context.shape[1]
        scale = DIM_HEAD ** (-0.5)
        q = (x @ W_q).reshape(b, n, HEADS, DIM_HEAD)
        k = (context @ W_k).reshape(b, j, HEADS, DIM_HEAD)
        v = (context @ W_v).reshape(b, j, HEADS, DIM_HEAD)
        sim = jnp.einsum('bihd,bjhd->bhij', q, k) * scale
        max_neg = -jnp.finfo(sim.dtype).max
        sim = jnp.where(mask[:, None, None, :], sim, max_neg)
        attn = jax.nn.softmax(sim, axis=-1)
        out = jnp.einsum('bhij,bjhd->bihd', attn, v).reshape(b, n, INNER)
        return out @ W_o + b_o

    def _L1_ffn_ref(x, Wg, W1, W2):
        import jax, jax.numpy as jnp
        import numpy as np
        B, S, D = x.shape
        E = Wg.shape[1]
        T = B * S
        cap = max(1, T // E)
        xt = x.reshape(T, D)
        logits = xt @ Wg
        probs = jax.nn.softmax(logits, axis=-1)
        pT = probs.T
        _, top_idx = jax.lax.top_k(pT, cap)
        sel = jnp.zeros((E, T), dtype=bool).at[jnp.arange(E)[:, None], top_idx].set(True)
        masked = jnp.where(sel, pT, -jnp.inf)
        assigned = sel.any(axis=0)
        tok2exp = jnp.where(assigned, jnp.argmax(masked, axis=0), jnp.argmax(pT, axis=0))
        weights = jnp.take_along_axis(probs, tok2exp[:, None], axis=1)[:, 0]
        out = jnp.zeros_like(xt)
        for e in range(E):
            gate = jnp.where(tok2exp == e, weights, 0.0)
            h = jax.nn.gelu(xt @ W1[e], approximate=False) @ W2[e]
            out = out + gate[:, None] * h
        return out.reshape(B, S, D)
    x = x + _L0_attn_ref(_layernorm(x, axis=-1), L0_attn_qkv_kernel, L0_attn_qkv_bias)
    x = x + _L0_xattn_ref(_layernorm(x, axis=-1), ctx_768, L0_xattn_Wq, L0_xattn_bq, L0_xattn_Wk, L0_xattn_bk, L0_xattn_Wv, L0_xattn_bv)
    x = x + _L0_ffn_ref(_layernorm(x, axis=-1), L0_ffn_gate_w, L0_ffn_w1, L0_ffn_b1, L0_ffn_w2, L0_ffn_b2, L0_ffn_w3, L0_ffn_b3, L0_ffn_sw1, L0_ffn_sb1, L0_ffn_sw2, L0_ffn_sb2, L0_ffn_sw3, L0_ffn_sb3)
    x = x + _L1_attn_ref(_layernorm(x, axis=-1), L1_attn_A, L1_attn_B, L1_attn_C, L1_attn_gamma, L1_attn_beta)
    x = x + _L1_xattn_ref(_layernorm(x, axis=-1), ctx_768, mask_BxS2_bk0, L1_xattn_W_q, L1_xattn_W_k, L1_xattn_W_v, L1_xattn_W_o, L1_xattn_b_o)
    x = x + _L1_ffn_ref(_layernorm(x, axis=-1), L1_ffn_Wg, L1_ffn_W1, L1_ffn_W2)
    return x

_drawn_inputs = setup_inputs


def setup_inputs(seed=0):
    import zlib

    import numpy as np

    out = dict(_drawn_inputs(seed))
    spreads = {'L0_attn_qkv_bias': (0.0, 0.1),
     'L0_ffn_b1': (0.0, 0.384),
     'L0_ffn_b2': (0.0, 0.1),
     'L0_ffn_b3': (0.0, 0.391),
     'L0_ffn_sb1': (0.0, 0.1),
     'L0_ffn_sb2': (0.0, 0.1),
     'L0_ffn_sb3': (0.0, 0.1),
     'L1_attn_gamma': (1.0, 0.2),
     'L1_attn_beta': (0.0, 0.1)}
    factors = {'L0_xattn_bq': 8.0,
     'L0_xattn_bk': 8.0,
     'L1_xattn_b_o': 8.0,
     'L1_ffn_Wg': 8.0,
     'L1_ffn_W1': 8.0,
     'L1_ffn_W2': 8.0}
    for name, (base, spread) in spreads.items():
        noise = np.random.default_rng([zlib.crc32(name.encode()), seed]).standard_normal(out[name].shape)
        drawn = base * np.exp(spread * noise) if base else spread * noise
        out[name] = jnp.asarray(drawn.astype(out[name].dtype))
    for name, factor in factors.items():
        out[name] = (out[name] * factor).astype(out[name].dtype)
    return out
```

```python
import concourse.bass as bass
from concourse import mybir
from contextlib import ExitStack


def decoder_kernel(nc: bass.Bass, w, out):
    fp32 = mybir.dt.float32
    bf16 = mybir.dt.bfloat16
    int32 = mybir.dt.int32
    uint8 = mybir.dt.uint8
    ALU = mybir.AluOpType
    ACT = mybir.ActivationFunctionType
    AX = mybir.AxisListType

    B, S, D = w["x"].shape
    DC = w["ctx_768"].shape[2]
    P = 128
    NT = B * S // P
    N = B * S
    HALF = N // 2
    EPS = 1e-5

    CH, HD = 16, 8
    GT = S // CH
    NPAIR = S // (2 * GT)
    VW = 2 * HD + 1
    ATTN_SCALE = 1.0 / (2.0 * D) ** 0.5
    XATTN0_SCALE = 1.0 / float(D) ** 0.5
    H1, DH1 = 8, 64
    XATTN1_SCALE = DH1 ** -0.5
    NHP = H1 // 2
    E0 = 8
    E1 = 8
    F1 = w["L1_ffn_W1"].shape[2] // P
    CAP = N // E1
    NS = 32
    BQ = P // NS
    ROUNDS = 6
    CLAMP = 1.0e6
    BITS, STEP = 30, 2
    NC = 2 ** STEP - 1

    ctx = ExitStack()
    with ctx:
        def sb(name, shape, dt=fp32):
            return ctx.enter_context(nc.sbuf_tensor(name, shape, dt))

        def sem(name):
            return ctx.enter_context(nc.semaphore(name))

        def per_row(ap, n):
            return ap.unsqueeze(2).broadcast_to([ap.shape[0], ap.shape[1], n])

        bank = [ctx.enter_context(nc.psum_tensor(f"bank{i}", [P, 512], fp32)) for i in range(8)]

        X = sb("X", [P, NT, D])
        XN = sb("XN", [P, NT, D])
        XT = sb("XT", [P, N])
        stats = sb("stats", [P, NT, 6])
        mv = sb("mv", [P, NT, 2])
        rs = sb("rs", [P, 6, NT])
        CTX = sb("CTX", [P, NT, DC])
        CTXT = sb("CTXT", [DC, N])
        ident = sb("ident", [P, P])
        identb = sb("identb", [P, P], bf16)
        causal = sb("causal", [P, NPAIR, S], bf16)
        onesb = sb("onesb", [P, P], bf16)
        trib = sb("trib", [P, P], bf16)
        em8 = sb("em8", [P, NT, E0])
        jconst = sb("jconst", [P, NC, E1], int32)
        magic = sb("magic", [P, NT], int32)
        vecs = sb("vecs", [31, P])
        cols = sb("cols", [P, 31])
        Wqkv = sb("Wqkv", [P, 3 * D])
        Wp = sb("Wp", [P, 3, D])
        Wq0 = sb("Wq0", [P, D])
        Wk0 = sb("Wk0", [DC, D])
        Wv0 = sb("Wv0", [DC, D])
        bv0 = sb("bv0", [P, D])
        W1a = sb("W1a", [P, E0 + 1, D])
        W3a = sb("W3a", [P, E0 + 1, D])
        W2a = sb("W2a", [P, E0 + 1, D])
        b2a = sb("b2a", [E0 + 1, D])
        Bn = sb("Bn", [NS, D])
        Cn = sb("Cn", [P, BQ, NS])
        BT = sb("BT", [P, NS])
        CT = sb("CT", [P, D])
        Apow = sb("Apow", [P, ROUNDS, 2, P])
        gamma = sb("gamma", [P, D])
        beta = sb("beta", [P, D])
        bo = sb("bo", [P, D])
        Wq1 = sb("Wq1", [P, H1 * DH1])
        Wk1 = sb("Wk1", [DC, H1 * DH1])
        Wv1 = sb("Wv1", [DC, H1 * DH1])
        Wo1 = sb("Wo1", [P, NHP, D])
        Wg = sb("Wg", [P, E1])
        Wb = sb("Wb", [P, 2 * E1 * F1 * P])
        W1b = Wb[:, 0:E1 * F1 * P].rearrange("p (e f) -> p e f", e=E1)
        W2b = Wb[:, E1 * F1 * P:].rearrange("p (e k d) -> p e k d", e=E1, d=D)
        Qr = Wb[:, :].rearrange("p (t c) -> p t c", c=CH)
        masku = sb("masku", [P, N], uint8)
        maskf = sb("maskf", [P, N])
        maskrow = sb("maskrow", [1, N], bf16)
        QKVT = sb("QKVT", [P, 3, N])
        big = sb("big", [P, 2 * CH * N // 4])
        Q2 = big[:, 0:CH * N // 4].rearrange("p (c t) -> p c t", c=CH)
        K2 = big[:, CH * N // 4:].rearrange("p (c t) -> p c t", c=CH)
        ys = big[:, :].rearrange("p (e t d) -> p e t d", e=E1, d=D)
        V2 = sb("V2", [P, CH, S])
        VB = B * NPAIR * VW
        att = sb("att", [P, VB + 2 * N])
        Vb = att[:, 0:VB].rearrange("p (b q r v) -> p b q r v", b=B, r=2, v=VW)
        mx0 = sb("mx0", [P, B, NPAIR])
        Es = sb("Es", [P, 3, 512])
        PTs = sb("PTs", [P, 2, 512])
        rO = sb("rO", [P, 8, 2, NPAIR])
        Opos = att[:, VB:VB + N].rearrange("p (a b e) -> p a b e", b=B, e=HD)
        OT2 = att[:, VB + N:VB + 2 * N].rearrange("p (c s) -> p c s", s=S)
        V2r = att[:, VB + N:VB + 2 * N].rearrange("p (q g r t c) -> p q g r t c", g=2, r=2, t=GT, c=CH)
        OT = sb("OT", [P, N])
        K0T = sb("K0T", [P, N])
        V0 = sb("V0", [P, NT, D])
        K1T = sb("K1T", [P, NHP, N])
        V1 = sb("V1", [P, NT, H1 * DH1])
        hid = att[:, 0:4 * N].rearrange("p (a b n) -> p a b n", a=2, b=2)
        Q1T = hid[:, :, :, :].rearrange("p a b n -> p (a b) n")
        sm = sb("sm", [P, NT, 3, 8])
        OTs = V2[:, :, :].rearrange("p c s -> p (c s)").rearrange("p (a h n) -> p a h n", a=2, n=P)
        rt = sb("rt", [P, 12, NT, E0])
        rv = sb("rv", [P, 8, NT])
        comb = sb("comb", [P, NT, E0 + 1])
        combT = OT[0:E0 + 1, :]
        thr = sb("thr", [P, E1], int32)
        cand = sb("cand", [P, NC, E1], int32)
        hit = sb("hit", [P, NC * E1, NT], bf16)
        cnt = sb("cnt", [P, NC, E1])
        acc = sb("acc", [P, NC, E1])
        add = sb("add", [P, E1], int32)
        eqb = sb("eqb", [P, NT, E1], bf16)
        ST = sb("ST", [P, BQ, S])
        GA = QKVT[:, 0, :].rearrange("p (t d) -> p t d", d=D)
        GB = QKVT[:, 1, :].rearrange("p (t d) -> p t d", d=D)
        nanm = QKVT[:, 2, :].bitcast(int32).rearrange("p (t d) -> p t d", d=D)

        qkv_d = nc.dram_tensor("qkv_scratch", [3, P, N], fp32).ap()
        o_d = nc.dram_tensor("o_scratch", [P, CH * S], fp32).ap()

        ld_x = sem("ld_x")
        ld_ctx = sem("ld_ctx")
        ld_vecs = sem("ld_vecs")
        ld_qkv = sem("ld_qkv")
        ld_x0 = sem("ld_x0")
        ld_mask = sem("ld_mask")
        ld_ssm = sem("ld_ssm")
        ld_abd = sem("ld_abd")
        ld_x1 = sem("ld_x1")
        ld_f0 = sem("ld_f0")
        ld_f1 = sem("ld_f1")
        ld_rows = sem("ld_rows")
        c_zero = sem("c_zero")
        c_ident = sem("c_ident")
        c_azero = sem("c_azero")
        c_misc0 = sem("c_misc0")
        c_misc = sem("c_misc")
        v_step = sem("v_step")
        xn_ready = sem("xn_ready")
        xt_psum = sem("xt_psum")
        xt_act = sem("xt_act")
        xt_dve = sem("xt_dve")
        prep_psum = sem("prep_psum")
        prep_act = sem("prep_act")
        prep_dve = sem("prep_dve")
        mask_ready = sem("mask_ready")
        k1_psum = sem("k1_psum")
        k1_ready = sem("k1_ready")
        v1_psum = sem("v1_psum")
        v1_ready = sem("v1_ready")
        pow_psum = sem("pow_psum")
        pow_ready = sem("pow_ready")
        qkv_psum = sem("qkv_psum")
        qkv_act = sem("qkv_act")
        qkv_dve = sem("qkv_dve")
        st_q = sem("st_q")
        st_k = sem("st_k")
        st_v = sem("st_v")
        ld_q2 = sem("ld_q2")
        ld_v2 = sem("ld_v2")
        v2_psum = sem("v2_psum")
        vb_act = sem("vb_act")
        vb_dve = sem("vb_dve")
        w_split = sem("w_split")
        q_zero = sem("q_zero")
        q_act = sem("q_act")
        q_dve = sem("q_dve")
        v_side = sem("v_side")
        a_scores = sem("a_scores")
        a_sub = sem("a_sub")
        a_exp = sem("a_exp")
        a_tr = sem("a_tr")
        a_trc = sem("a_trc")
        a_pv = sem("a_pv")
        a_norm = sem("a_norm")
        o_psum = sem("o_psum")
        o_act = sem("o_act")
        o_dve = sem("o_dve")
        st_o = sem("st_o")
        ld_o = sem("ld_o")
        x_psum = sem("x_psum")
        x_added = sem("x_added")
        b_q = sem("b_q")
        b_qc = sem("b_qc")
        b_scores = sem("b_scores")
        b_sub = sem("b_sub")
        b_exp = sem("b_exp")
        b_prob = sem("b_prob")
        b_tr = sem("b_tr")
        b_trc = sem("b_trc")
        b_pv = sem("b_pv")
        b_added = sem("b_added")
        g_psum = sem("g_psum")
        g_sub = sem("g_sub")
        g_exp = sem("g_exp")
        g_comb = sem("g_comb")
        g_combt = sem("g_combt")
        g_combc = sem("g_combc")
        f_h1 = sem("f_h1")
        f_h3 = sem("f_h3")
        f_silu = sem("f_silu")
        f_h = sem("f_h")
        f_out = sem("f_out")
        f_acc = sem("f_acc")
        s_psum = sem("s_psum")
        s_state = sem("s_state")
        s_y = sem("s_y")
        s_gelu = sem("s_gelu")
        s_added = sem("s_added")
        c_q = sem("c_q")
        c_qact = sem("c_qact")
        c_qdve = sem("c_qdve")
        c_scores = sem("c_scores")
        c_sub = sem("c_sub")
        c_exp = sem("c_exp")
        c_prob = sem("c_prob")
        c_tr = sem("c_tr")
        c_trc = sem("c_trc")
        c_pv = sem("c_pv")
        c_otc = sem("c_otc")
        c_wo = sem("c_wo")
        c_added = sem("c_added")
        r_psum = sem("r_psum")
        r_sub = sem("r_sub")
        r_exp = sem("r_exp")
        r_hit = sem("r_hit")
        r_cnt = sem("r_cnt")
        r_eq = sem("r_eq")
        r_pre = sem("r_pre")
        m_up = sem("m_up")
        m_gelu = sem("m_gelu")
        m_down = sem("m_down")
        m_ys = sem("m_ys")
        m_done = sem("m_done")
        st_out = sem("st_out")

        block = ctx.enter_context(nc.Block())

        def seq(k):
            return 4 * (k % 4) + k // 4

        @block.sync
        def _(sp):
            def tokens(ap):
                return ap.rearrange("b s d -> (b s) d").rearrange("(t p) d -> p t d", p=P)

            sp.dma_start(X[:, :, :], tokens(w["x"])).then_inc(ld_x, 16)
            sp.dma_start(CTX[:, :, :], tokens(w["ctx_768"])).then_inc(ld_ctx, 16)
            for part in range(3):
                sp.dma_start(vecs[part:part + 1, :].rearrange("o (c e) -> o c e", e=HD),
                             w["L0_attn_qkv_bias"].rearrange("o (c s e) -> o c s e", s=3, e=HD)[:, :, part, :]
                             ).then_inc(ld_vecs, 16)
            for row, name in ((3, "L0_xattn_bq"), (4, "L0_xattn_bk"), (13, "L0_ffn_sb1"), (22, "L0_ffn_sb3")):
                sp.dma_start(vecs[row:row + 1, :], w[name].unsqueeze(0)).then_inc(ld_vecs, 16)
            for row, name in ((5, "L0_ffn_b1"), (14, "L0_ffn_b3"), (23, "L0_ffn_gate_w")):
                sp.dma_start(vecs[row:row + 8, :], w[name]).then_inc(ld_vecs, 16)
            sp.dma_start(Wqkv[:, :], w["L0_attn_qkv_kernel"]).then_inc(ld_qkv, 16)
            sp.dma_start(Wk0[:, :], w["L0_xattn_Wk"]).then_inc(ld_x0, 16)
            sp.dma_start(Wv0[:, :], w["L0_xattn_Wv"]).then_inc(ld_x0, 16)
            sp.dma_start(Wq0[:, :], w["L0_xattn_Wq"]).then_inc(ld_x0, 16)
            sp.dma_start(Bn[:, :], w["L1_attn_B"]).then_inc(ld_ssm, 16)
            for q in range(BQ):
                sp.dma_start(Cn[:, q, :], w["L1_attn_C"]).then_inc(ld_ssm, 16)
            sp.wait_ge(c_azero, 1)
            for q in range(BQ):
                sp.dma_start(Apow[q * NS:(q + 1) * NS, 0, 0, q * NS:(q + 1) * NS],
                             w["L1_attn_A"]).then_inc(ld_abd, 16)
            sp.dma_start(bv0[:, :], w["L0_xattn_bv"].partition_broadcast(P)).then_inc(ld_rows, 16)
            sp.dma_start(masku[:, :], w["mask_BxS2_bk0"].rearrange("b s -> (b s)").partition_broadcast(P)
                         ).then_inc(ld_mask, 16)
            sp.dma_start(Wk1[:, :], w["L1_xattn_W_k"]).then_inc(ld_x1, 16)
            sp.dma_start(Wv1[:, :], w["L1_xattn_W_v"]).then_inc(ld_x1, 16)
            sp.dma_start(Wq1[:, :], w["L1_xattn_W_q"]).then_inc(ld_x1, 16)
            sp.dma_start(Wo1[:, :, :], w["L1_xattn_W_o"].rearrange("(h p) d -> p h d", p=P)).then_inc(ld_x1, 16)

            for part, done in ((0, st_q), (1, st_k), (2, st_v)):
                if part < 2:
                    sp.wait_ge(qkv_act, 2 * part + 2)
                else:
                    sp.wait_ge(qkv_dve, 2)
                sp.dma_start(qkv_d[part, :, :], QKVT[:, part, :]).then_inc(done, 16)
            sp.wait_ge(q_zero, 1)
            for part, done, dst in ((0, st_q, Q2), (1, st_k, K2)):
                sp.wait_ge(done, 16)
                for quarter in range(4):
                    src = qkv_d[part, :, quarter * 256:(quarter + 1) * 256]
                    sp.dma_start(dst[32 * quarter:32 * quarter + HD, :, :],
                                 src.rearrange("(c e) t -> e c t", e=HD)).then_inc(ld_q2, 16)
            sp.wait_ge(st_v, 16)
            for b in range(B):
                src = qkv_d[2, :, b * S:(b + 1) * S]
                sp.dma_start(V2[b * HD:(b + 1) * HD, :, :],
                             src.rearrange("(c e) t -> e c t", e=HD)).then_inc(ld_v2, 16)

            for dst, name, one in ((W1a, "L0_ffn_w1", "L0_ffn_sw1"), (W3a, "L0_ffn_w3", "L0_ffn_sw3"),
                                   (W2a, "L0_ffn_w2", "L0_ffn_sw2")):
                sp.dma_start(dst[:, 0:E0, :], w[name].rearrange("e d f -> d e f")).then_inc(ld_f0, 16)
                sp.dma_start(dst[:, E0, :], w[one]).then_inc(ld_f0, 16)
            sp.dma_start(b2a[0:E0, :], w["L0_ffn_b2"]).then_inc(ld_f0, 16)
            sp.dma_start(b2a[E0:E0 + 1, :], w["L0_ffn_sb2"].unsqueeze(0)).then_inc(ld_f0, 16)
            for dst, name in ((gamma, "L1_attn_gamma"), (beta, "L1_attn_beta"), (bo, "L1_xattn_b_o")):
                sp.dma_start(dst[:, :], w[name].partition_broadcast(P)).then_inc(ld_rows, 16)
            sp.dma_start(Wg[:, :], w["L1_ffn_Wg"]).then_inc(ld_f1, 16)
            sp.wait_ge(o_act, 1)
            sp.wait_ge(o_dve, 1)
            sp.dma_start(o_d, OT2[:, :, :].rearrange("p c s -> p (c s)")).then_inc(st_o, 16)
            sp.wait_ge(st_o, 16)
            for c in range(CH):
                src = o_d.rearrange("(b e) (c s) -> c e b s", e=HD, s=S)[c, :, :, :]
                sp.dma_start(OT[c * HD:(c + 1) * HD, :].rearrange("e (b s) -> e b s", s=S), src).then_inc(ld_o, 16)

            sp.wait_ge(a_scores, B)
            sp.dma_start(W1b[:, :, :], w["L1_ffn_W1"].rearrange("e d f -> d e f")).then_inc(ld_f1, 16)
            for e in range(E1):
                sp.dma_start(W2b[:, e, :, :], w["L1_ffn_W2"][e, :, :].rearrange("(k p) d -> p k d", p=P)
                             ).then_inc(ld_f1, 16)

            for t in range(NT):
                sp.wait_ge(m_done, t + 1)
                sp.dma_start(out.rearrange("b s d -> (b s) d")[t * P:(t + 1) * P, :], X[:, t, :]
                             ).then_inc(st_out, 16)
            sp.wait_ge(st_out, 16 * NT)

        @block.gpsimd
        def _(pool):
            nc.gpsimd.memset(ident[:, :], 0.0).then_inc(c_zero, 1)
            pool.wait_ge(c_zero, 1)
            nc.gpsimd.affine_select(out=ident[:, :], in_=ident[:, :], compare_op=ALU.not_equal, fill=1.0, base=0,
                                    pattern=[[-1, P]], channel_multiplier=1).then_inc(c_ident, 1)
            nc.gpsimd.memset(Apow[:, 0, 0, :], 0.0).then_inc(c_azero, 1)
            nc.gpsimd.memset(causal[:, :, :], 0.0).then_inc(c_misc0, 1)
            nc.gpsimd.memset(Q2, 0.0).then_inc(q_zero, 1)
            nc.gpsimd.memset(trib[:, :], 1.0).then_inc(c_misc0, 1)
            nc.gpsimd.memset(Vb[:, :, :, :, :], 0.0).then_inc(c_misc0, 1)
            nc.gpsimd.iota(jconst[:, :, :], pattern=[[1, NC], [0, E1]], base=1, channel_multiplier=0).then_inc(c_misc, 1)
            nc.gpsimd.memset(onesb[:, :], 1.0).then_inc(c_misc, 1)
            nc.gpsimd.memset(magic[:, :], 0x5f3759df).then_inc(c_misc, 1)
            pool.wait_ge(c_ident, 1)
            nc.gpsimd.tensor_copy(identb[:, :], ident[:, :]).then_inc(c_misc, 1)
            pool.wait_ge(ld_qkv, 16)
            nc.gpsimd.tensor_copy(Wp[:, :, :].rearrange("d s (c e) -> d c s e", e=HD),
                                  Wqkv[:, :].rearrange("d (c s e) -> d c s e", s=3, e=HD)).then_inc(w_split, 1)
            for e in range(E0):
                nc.gpsimd.memset(em8[:, :, e], float(e - E0)).then_inc(c_misc, 1)
            pool.wait_ge(c_misc0, 3)
            for half in range(2):
                pool.wait_ge(c_misc, 4 + E0 + half)
                part = causal[half * S:(half + 1) * S, :, :]
                nc.gpsimd.affine_select(out=part, in_=part, compare_op=ALU.is_ge, fill=-1.0e38, base=0,
                                        pattern=[[0, NPAIR], [-1, S]], channel_multiplier=1).then_inc(c_misc, 1)
            pool.wait_ge(c_misc, 4 + E0 + 2)
            nc.gpsimd.affine_select(out=trib[:, :], in_=trib[:, :], compare_op=ALU.is_gt, fill=0.0, base=0,
                                    pattern=[[1, P]], channel_multiplier=-1).then_inc(c_misc, 1)
            for p2 in range(2):
                pool.wait_ge(c_misc, 4 + E0 + 3 + p2)
                nc.gpsimd.memset(Vb[p2 * S:(p2 + 1) * S, :, :, p2, 2 * HD], 1.0).then_inc(c_misc, 1)
            pool.wait_ge(c_misc, 4 + E0 + 5)
            nc.gpsimd.memset(comb[:, :, E0], 1.0).then_inc(c_misc, 1)
        C_MISC = 4 + E0 + 2 + 1 + 2 + 1

        @block.tensor
        def _(pe):
            mm = nc.tensor.matmul

            def transpose_xn(n):
                pe.wait_ge(xn_ready, NT * (n + 1))
                for t in range(NT):
                    last = nc.tensor.transpose(bank[t // 4][:, (t % 4) * P:(t % 4 + 1) * P], XN[:, t, :], ident[:, :])
                    if t % 4 == 3:
                        last.then_inc(xt_psum, 1)

            def wait_xt(n):
                pe.wait_ge(xt_act, n + 1)
                pe.wait_ge(xt_dve, n + 1)
            pe.wait_ge(c_ident, 1)
            pe.wait_ge(ld_vecs, 160)
            nc.tensor.transpose(bank[4][:, 0:31], vecs[:, :], ident[0:31, 0:31]).then_inc(prep_psum, 1)
            pe.wait_ge(ld_ctx, 16)
            for h in range(2):
                for t in range(4):
                    last = nc.tensor.transpose(bank[5 + h][0:DC, t * P:(t + 1) * P], CTX[:, 4 * h + t, :], ident[:, :])
                last.then_inc(prep_psum, 1)
            pe.wait_ge(ld_ssm, 80)
            pe.wait_ge(ld_abd, 64)
            nc.tensor.transpose(bank[7][:, 0:NS], Bn[:, :], ident[0:NS, 0:NS])
            nc.tensor.transpose(bank[7][:, NS:NS + P], Cn[:, :, :].rearrange("p q n -> p (q n)"), ident[:, :])
            nc.tensor.transpose(bank[7][:, NS + P:NS + 2 * P], Apow[:, 0, 0, :], ident[:, :]).then_inc(prep_psum, 1)
            pe.wait_ge(ld_x0, 48)
            pe.wait_ge(prep_act, 3)
            for h in range(2):
                mm(bank[4 + h][:, :], Wk0[:, :], CTXT[:, h * HALF:(h + 1) * HALF], start=True, stop=True
                   ).then_inc(prep_psum, 1)
            transpose_xn(0)
            pe.wait_ge(prep_act, 4)
            for h in range(2):
                for t in range(4):
                    last = mm(bank[6 + h][:, t * P:(t + 1) * P], CTXT[:, (4 * h + t) * P:(4 * h + t + 1) * P],
                              Wv0[:, :], start=True, stop=True)
                last.then_inc(prep_psum, 1)
            wait_xt(0)
            pe.wait_ge(w_split, 1)
            for s in range(3):
                for h in range(2):
                    if s == 1 and h == 0:
                        pe.wait_ge(prep_act, 6)
                    if s == 2 and h == 0:
                        pe.wait_ge(prep_dve, 2)
                    mm(bank[2 + 2 * s + h][:, :], Wp[:, s, :],
                       XT[:, h * HALF:(h + 1) * HALF], start=True, stop=True).then_inc(qkv_psum, 1)
            pe.wait_ge(ld_x1, 64)
            pe.wait_ge(qkv_act, 2)
            for i in range(8):
                if i >= 4:
                    pe.wait_ge(k1_ready, i - 3)
                mm(bank[i % 4][:, :], Wk1[:, (i // 2) * P:(i // 2 + 1) * P],
                   CTXT[:, (i % 2) * HALF:(i % 2 + 1) * HALF], start=True, stop=True).then_inc(k1_psum, 1)
                if i == 0:
                    pe.wait_ge(qkv_act, 4)
                    pe.wait_ge(qkv_dve, 2)
                if i >= 4:
                    pe.wait_ge(v1_ready, i - 3)
                mm(bank[4 + i % 4][:, :], CTXT[:, i * P:(i + 1) * P], Wv1[:, :], start=True, stop=True
                   ).then_inc(v1_psum, 1)
            pe.wait_ge(k1_ready, 8)
            for r in range(1, ROUNDS):
                if r >= 2:
                    pe.wait_ge(pow_ready, r - 1)
                mm(bank[0][:, 0:P], Apow[:, r - 1, 1, :], Apow[:, r - 1, 0, :], start=True, stop=True)
                mm(bank[0][:, P:2 * P], Apow[:, r - 1, 0, :], Apow[:, r - 1, 1, :], start=True, stop=True
                   ).then_inc(pow_psum, 1)
            pe.wait_ge(v_side, 4)
            pe.wait_ge(v1_ready, 8)
            for g2 in range(2):
                for p4 in range(4):
                    src = V2r[:, p4, g2, :, :, :].rearrange("p r t c -> p (r t c)")
                    last = nc.tensor.transpose(bank[6 + g2][:, p4 * P:(p4 + 1) * P], src, ident[:, :])
                last.then_inc(v2_psum, 1)
            pe.wait_ge(ld_q2, 128)
            pe.wait_ge(q_act, 1)
            pe.wait_ge(q_dve, 1)
            pe.wait_ge(c_misc, C_MISC)
            pe.wait_ge(pow_ready, ROUNDS - 1)

            def head_cols(t, b, pair, g2):
                first = (b % 4) * S + pair * 2 * GT + g2 * GT
                row = 32 * (b // 4)
                return t[row:row + HD, :, first:first + GT].rearrange("e c t -> e t c")

            def q_cols(b, pair, g2):
                first = (b % 4) * S + pair * 2 * GT + g2 * GT
                row = 32 * (b // 4)
                return Qr[row:row + HD, first:first + GT, :].rearrange("e t c -> e (t c)")

            def scores(k):
                b = seq(k)
                if k >= 4:
                    pe.wait_ge(a_sub, k - 3)
                dst = bank[k % 4]
                mm(dst[:, :], identb[:, :], causal[:, :, :].rearrange("p a s -> p (a s)"), start=True, stop=False,
                   skip_group_check=True)
                for pair in range(NPAIR):
                    for g2 in range(2):
                        last = mm(dst[g2 * S:(g2 + 1) * S, pair * S:(pair + 1) * S], q_cols(b, pair, g2),
                                  head_cols(K2, b, pair, g2), start=False, stop=(pair == NPAIR - 1),
                                  skip_group_check=True)
                last.then_inc(a_scores, 1)

            def transpose_probs(k):
                pe.wait_ge(a_exp, k + 1)
                if k >= 2:
                    pe.wait_ge(a_trc, k - 1)
                for p4 in range(4):
                    last = nc.tensor.transpose(bank[4 + k % 2][:, p4 * P:(p4 + 1) * P],
                                               Es[:, k % 3, p4 * P:(p4 + 1) * P], ident[:, :])
                last.then_inc(a_tr, 1)

            def weigh_values(k):
                b = seq(k)
                pe.wait_ge(a_trc, k + 1)
                if k == 0:
                    pe.wait_ge(vb_act, 2)
                    pe.wait_ge(vb_dve, 2)
                if k >= 4 and k % 2 == 0:
                    pe.wait_ge(a_norm, k // 2 - 1)
                for p4 in range(4):
                    first = ((k % 2) * 4 + p4) * 2 * VW
                    last = mm(bank[6 + (k // 2) % 2][:, first:first + 2 * VW],
                              PTs[:, k % 2, p4 * P:(p4 + 1) * P],
                              Vb[:, b, p4, :, :].rearrange("p r v -> p (r v)"), start=True, stop=True)
                last.then_inc(a_pv, 1)

            for k in range(B + 3):
                if k < B:
                    scores(k)
                if 2 <= k < B + 2:
                    transpose_probs(k - 2)
                if k >= 3:
                    weigh_values(k - 3)
            pe.wait_ge(a_norm, B // 2)
            for pair in range(NPAIR):
                last = nc.tensor.transpose(bank[pair // 4][:, (pair % 4) * P:(pair % 4 + 1) * P],
                                           Opos[:, pair, :, :].rearrange("p b e -> p (b e)"), ident[:, :])
                if pair % 4 == 3:
                    last.then_inc(o_psum, 1)
            pe.wait_ge(ld_o, 16 * CH)
            for t in range(NT):
                last = nc.tensor.transpose(bank[2 + t // 4][:, (t % 4) * P:(t % 4 + 1) * P],
                                           OT[:, t * P:(t + 1) * P], ident[:, :])
                if t % 4 == 3:
                    last.then_inc(x_psum, 1)

            transpose_xn(1)
            wait_xt(1)
            for h in range(2):
                mm(bank[2 + h][:, :], Wq0[:, :], XT[:, h * HALF:(h + 1) * HALF], start=True, stop=True
                   ).then_inc(b_q, 1)
            pe.wait_ge(b_qc, 2)
            for b in range(B):
                u, o, r = b // 4, (b // 2) % 2, b % 2
                last = mm(bank[4][o * S:(o + 1) * S, (2 * u + r) * S:(2 * u + r + 1) * S],
                          QKVT[:, 0, b * S:(b + 1) * S], K0T[:, b * S:(b + 1) * S], start=True, stop=True)
            last.then_inc(b_scores, 1)
            pe.wait_ge(b_prob, 1)
            for u in range(4):
                last = nc.tensor.transpose(bank[5][:, u * P:(u + 1) * P], Es[:, 0, u * P:(u + 1) * P], ident[:, :])
            last.then_inc(b_tr, 1)
            pe.wait_ge(b_trc, 1)
            for b in range(B):
                u, o, r = b // 4, (b // 2) % 2, b % 2
                t = b // 2
                last = mm(bank[6 + t // 4][r * S:(r + 1) * S, (t % 4) * P:(t % 4 + 1) * P],
                          PTs[r * S:(r + 1) * S, 0, u * P + o * S:u * P + (o + 1) * S],
                          V0[r * S:(r + 1) * S, t, :], start=True, stop=True)
            last.then_inc(b_pv, 1)

            transpose_xn(2)
            wait_xt(2)
            for t in range(NT):
                last = mm(bank[4][:, t * E0:(t + 1) * E0], XT[:, t * P:(t + 1) * P], cols[:, 23:31],
                          start=True, stop=True)
            last.then_inc(g_psum, 1)
            pe.wait_ge(ld_f0, 128)

            def up0(e):
                for h in range(2):
                    if e >= 1:
                        pe.wait_ge(f_silu, 2 * (e - 1) + h + 1)
                    mm(bank[h][:, :], W1a[:, e, :], XT[:, h * HALF:(h + 1) * HALF], start=True, stop=True
                       ).then_inc(f_h1, 1)
                    if e >= 1:
                        pe.wait_ge(f_h, 2 * (e - 1) + h + 1)
                    mm(bank[2 + h][:, :], W3a[:, e, :], XT[:, h * HALF:(h + 1) * HALF], start=True, stop=True
                       ).then_inc(f_h3, 1)

            def down0(e):
                shared = e == E0
                for h in range(2):
                    pe.wait_ge(f_h, 2 * e + h + 1)
                    if e >= 2:
                        pe.wait_ge(f_acc, 2 * (e - 2) + h + 1)
                    elif e == 1:
                        pe.wait_ge(g_combc, h + 1)
                    elif h == 0:
                        pe.wait_ge(g_sub, 1)
                    for t in range(4):
                        dst = bank[4 + 2 * (e % 2) + h][:, t * P:(t + 1) * P]
                        tile = slice((4 * h + t) * P, (4 * h + t + 1) * P)
                        last = mm(dst, hid[:, e % 2, 0, tile], W2a[:, e, :], start=True, stop=not shared)
                        if shared:
                            last = mm(dst, combT[:, tile], b2a[:, :], start=False, stop=True)
                    last.then_inc(f_out, 1)

            up0(0)
            pe.wait_ge(g_comb, 1)
            for t in range(NT):
                last = nc.tensor.transpose(bank[6 + t // 4][0:E0 + 1, (t % 4) * P:(t % 4 + 1) * P], comb[:, t, :],
                                           ident[:, :])
                if t % 4 == 3:
                    last.then_inc(g_combt, 1)
            for e in range(E0 + 1):
                if e < E0:
                    up0(e + 1)
                down0(e)

            transpose_xn(3)
            wait_xt(3)
            for q in range(BQ):
                last = mm(bank[2][q * NS:(q + 1) * NS, 0:BQ * S], BT[:, :], XT[:, q * BQ * S:(q + 1) * BQ * S],
                          start=True, stop=False, skip_group_check=True)
            last.then_inc(s_psum, 1)
            for r in range(ROUNDS):
                k = 2 ** r
                pe.wait_ge(s_state, r + 1)
                dst = bank[2][:, 0:BQ * S].rearrange("p (b s) -> p b s", s=S)[:, :, k:S]
                mm(dst, Apow[:, r, 1, :], ST[:, :, 0:S - k], start=False, stop=(r == ROUNDS - 1),
                   skip_group_check=True).then_inc(s_psum, 1)
            pe.wait_ge(s_state, ROUNDS + 1)
            for t in range(NT):
                q = t // 2
                last = mm(bank[3 + q][:, (t % 2) * P:(t % 2 + 1) * P],
                          ST[q * NS:(q + 1) * NS, 2 * (t % 2):2 * (t % 2) + 2, :].rearrange("p b s -> p (b s)"),
                          CT[q * NS:(q + 1) * NS, :], start=True, stop=True)
                if t % 2 == 1:
                    last.then_inc(s_y, 1)

            transpose_xn(4)
            wait_xt(4)
            for i in range(8):
                if i >= 4:
                    if i % 2 == 0:
                        pe.wait_ge(c_qact, (i - 4) // 2 + 1)
                    else:
                        pe.wait_ge(c_qdve, (i - 5) // 2 + 1)
                mm(bank[2 + i % 4][:, :], Wq1[:, (i // 2) * P:(i // 2 + 1) * P],
                   XT[:, (i % 2) * HALF:(i % 2 + 1) * HALF], start=True, stop=True).then_inc(c_q, 1)
            pe.wait_ge(c_qact, 4)
            pe.wait_ge(c_qdve, 4)
            pe.wait_ge(mask_ready, 2)

            def scores1(t):
                if t >= 3:
                    pe.wait_ge(c_sub, t - 2)
                dst = bank[t % 3]
                bias = maskrow[0:1, t * P:(t + 1) * P].unsqueeze(1).broadcast_to([1, NHP, P])
                mm(dst[:, :], onesb[0:1, :], bias, start=True, stop=False, skip_group_check=True)
                for hp in range(NHP):
                    for b2 in range(2):
                        for h2 in range(2):
                            tok = slice(t * P + b2 * S, t * P + (b2 + 1) * S)
                            last = mm(dst[h2 * S:(h2 + 1) * S, (2 * hp + b2) * S:(2 * hp + b2 + 1) * S],
                                      Q1T[h2 * DH1:(h2 + 1) * DH1, hp, tok], K1T[h2 * DH1:(h2 + 1) * DH1, hp, tok],
                                      start=False, stop=(hp == NHP - 1), skip_group_check=True)
                last.then_inc(c_scores, 1)

            def transpose_probs1(t):
                pe.wait_ge(c_prob, t + 1)
                if t >= 2:
                    pe.wait_ge(c_trc, t - 1)
                for hp in range(NHP):
                    last = nc.tensor.transpose(bank[4 + t % 2][:, hp * P:(hp + 1) * P],
                                               Es[:, t % 3, hp * P:(hp + 1) * P], ident[:, :])
                last.then_inc(c_tr, 1)

            def weigh_values1(t):
                pe.wait_ge(c_trc, t + 1)
                if t >= 1:
                    pe.wait_ge(c_otc, 2 * t)
                for hp in range(NHP):
                    for b2 in range(2):
                        for h2 in range(2):
                            h = 2 * hp + h2
                            last = mm(bank[6 + b2][h2 * S:(h2 + 1) * S, hp * S:(hp + 1) * S],
                                      V1[b2 * S:(b2 + 1) * S, t, h * DH1:(h + 1) * DH1],
                                      PTs[b2 * S:(b2 + 1) * S, t % 2, hp * P + h2 * S:hp * P + (h2 + 1) * S],
                                      start=True, stop=True)
                last.then_inc(c_pv, 1)

            def project_out(t):
                pe.wait_ge(c_otc, 2 * t + 2)
                if t >= 1:
                    pe.wait_ge(c_added, t)
                for hp in range(NHP):
                    last = mm(bank[3][:, 0:D], OTs[:, t % 2, hp, :], Wo1[:, hp, :],
                              start=(hp == 0), stop=(hp == NHP - 1))
                last.then_inc(c_wo, 1)

            for t in range(NT + 4):
                if t < NT:
                    scores1(t)
                if 2 <= t < NT + 2:
                    transpose_probs1(t - 2)
                if 3 <= t < NT + 3:
                    weigh_values1(t - 3)
                if t >= 4:
                    project_out(t - 4)

            transpose_xn(5)
            wait_xt(5)
            pe.wait_ge(ld_f1, 160)
            for t in range(NT):
                last = mm(bank[2][:, t * E1:(t + 1) * E1], XT[:, t * P:(t + 1) * P], Wg[:, :], start=True, stop=True)
            last.then_inc(r_psum, 1)

            def up1(e):
                for f in range(F1):
                    for h in range(2):
                        i = 4 * e + 2 * f + h
                        if i >= 4:
                            pe.wait_ge(m_gelu, i - 3)
                        mm(bank[(0, 1, 4, 5)[i % 4]][:, :], W1b[:, e, f * P:(f + 1) * P],
                           XT[:, h * HALF:(h + 1) * HALF], start=True, stop=True).then_inc(m_up, 1)

            def down1(e):
                for h in range(2):
                    pe.wait_ge(m_gelu, 4 * e + 2 + h + 1)
                    if e >= 1:
                        pe.wait_ge(m_ys, 2 * (e - 1) + h + 1)
                    for t in range(4):
                        tile = slice((4 * h + t) * P, (4 * h + t + 1) * P)
                        for f in range(F1):
                            last = mm(bank[6 + h][:, t * P:(t + 1) * P], hid[:, e % 2, f, tile], W2b[:, e, f, :],
                                      start=(f == 0), stop=(f == F1 - 1))
                    last.then_inc(m_down, 1)

            def count(i):
                pe.wait_ge(r_hit, i + 1)
                mm(bank[3][:, 0:NC * E1 * NT], onesb[:, :], hit[:, :, :].rearrange("p a t -> p (a t)"),
                   start=True, stop=True).then_inc(r_cnt, 1)

            def prefix():
                pe.wait_ge(r_eq, 1)
                mm(bank[2][:, 0:NT * E1], trib[:, :], eqb[:, :, :].rearrange("p t e -> p (t e)"),
                   start=True, stop=False, skip_group_check=True)
                for t in range(NT - 1):
                    rest = NT - 1 - t
                    src = eqb[:, t, :].unsqueeze(1).broadcast_to([P, rest, E1])
                    last = mm(bank[2][:, (t + 1) * E1:NT * E1], onesb[:, :], src, start=False, stop=(t == NT - 2),
                              skip_group_check=True)
                last.then_inc(r_pre, 1)

            search = BITS // STEP
            up1(0)
            done = 0
            for e in range(E1):
                for _i in range(4):
                    if done < search:
                        count(done)
                        done += 1
                    elif done == search:
                        count(done)
                        prefix()
                        done += 1
                if e + 1 < E1:
                    up1(e + 1)
                down1(e)

        @block.scalar
        def _(act):
            AF = nc.scalar.activation

            def copy_xt(n):
                act.wait_ge(xt_psum, 2 * n + 1)
                AF(XT[:, 0:HALF], bank[0][:, :], ACT.Copy).then_inc(xt_act, 1)

            act.wait_ge(prep_psum, 1)
            AF(cols[:, :], bank[4][:, 0:31], ACT.Copy).then_inc(prep_act, 1)
            for h in range(2):
                act.wait_ge(prep_psum, 2 + h)
                AF(CTXT[:, h * HALF:(h + 1) * HALF], bank[5 + h][0:DC, :], ACT.Copy).then_inc(prep_act, 1)
            act.wait_ge(prep_psum, 4)
            AF(BT[:, :], bank[7][:, 0:NS], ACT.Copy)
            AF(CT[:, :], bank[7][:, NS:NS + P], ACT.Copy)
            AF(Apow[:, 0, 1, :], bank[7][:, NS + P:NS + 2 * P], ACT.Copy).then_inc(prep_act, 1)
            for h in range(2):
                act.wait_ge(prep_psum, 5 + h)
                if h == 0:
                    act.wait_ge(prep_act, 4)
                AF(K0T[:, h * HALF:(h + 1) * HALF], bank[4 + h][:, :], ACT.Identity, bias=cols[:, 4:5]
                   ).then_inc(prep_act, 1)
            copy_xt(0)
            for s in range(2):
                for h in range(2):
                    act.wait_ge(qkv_psum, 2 * s + h + 1)
                    AF(QKVT[:, s, h * HALF:(h + 1) * HALF], bank[2 + 2 * s + h][:, :], ACT.Identity,
                       bias=cols[:, s:s + 1]).then_inc(qkv_act, 1)
            for i in range(8):
                act.wait_ge(v1_psum, i + 1)
                AF(V1[:, i, :], bank[4 + i % 4][:, :], ACT.Copy).then_inc(v1_ready, 1)
            for r in range(1, ROUNDS):
                act.wait_ge(pow_psum, r)
                AF(Apow[:, r, :, :], bank[0][:, 0:2 * P].rearrange("p (a n) -> p a n", a=2), ACT.Copy
                   ).then_inc(pow_ready, 1)
            act.wait_ge(ld_q2, 128)
            AF(Qr[:, 0:N // 8, :], Q2[:, :, 0:N // 8].rearrange("e c t -> e t c"), ACT.Copy).then_inc(q_act, 1)
            act.wait_ge(v2_psum, 1)
            act.wait_ge(c_misc, C_MISC)
            for p2 in range(2):
                AF(Vb[p2 * S:(p2 + 1) * S, :, :, p2, 0:HD].rearrange("p b q e -> p q b e"),
                   bank[6][p2 * S:(p2 + 1) * S, :].rearrange("p (q b e) -> p q b e", q=4, e=HD), ACT.Copy
                   ).then_inc(vb_act, 1)

            for k in range(B + 1):
                if k < B:
                    act.wait_ge(a_sub, k + 1)
                    AF(Es[:, k % 3, :], Es[:, k % 3, :], ACT.Exp, scale=ATTN_SCALE).then_inc(a_exp, 1)
                if k >= 1:
                    act.wait_ge(a_tr, k)
                    if k >= 3:
                        act.wait_ge(a_pv, k - 2)
                    AF(PTs[:, (k - 1) % 2, :], bank[4 + (k - 1) % 2][:, :], ACT.Copy).then_inc(a_trc, 1)
            act.wait_ge(o_psum, 1)
            AF(OT2[:, :, 0:S // 2].rearrange("p c (q u) -> p q u c", u=8),
               bank[0][:, :].rearrange("p (q u c) -> p q u c", q=4, c=CH), ACT.Copy).then_inc(o_act, 1)

            copy_xt(1)
            for h in range(2):
                act.wait_ge(b_q, h + 1)
                AF(QKVT[:, 0, h * HALF:(h + 1) * HALF], bank[2 + h][:, :], ACT.Identity, bias=cols[:, 3:4]
                   ).then_inc(b_qc, 1)
            act.wait_ge(b_sub, 1)
            AF(Es[:, 0, :], Es[:, 0, :], ACT.Exp, scale=XATTN0_SCALE).then_inc(b_exp, 1)
            act.wait_ge(b_tr, 1)
            AF(PTs[:, 0, :], bank[5][:, :], ACT.Copy).then_inc(b_trc, 1)

            copy_xt(2)
            act.wait_ge(g_sub, 1)
            AF(rt[:, 1, :, :], rt[:, 1, :, :], ACT.Exp).then_inc(g_exp, 1)
            for e in range(E0 + 1):
                for h in range(2):
                    act.wait_ge(f_h1, 2 * e + h + 1)
                    if e >= 1:
                        act.wait_ge(f_h, 2 * (e - 1) + h + 1)
                    AF(hid[:, 0, 1, h * HALF:(h + 1) * HALF], bank[h][:, :], ACT.Silu, bias=cols[:, 5 + e:6 + e]
                       ).then_inc(f_silu, 1)
                if e == 0:
                    for h in range(2):
                        act.wait_ge(g_combt, h + 1)
                        AF(combT[:, h * HALF:(h + 1) * HALF], bank[6 + h][0:E0 + 1, :], ACT.Copy
                           ).then_inc(g_combc, 1)

            copy_xt(3)
            for h in range(4):
                act.wait_ge(s_y, h + 1)
                AF(GA[:, 2 * h:2 * h + 2, :], bank[3 + h][:, 0:2 * D].rearrange("p (t d) -> p t d", d=D), ACT.Gelu
                   ).then_inc(s_gelu, 1)

            copy_xt(4)
            for i in range(0, 8, 2):
                act.wait_ge(c_q, i + 1)
                AF(Q1T[:, i // 2, 0:HALF], bank[2 + i % 4][:, :], ACT.Copy).then_inc(c_qact, 1)
            for t in range(NT + 3):
                if t < NT:
                    act.wait_ge(c_sub, t + 1)
                    AF(Es[:, t % 3, :], Es[:, t % 3, :], ACT.Exp, scale=XATTN1_SCALE).then_inc(c_exp, 1)
                if 2 <= t < NT + 2:
                    act.wait_ge(c_tr, t - 1)
                    if t >= 4:
                        act.wait_ge(c_pv, t - 3)
                    AF(PTs[:, t % 2, :], bank[4 + t % 2][:, :], ACT.Copy).then_inc(c_trc, 1)
                if t >= 3:
                    act.wait_ge(c_pv, t - 2)
                    if t >= 5:
                        act.wait_ge(c_wo, t - 4)
                    for b2 in range(2):
                        AF(OTs[:, (t - 3) % 2, :, b2 * S:(b2 + 1) * S],
                           bank[6 + b2][:, 0:NHP * S].rearrange("p (h n) -> p h n", n=S), ACT.Copy
                           ).then_inc(c_otc, 1)

            copy_xt(5)
            act.wait_ge(r_sub, 1)
            AF(rt[:, 1, :, :], rt[:, 1, :, :], ACT.Exp).then_inc(r_exp, 1)

            def gelu(e):
                for f in range(F1):
                    for h in range(2):
                        i = 4 * e + 2 * f + h
                        act.wait_ge(m_up, i + 1)
                        if e >= 2:
                            act.wait_ge(m_down, 2 * (e - 2) + h + 1)
                        AF(hid[:, e % 2, f, h * HALF:(h + 1) * HALF], bank[(0, 1, 4, 5)[i % 4]][:, :], ACT.Gelu
                           ).then_inc(m_gelu, 1)

            gelu(0)
            for e in range(E1):
                if e + 1 < E1:
                    gelu(e + 1)
                for h in range(2):
                    act.wait_ge(m_down, 2 * e + h + 1)
                    AF(ys[:, e, 4 * h:4 * h + 4, :], bank[6 + h][:, :].rearrange("p (t d) -> p t d", d=D), ACT.Copy
                       ).then_inc(m_ys, 1)

        @block.vector
        def _(dve):
            V = nc.vector
            steps = [0]

            def then(ins):
                steps[0] += 1
                ins.then_inc(v_step, 1)
                dve.wait_ge(v_step, steps[0])

            def moments(src):
                for t in range(NT):
                    last = V.bn_stats(stats[:, t, :], src[:, t, :])
                then(last)
                for t in range(NT):
                    last = V.bn_aggr(mv[:, t, :], stats[:, t, :])
                then(last)
                var, r, y2, p = rs[:, 1, :], rs[:, 0, :], rs[:, 2, :], rs[:, 3, :]
                then(V.tensor_scalar(var, mv[:, :, 1], EPS, None, ALU.add))
                then(V.tensor_scalar(rs[:, 4, :].bitcast(int32), var.bitcast(int32), 1, None, ALU.logical_shift_right))
                then(V.tensor_tensor(r.bitcast(int32), magic[:, :], rs[:, 4, :].bitcast(int32), ALU.subtract))
                for _i in range(2):
                    then(V.tensor_tensor(y2, r, r, ALU.mult))
                    then(V.tensor_tensor(y2, y2, var, ALU.mult))
                    then(V.tensor_scalar(p, y2, 0.375, -1.25, ALU.mult, ALU.add))
                    then(V.tensor_tensor(p, p, y2, ALU.mult))
                    then(V.scalar_tensor_tensor(r, p, 1.875, r, ALU.add, ALU.mult))

            def layernorm(n):
                moments(X)
                for t in range(NT):
                    V.tensor_scalar(XN[:, t, :], X[:, t, :], mv[:, t, 0:1], rs[:, 0, t:t + 1], ALU.subtract, ALU.mult
                                    ).then_inc(xn_ready, 1)

            def copy_xt(n):
                dve.wait_ge(xt_psum, 2 * n + 2)
                V.tensor_copy(XT[:, HALF:N], bank[1][:, :]).then_inc(xt_dve, 1)

            def softmax_small(logits, sub_done, exp_done):
                then(V.tensor_reduce(rv[:, 0, :], logits, AX.X, ALU.max))
                V.tensor_tensor(rt[:, 1, :, :], logits, per_row(rv[:, 0, :], E0), ALU.subtract).then_inc(sub_done, 1)
                dve.wait_ge(exp_done, 1)
                then(V.tensor_reduce(rv[:, 1, :], rt[:, 1, :, :], AX.X, ALU.add))
                then(V.reciprocal(rv[:, 2, :], rv[:, 1, :]))
                then(V.tensor_tensor(rt[:, 0, :, :], rt[:, 1, :, :], per_row(rv[:, 2, :], E0), ALU.mult))

            def first_max(src, one_hot):
                then(V.tensor_reduce(rv[:, 3, :], src, AX.X, ALU.max))
                then(V.tensor_tensor(rt[:, 2, :, :], src, per_row(rv[:, 3, :], E0), ALU.is_equal))
                then(V.tensor_tensor(rt[:, 2, :, :], rt[:, 2, :, :], em8[:, :, :], ALU.mult))
                then(V.tensor_reduce(rv[:, 4, :], rt[:, 2, :, :], AX.X, ALU.min))
                then(V.tensor_tensor(one_hot, em8[:, :, :], per_row(rv[:, 4, :], E0), ALU.is_equal))

            dve.wait_ge(ld_x, 16)
            dve.wait_ge(c_misc, 3)
            layernorm(0)
            for h in range(2):
                if h == 0:
                    dve.wait_ge(ld_rows, 16)
                dve.wait_ge(prep_psum, 7 + h)
                V.tensor_tensor(V0[:, 4 * h:4 * h + 4, :], bank[6 + h][:, :].rearrange("p (t d) -> p t d", d=D),
                                bv0[:, :].unsqueeze(1).broadcast_to([P, 4, D]), ALU.add).then_inc(prep_dve, 1)
            copy_xt(0)
            for h in range(2):
                dve.wait_ge(qkv_psum, 5 + h)
                if h == 0:
                    dve.wait_ge(prep_act, 1)
                V.tensor_scalar(QKVT[:, 2, h * HALF:(h + 1) * HALF], bank[6 + h][:, :], cols[:, 2:3], None, ALU.add
                                ).then_inc(qkv_dve, 1)
            dve.wait_ge(ld_mask, 16)
            V.tensor_copy(maskf[:, :], masku[:, :]).then_inc(mask_ready, 1)
            dve.wait_ge(mask_ready, 1)
            V.tensor_scalar(maskrow[:, :], maskf[0:1, :], 1.0, 2.0 ** 127, ALU.subtract, ALU.mult
                            ).then_inc(mask_ready, 1)
            for i in range(8):
                dve.wait_ge(k1_psum, i + 1)
                h = i % 2
                V.tensor_tensor(K1T[:, i // 2, h * HALF:(h + 1) * HALF], bank[i % 4][:, :],
                                maskf[:, h * HALF:(h + 1) * HALF], ALU.mult).then_inc(k1_ready, 1)
            dve.wait_ge(ld_v2, 16 * B)
            for g2 in range(2):
                for p2 in range(2):
                    src = V2[:, :, :].rearrange("p c (q r g t) -> p q r g t c", r=2, g=2, t=GT)[:, :, p2, g2, :, :]
                    V.tensor_copy(V2r[:, :, g2, p2, :, :], src).then_inc(v_side, 1)
            dve.wait_ge(ld_q2, 128)
            V.tensor_copy(Qr[:, N // 8:, :], Q2[:, :, N // 8:].rearrange("e c t -> e t c")).then_inc(q_dve, 1)
            dve.wait_ge(v2_psum, 2)
            dve.wait_ge(c_misc, C_MISC)
            for p2 in range(2):
                V.tensor_copy(Vb[p2 * S:(p2 + 1) * S, :, :, p2, HD:2 * HD].rearrange("p b q e -> p q b e"),
                              bank[7][p2 * S:(p2 + 1) * S, :].rearrange("p (q b e) -> p q b e", q=4, e=HD)
                              ).then_inc(vb_dve, 1)

            def normalise(m):
                dve.wait_ge(a_pv, 2 * m + 2)
                o = bank[6 + m % 2][:, 0:2 * NPAIR * VW].rearrange("p (k a v) -> p k a v", k=2, v=VW)
                then(V.reciprocal(rO[:, m, :, :], o[:, :, :, 2 * HD]))
                b = seq(2 * m)
                for g2 in range(2):
                    rows = slice(g2 * S, (g2 + 1) * S)
                    for j in range(2):
                        last = V.tensor_tensor(Opos[rows, :, b + 4 * j, :], o[rows, j, :, g2 * HD:(g2 + 1) * HD],
                                               per_row(rO[rows, m, j, :], HD), ALU.mult)
                last.then_inc(a_norm, 1)

            for k in range(B):
                dve.wait_ge(a_scores, k + 1)
                s = bank[k % 4][:, :].rearrange("p (a s) -> p a s", s=S)
                then(V.tensor_reduce(mx0[:, k, :], s, AX.X, ALU.max))
                if k >= 3:
                    dve.wait_ge(a_tr, k - 2)
                V.tensor_tensor(Es[:, k % 3, :].rearrange("p (a s) -> p a s", s=S), s, per_row(mx0[:, k, :], S),
                                ALU.subtract).then_inc(a_sub, 1)
                if k >= 5 and k % 2 == 1:
                    normalise((k - 5) // 2)
            for m in range(B // 2 - 2, B // 2):
                normalise(m)
            dve.wait_ge(o_psum, 2)
            V.tensor_copy(OT2[:, :, S // 2:S].rearrange("p c (q u) -> p q u c", u=8),
                          bank[1][:, :].rearrange("p (q u c) -> p q u c", q=4, c=CH)).then_inc(o_dve, 1)
            for h in range(2):
                dve.wait_ge(x_psum, h + 1)
                V.tensor_tensor(X[:, 4 * h:4 * h + 4, :], bank[2 + h][:, :].rearrange("p (t d) -> p t d", d=D),
                                X[:, 4 * h:4 * h + 4, :], ALU.add).then_inc(x_added, 1)
            dve.wait_ge(x_added, 2)

            layernorm(1)
            copy_xt(1)
            dve.wait_ge(b_scores, 1)
            s = bank[4][:, :].rearrange("p (a s) -> p a s", s=S)
            e0 = Es[:, 0, :].rearrange("p (a s) -> p a s", s=S)
            then(V.tensor_reduce(sm[:, 0, 0, :], s, AX.X, ALU.max))
            V.tensor_tensor(e0, s, per_row(sm[:, 0, 0, :], S), ALU.subtract).then_inc(b_sub, 1)
            dve.wait_ge(b_exp, 1)
            then(V.tensor_reduce(sm[:, 0, 1, :], e0, AX.X, ALU.add))
            then(V.reciprocal(sm[:, 0, 2, :], sm[:, 0, 1, :]))
            V.tensor_tensor(e0, e0, per_row(sm[:, 0, 2, :], S), ALU.mult).then_inc(b_prob, 1)
            dve.wait_ge(b_pv, 1)
            for h in range(2):
                V.tensor_tensor(X[:, 4 * h:4 * h + 4, :], bank[6 + h][:, :].rearrange("p (t d) -> p t d", d=D),
                                X[:, 4 * h:4 * h + 4, :], ALU.add).then_inc(b_added, 1)
            dve.wait_ge(b_added, 2)

            layernorm(2)
            copy_xt(2)
            dve.wait_ge(g_psum, 1)
            softmax_small(bank[4][:, 0:NT * E0].rearrange("p (t e) -> p t e", e=E0), g_sub, g_exp)
            first_max(rt[:, 0, :, :], rt[:, 3, :, :])
            then(V.scalar_tensor_tensor(rt[:, 4, :, :], rt[:, 3, :, :], -2.0, rt[:, 0, :, :], ALU.mult, ALU.add))
            first_max(rt[:, 4, :, :], rt[:, 5, :, :])
            then(V.tensor_tensor(rt[:, 3, :, :], rt[:, 3, :, :], rt[:, 5, :, :], ALU.add))
            V.tensor_tensor(comb[:, :, 0:E0], rt[:, 3, :, :], rt[:, 0, :, :], ALU.mult).then_inc(g_comb, 1)
            dve.wait_ge(g_comb, 1)

            def gate0(e):
                for h in range(2):
                    dve.wait_ge(f_silu, 2 * e + h + 1)
                    dve.wait_ge(f_h3, 2 * e + h + 1)
                    if e >= 2:
                        dve.wait_ge(f_out, 2 * (e - 2) + h + 1)
                    cut = slice(h * HALF, (h + 1) * HALF)
                    V.scalar_tensor_tensor(hid[:, e % 2, 0, cut], bank[2 + h][:, :], cols[:, 14 + e:15 + e],
                                           hid[:, 0, 1, cut], ALU.add, ALU.mult).then_inc(f_h, 1)

            def add0(e):
                for h in range(2):
                    dve.wait_ge(f_out, 2 * e + h + 1)
                    src = bank[4 + 2 * (e % 2) + h]
                    for t in range(4):
                        tt = 4 * h + t
                        last = V.scalar_tensor_tensor(X[:, tt, :], src[:, t * P:(t + 1) * P], comb[:, tt, e:e + 1],
                                                      X[:, tt, :], ALU.mult, ALU.add)
                    last.then_inc(f_acc, 1)

            gate0(0)
            for e in range(E0 + 1):
                if e < E0:
                    gate0(e + 1)
                if e >= 1:
                    dve.wait_ge(f_acc, 2 * e)
                add0(e)
            dve.wait_ge(f_acc, 2 * (E0 + 1))

            layernorm(3)
            copy_xt(3)
            for r in range(ROUNDS + 1):
                dve.wait_ge(s_psum, r + 1)
                V.tensor_copy(ST[:, :, :], bank[2][:, 0:BQ * S].rearrange("p (b s) -> p b s", s=S)
                              ).then_inc(s_state, 1)
            dve.wait_ge(s_gelu, 4)
            moments(GA)
            for t in range(NT):
                last = V.tensor_scalar(GB[:, t, :], GA[:, t, :], mv[:, t, 0:1], rs[:, 0, t:t + 1], ALU.subtract,
                                       ALU.mult)
            then(last)
            dve.wait_ge(ld_rows, 64)
            wide = [P, NT, D]
            then(V.tensor_tensor(GB[:, :, :], GB[:, :, :], gamma[:, :].unsqueeze(1).broadcast_to(wide), ALU.mult))
            then(V.tensor_tensor(GB[:, :, :], GB[:, :, :], beta[:, :].unsqueeze(1).broadcast_to(wide), ALU.add))
            then(V.tensor_tensor(nanm[:, :, :], GB[:, :, :], GB[:, :, :], ALU.is_equal))
            then(V.tensor_scalar(GA[:, :, :], GB[:, :, :], CLAMP, -CLAMP, ALU.min, ALU.max))
            then(V.tensor_tensor(GA[:, :, :], GA[:, :, :], nanm[:, :, :], ALU.mult))
            then(V.tensor_scalar(nanm[:, :, :], GB[:, :, :], 0.0, 0.0, ALU.mult, ALU.is_equal))
            then(V.copy_predicated(GA[:, :, :], nanm[:, :, :], GB[:, :, :]))
            then(V.tensor_tensor(X[:, :, :], GA[:, :, :], X[:, :, :], ALU.add))

            layernorm(4)
            dve.wait_ge(xn_ready, 5 * NT)
            then(V.tensor_tensor(X[:, :, :], X[:, :, :], bo[:, :].unsqueeze(1).broadcast_to(wide), ALU.add))
            copy_xt(4)
            for i in range(1, 8, 2):
                dve.wait_ge(c_q, i + 1)
                V.tensor_copy(Q1T[:, i // 2, HALF:N], bank[2 + i % 4][:, :]).then_inc(c_qdve, 1)

            def probs1(t):
                dve.wait_ge(c_exp, t + 1)
                e = Es[:, t % 3, :].rearrange("p (a s) -> p a s", s=S)
                then(V.tensor_reduce(sm[:, t, 1, :], e, AX.X, ALU.add))
                then(V.reciprocal(sm[:, t, 2, :], sm[:, t, 1, :]))
                V.tensor_tensor(e, e, per_row(sm[:, t, 2, :], S), ALU.mult).then_inc(c_prob, 1)

            def add1(t):
                dve.wait_ge(c_wo, t + 1)
                V.tensor_tensor(X[:, t, :], bank[3][:, 0:D], X[:, t, :], ALU.add
                                ).then_inc(c_added, 1)

            for t in range(NT + 1):
                if t < NT:
                    dve.wait_ge(c_scores, t + 1)
                    s = bank[t % 3][:, :].rearrange("p (a s) -> p a s", s=S)
                    then(V.tensor_reduce(sm[:, t, 0, :], s, AX.X, ALU.max))
                    if t >= 3:
                        dve.wait_ge(c_tr, t - 2)
                    V.tensor_tensor(Es[:, t % 3, :].rearrange("p (a s) -> p a s", s=S), s,
                                    per_row(sm[:, t, 0, :], S), ALU.subtract).then_inc(c_sub, 1)
                if t >= 1:
                    probs1(t - 1)
                if t >= 4:
                    add1(t - 4)
            for t in range(NT - 3, NT):
                add1(t)
            dve.wait_ge(c_added, NT)

            layernorm(5)
            copy_xt(5)
            dve.wait_ge(r_psum, 1)
            softmax_small(bank[2][:, 0:NT * E1].rearrange("p (t e) -> p t e", e=E1), r_sub, r_exp)
            prob = rt[:, 0, :, :]
            prob_et = rt[:, 0, :, :].rearrange("p t e -> p e t")
            then(V.memset(thr[:, :], 0))
            search = BITS // STEP

            def candidates(shift):
                then(V.tensor_scalar(cand[:, :, :], jconst[:, :, :], shift, None, ALU.logical_shift_left))
                then(V.tensor_tensor(cand[:, :, :], cand[:, :, :], thr[:, :].unsqueeze(1).broadcast_to([P, NC, E1]),
                                     ALU.bitwise_or))

            for i in range(search):
                shift = BITS - STEP * (i + 1)
                candidates(shift)
                for j in range(NC):
                    last = V.tensor_tensor(hit[:, j * E1:(j + 1) * E1, :], prob_et, per_row(cand[:, j, :].bitcast(fp32), NT),
                                           ALU.is_ge)
                last.then_inc(r_hit, 1)
                dve.wait_ge(r_cnt, i + 1)
                then(V.tensor_reduce(cnt[:, :, :].rearrange("p j e -> p (j e)"),
                                     bank[3][:, 0:NC * E1 * NT].rearrange("p (a t) -> p a t", t=NT), AX.X, ALU.add))
                then(V.tensor_scalar(acc[:, :, :], cnt[:, :, :], CAP - 0.5, float(2 ** shift), ALU.is_ge, ALU.mult))
                with nc.allow_low_precision(reason="up to NC times one power of two: exact"):
                    then(V.tensor_reduce(add[:, :], acc[:, :, :].rearrange("p j e -> p e j"), AX.X, ALU.add))
                then(V.tensor_tensor(thr[:, :], thr[:, :], add[:, :], ALU.bitwise_or))
            level = thr[:, :].bitcast(fp32).unsqueeze(1).broadcast_to([P, NT, E1])
            above, tie, ahead = rt[:, 6, :, :], rt[:, 7, :, :], rt[:, 8, :, :]
            then(V.memset(hit[:, :, :], 0.0))
            then(V.tensor_tensor(above, prob, level, ALU.is_gt))
            V.tensor_copy(hit[:, 0:E1, :], above.rearrange("p t e -> p e t")).then_inc(r_hit, 1)
            V.tensor_tensor(tie, prob, level, ALU.is_equal)
            V.tensor_tensor(eqb[:, :, :], prob, level, ALU.is_equal).then_inc(r_eq, 1)
            dve.wait_ge(r_cnt, search + 1)
            then(V.tensor_reduce(cnt[:, 0, :], bank[3][:, 0:E1 * NT].rearrange("p (a t) -> p a t", t=NT), AX.X, ALU.add))
            then(V.tensor_scalar(acc[:, 0, :], cnt[:, 0, :], -1.0, float(CAP), ALU.mult, ALU.add))
            dve.wait_ge(r_pre, 1)
            then(V.tensor_tensor(ahead, bank[2][:, 0:NT * E1].rearrange("p (t e) -> p t e", e=E1),
                                 acc[:, 0, :].unsqueeze(1).broadcast_to([P, NT, E1]), ALU.is_lt))
            then(V.tensor_tensor(ahead, ahead, tie, ALU.mult))
            then(V.tensor_tensor(above, above, ahead, ALU.add))
            then(V.tensor_reduce(rv[:, 5, :], above, AX.X, ALU.max))
            then(V.tensor_tensor(tie, above, per_row(rv[:, 5, :], E1), ALU.subtract))
            then(V.scalar_tensor_tensor(tie, tie, 4.0, prob, ALU.mult, ALU.add))
            first_max(tie, ahead)
            then(V.tensor_tensor(rt[:, 9, :, :], ahead, prob, ALU.mult))
            for e in range(E1):
                for t in range(NT):
                    if t % 4 == 0:
                        dve.wait_ge(m_ys, 2 * e + t // 4 + 1)
                    last = V.scalar_tensor_tensor(X[:, t, :], ys[:, e, t, :], rt[:, 9, t, e:e + 1], X[:, t, :],
                                                  ALU.mult, ALU.add)
                    if e == E1 - 1:
                        last.then_inc(m_done, 1)
                if e < E1 - 1:
                    then(last)


_NAMES = ["x", "ctx_768", "mask_BxS2_bk0", "L0_attn_qkv_kernel", "L0_attn_qkv_bias", "L0_xattn_Wq", "L0_xattn_bq",
          "L0_xattn_Wk", "L0_xattn_bk", "L0_xattn_Wv", "L0_xattn_bv", "L0_ffn_gate_w", "L0_ffn_w1", "L0_ffn_b1",
          "L0_ffn_w2", "L0_ffn_b2", "L0_ffn_w3", "L0_ffn_b3", "L0_ffn_sw1", "L0_ffn_sb1", "L0_ffn_sw2", "L0_ffn_sb2",
          "L0_ffn_sw3", "L0_ffn_sb3", "L1_attn_A", "L1_attn_B", "L1_attn_C", "L1_attn_gamma", "L1_attn_beta",
          "L1_xattn_W_q", "L1_xattn_W_k", "L1_xattn_W_v", "L1_xattn_W_o", "L1_xattn_b_o", "L1_ffn_Wg", "L1_ffn_W1",
          "L1_ffn_W2"]


def kernel(**inputs):
    import numpy as np
    import concourse.bacc as bacc
    from concourse import mybir as _mybir
    from concourse.bass_utils import run_bass_kernel_spmd

    nc = bacc.Bacc("TRN2", target_bir_lowering=False, num_devices=1)
    arrays, w = {}, {}
    for name in _NAMES:
        a = np.ascontiguousarray(inputs[name])
        arrays[f"in_{name}"] = a
        w[name] = nc.dram_tensor(f"in_{name}", a.shape, _mybir.dt.from_np(a.dtype), kind="ExternalInput").ap()
    out = nc.dram_tensor("out", arrays["in_x"].shape, _mybir.dt.float32, kind="ExternalOutput").ap()
    decoder_kernel(nc, w, out)
    r = run_bass_kernel_spmd(nc, [arrays], core_ids=[0])
    return r.results[0]["out"]
```

```python
import concourse.bass as bass
from concourse import mybir
from contextlib import ExitStack


def decoder_kernel(nc: bass.Bass, w, out):
    fp32 = mybir.dt.float32
    bf16 = mybir.dt.bfloat16
    int32 = mybir.dt.int32
    uint8 = mybir.dt.uint8
    ALU = mybir.AluOpType
    ACT = mybir.ActivationFunctionType
    AX = mybir.AxisListType

    B, S, D = w["x"].shape
    DC = w["ctx_768"].shape[2]
    P = 128
    NT = B * S // P
    N = B * S
    HALF = N // 2
    EPS = 1e-5

    CH, HD = 16, 8
    GT = S // CH
    NPAIR = S // (2 * GT)
    VW = 2 * HD + 1
    VN = 6 * VW
    TERMS = 9
    ATTN_SCALE = 1.0 / (2.0 * D) ** 0.5
    XATTN0_SCALE = 1.0 / float(D) ** 0.5
    H1, DH1 = 8, 64
    XATTN1_SCALE = DH1 ** -0.5
    NHP = H1 // 2
    E0 = 8
    E1 = 8
    F1 = w["L1_ffn_W1"].shape[2] // P
    CAP = N // E1
    NS = 32
    BQ = P // NS
    ROUNDS = 6
    CLAMP = 1.0e6
    BITS, STEP = 30, 2
    NC = 2 ** STEP - 1
    HT = NT // 2
    HB = B // 2

    ctx = ExitStack()
    with ctx:
        def sb(name, shape, dt=fp32):
            return ctx.enter_context(nc.sbuf_tensor(name, shape, dt))

        def sem(name):
            return ctx.enter_context(nc.semaphore(name))

        def per_row(ap, n):
            return ap.unsqueeze(2).broadcast_to([ap.shape[0], ap.shape[1], n])

        def per_col(ap, n):
            return ap.unsqueeze(1).broadcast_to([ap.shape[0], n, ap.shape[1]])

        bank = [ctx.enter_context(nc.psum_tensor(f"bank{i}", [P, 512], fp32)) for i in range(8)]


        X = sb("X", [P, NT, D])
        XN = sb("XN", [P, NT, D])
        XT = sb("XT", [P, N])
        stats = sb("stats", [P, NT, 6])
        mv = sb("mv", [P, NT, 2])
        rs = sb("rs", [P, 5, NT])
        CTX = sb("CTX", [P, NT, DC])
        CTXT = sb("CTXT", [DC, N])
        ident = sb("ident", [P, P])
        perm = sb("perm", [P, P], bf16)
        causal = sb("causal", [P, NPAIR, S], bf16)
        onesb = sb("onesb", [P, P], bf16)
        trib = sb("trib", [P, P], bf16)
        em8 = sb("em8", [P, NT, E0])
        jconst = sb("jconst", [P, NC, E1], int32)
        magic = sb("magic", [P, HT], int32)
        vecs = sb("vecs", [31, P])
        cols = sb("cols", [P, 31])
        Wp = sb("Wp", [P, 3, D])
        Wq0 = sb("Wq0", [P, D])
        Wk0 = sb("Wk0", [DC, D])
        Wv0 = sb("Wv0", [DC, D])
        bv0 = sb("bv0", [P, D])
        W1a = sb("W1a", [P, E0 + 1, D])
        W3a = sb("W3a", [P, E0 + 1, D])
        W2a = sb("W2a", [P, E0 + 1, D])
        b2a = sb("b2a", [E0 + 1, D])
        Bn = sb("Bn", [NS, D])
        Cn = sb("Cn", [P, BQ, NS])
        BT = sb("BT", [P, NS])
        CT = sb("CT", [P, BQ, D])
        Apow = sb("Apow", [P, ROUNDS, 2, P])
        gamma = sb("gamma", [P, D])
        beta = sb("beta", [P, D])
        bo = sb("bo", [P, D])
        Wq1 = sb("Wq1", [P, H1 * DH1])
        Wk1 = sb("Wk1", [DC, H1 * DH1])
        Wv1 = sb("Wv1", [DC, H1 * DH1])
        Wo1 = sb("Wo1", [P, NHP, D])
        Wqkv = Wo1[:, 0:3, :].rearrange("p a d -> p (a d)")
        Wg = sb("Wg", [P, E1])
        Wb = sb("Wb", [P, 2 * E1 * F1 * P])
        W1b = Wb[:, 0:E1 * F1 * P].rearrange("p (e f) -> p e f", e=E1)
        W2b = Wb[:, E1 * F1 * P:].rearrange("p (e k d) -> p e k d", e=E1, d=D)
        QS = Wb[:, 0:3 * N].bitcast(bf16).rearrange("p (s a n) -> p s a n", s=2, a=3)
        masku = sb("masku", [P, N], uint8)
        maskf = sb("maskf", [P, N])
        maskrow = sb("maskrow", [1, N], bf16)
        QKVT = sb("QKVT", [P, 3, N])
        big = sb("big", [P, 16 * N])
        Q9 = big[0:TERMS * HD, 0:8 * N].bitcast(bf16).rearrange("p (h n) -> p h n", h=2)
        K9 = big[0:TERMS * HD, 8 * N:].bitcast(bf16).rearrange("p (h n) -> p h n", h=2)
        K1T = big[:, 0:4 * N].rearrange("p (a n) -> p a n", n=N)
        V1 = big[:, 4 * N:8 * N].rearrange("p (t n) -> p t n", t=NT)
        ys = big[:, 8 * N:].rearrange("p (e t d) -> p e t d", e=E1, d=D)
        V2 = sb("V2", [P, CH, S])
        VB = B * NPAIR * VW
        VP = VB + VN - 2 * VW
        att = sb("att", [P, VP + 2 * N])
        Vb = att[:, 0:VB].rearrange("p (b q r v) -> p b q r v", b=B, r=2, v=VW)
        Opos = att[:, VP:VP + N].rearrange("p (h a e b) -> p h a e b", h=2, a=NPAIR, e=HD)
        V2r = att[:, VP + N:VP + 2 * N].rearrange("p (q g r c t) -> p q g r c t", g=2, r=2, t=GT, c=CH)
        OT2 = att[0:S, VP + N:VP + 2 * N].rearrange("p (c s) -> p c s", s=S)
        OT = sb("OT", [P, N])
        mx0 = sb("mx0", [P, B, NPAIR])
        Es = sb("Es", [P, 3, 512])
        PTs = sb("PTs", [P, 2, 512])
        rO = sb("rO", [P, B, NPAIR])
        K0T = sb("K0T", [P, N])
        V0 = sb("V0", [P, NT, D])
        Q0T = QKVT[:, 0, :]
        E0s = QKVT[:, 1, :]
        hid = att[:, 0:4 * N].rearrange("p (a b n) -> p a b n", a=2, b=2)
        Q1T = att[:, 0:4 * N].rearrange("p (a n) -> p a n", a=4)
        sm = sb("sm", [P, NT + 2, 3, 8])
        OTs = V2[:, :, :].rearrange("p c s -> p (c s)").rearrange("p (a h n) -> p a h n", a=2, n=P)
        rt = sb("rt", [P, 10, NT, E0])
        rv = sb("rv", [P, 6, NT])
        comb = sb("comb", [P, NT, E0 + 1])
        combT = OT[0:E0 + 1, :]
        hid0 = att[:, 0:N].rearrange("p (a n) -> p a n", a=2)
        sil0 = att[:, N:N + HALF]
        thr = sb("thr", [P, E1], int32)
        cand = sb("cand", [P, NC, E1], int32)
        hit = sb("hit", [P, NC * E1, NT], bf16)
        cnt = sb("cnt", [P, NC, E1])
        acc = sb("acc", [P, NC, E1])
        add = sb("add", [P, E1], int32)
        eqb = sb("eqb", [P, NT, E1], bf16)
        ST = sb("ST", [P, 2, 2, S])
        GA = QKVT[:, 2, :].rearrange("p (t d) -> p t d", d=D)
        GB = XN[:, :, :]
        nanm = QKVT[:, 1, :].bitcast(int32).rearrange("p (t d) -> p t d", d=D)

        qk_d = nc.dram_tensor("qk_scratch", [2, 2, 3, HD, CH, HALF], bf16).ap()
        v_d = nc.dram_tensor("v_scratch", [P, N], fp32).ap()
        o_d = nc.dram_tensor("o_scratch", [2, P, HALF], fp32).ap()

        def pair_of(name):
            return [sem(f"{name}_a"), sem(f"{name}_b")]

        ld_x = pair_of("ld_x")
        ld_ctx = sem("ld_ctx")
        ld_vecs = sem("ld_vecs")
        ld_qkv = sem("ld_qkv")
        ld_x0 = sem("ld_x0")
        ld_bv = sem("ld_bv")
        ld_mask = sem("ld_mask")
        ld_ssm = sem("ld_ssm")
        ld_x1 = sem("ld_x1")
        ld_f0 = sem("ld_f0")
        ld_f1 = sem("ld_f1")
        ld_rows = sem("ld_rows")
        c_zero = sem("c_zero")
        c_ident = sem("c_ident")
        c_magic = sem("c_magic")
        c_azero = sem("c_azero")
        c_fill = sem("c_fill")
        c_wp = sem("c_wp")
        c_misc = sem("c_misc")
        v_step = sem("v_step")
        xn_ready = pair_of("xn_ready")
        xt_psum = pair_of("xt_psum")
        xt_ready = pair_of("xt_ready")
        prep_psum = sem("prep_psum")
        prep_act = sem("prep_act")
        v0_psum = sem("v0_psum")
        v0_ready = sem("v0_ready")
        mask_ready = sem("mask_ready")
        k1_psum = sem("k1_psum")
        k1_ready = sem("k1_ready")
        v1_psum = sem("v1_psum")
        v1_ready = sem("v1_ready")
        pow_psum = sem("pow_psum")
        pow_ready = sem("pow_ready")
        qk_psum = sem("qk_psum")
        qk_copied = sem("qk_copied")
        qk_rest = sem("qk_rest")
        qk_mid = sem("qk_mid")
        qk_low = sem("qk_low")
        v_psum = sem("v_psum")
        v_copied = sem("v_copied")
        st_qk = [pair_of("st_q"), pair_of("st_k")]
        ld_qk = pair_of("ld_qk")
        st_v = sem("st_v")
        ld_v2 = sem("ld_v2")
        v_order = sem("v_order")
        v2_psum = sem("v2_psum")
        vb_act = sem("vb_act")
        vb_dve = sem("vb_dve")
        a_scores = sem("a_scores")
        a_sub = sem("a_sub")
        a_exp = sem("a_exp")
        a_tr = sem("a_tr")
        a_trc = sem("a_trc")
        a_pv = sem("a_pv")
        a_norm = sem("a_norm")
        o_psum = pair_of("o_psum")
        o_act = pair_of("o_act")
        o_dve = pair_of("o_dve")
        st_o = pair_of("st_o")
        ld_o = pair_of("ld_o")
        x_psum = pair_of("x_psum")
        x_added = pair_of("x_added")
        b_q = pair_of("b_q")
        b_qc = pair_of("b_qc")
        b_scores = pair_of("b_scores")
        b_sub = pair_of("b_sub")
        b_exp = pair_of("b_exp")
        b_prob = pair_of("b_prob")
        b_tr = pair_of("b_tr")
        b_trc = pair_of("b_trc")
        b_pv = pair_of("b_pv")
        b_added = pair_of("b_added")
        g_psum = pair_of("g_psum")
        g_sub = pair_of("g_sub")
        g_exp = pair_of("g_exp")
        g_comb = pair_of("g_comb")
        g_combt = pair_of("g_combt")
        g_combc = pair_of("g_combc")
        f_h1 = sem("f_h1")
        f_h3 = sem("f_h3")
        f_silu = sem("f_silu")
        f_h = sem("f_h")
        f_out = sem("f_out")
        f_acc = sem("f_acc")
        s_psum = pair_of("s_psum")
        s_state = pair_of("s_state")
        s_y = pair_of("s_y")
        s_gelu = pair_of("s_gelu")
        c_q = pair_of("c_q")
        c_qc = pair_of("c_qc")
        c_scores = sem("c_scores")
        c_sub = sem("c_sub")
        c_exp = sem("c_exp")
        c_prob = sem("c_prob")
        c_tr = sem("c_tr")
        c_trc = sem("c_trc")
        c_pv = sem("c_pv")
        c_otc = sem("c_otc")
        c_wo = sem("c_wo")
        c_added = sem("c_added")
        r_psum = sem("r_psum")
        r_sub = sem("r_sub")
        r_exp = sem("r_exp")
        r_hit = sem("r_hit")
        r_cnt = sem("r_cnt")
        r_eq = sem("r_eq")
        r_pre = sem("r_pre")
        m_up = sem("m_up")
        m_gelu = sem("m_gelu")
        m_down = sem("m_down")
        m_ys = sem("m_ys")
        m_done = sem("m_done")
        st_out = sem("st_out")

        block = ctx.enter_context(nc.Block())

        def half(h):
            return slice(h * HALF, (h + 1) * HALF)

        def tiles(h):
            return slice(h * HT, (h + 1) * HT)

        SEARCH = BITS // STEP

        @block.sync
        def _(sp):
            def tokens(ap):
                return ap.rearrange("b s d -> (b s) d").rearrange("(t p) d -> p t d", p=P)

            for h in range(2):
                sp.dma_start(X[:, tiles(h), :], tokens(w["x"])[:, tiles(h), :]).then_inc(ld_x[h], 16)
            sp.dma_start(Wqkv[:, :], w["L0_attn_qkv_kernel"]).then_inc(ld_qkv, 16)
            sp.dma_start(vecs[0:3, :].rearrange("s (c e) -> s c e", e=HD),
                         w["L0_attn_qkv_bias"].rearrange("o (c s e) -> (o s) c e", s=3, e=HD)).then_inc(ld_vecs, 16)
            for row, name in ((3, "L0_xattn_bq"), (4, "L0_xattn_bk"), (13, "L0_ffn_sb1"), (22, "L0_ffn_sb3")):
                sp.dma_start(vecs[row:row + 1, :], w[name].unsqueeze(0)).then_inc(ld_vecs, 16)
            for row, name in ((5, "L0_ffn_b1"), (14, "L0_ffn_b3"), (23, "L0_ffn_gate_w")):
                sp.dma_start(vecs[row:row + 8, :], w[name]).then_inc(ld_vecs, 16)
            sp.dma_start(CTX[:, :, :], tokens(w["ctx_768"])).then_inc(ld_ctx, 16)
            sp.dma_start(Wk0[:, :], w["L0_xattn_Wk"]).then_inc(ld_x0, 16)
            sp.dma_start(Wv0[:, :], w["L0_xattn_Wv"]).then_inc(ld_x0, 16)
            sp.dma_start(Wq0[:, :], w["L0_xattn_Wq"]).then_inc(ld_x0, 16)

            for h in range(2):
                for s in range(2):
                    i = 2 * h + s
                    sp.wait_ge(qk_low, i + 1)
                    for a in range(3):
                        sp.dma_start(qk_d[s, h, a, :, :, :].rearrange("e c n -> c e n"),
                                     QS[:, s, a, half(h)]).then_inc(st_qk[s][h], 16)
                for s in range(2):
                    sp.wait_ge(st_qk[s][h], 48)
                    parts = qk_d[s, h, :, :, :, :].rearrange("a e c n -> a e (c n)")
                    for j in range(3):
                        for first, last, at in (((0, 3, 0),) if s == 0 or j == 0 else ((j, 3, 0), (0, j, 3 - j))):
                            rows = slice((3 * j + at) * HD, (3 * j + at + last - first) * HD)
                            dst = (Q9, K9)[s][rows, h, :]
                            sp.dma_start(dst, parts[first:last, :, :].rearrange("a e n -> (a e) n")
                                         ).then_inc(ld_qk[h], 16)
                if h == 0:
                    sp.wait_ge(v_copied, 2)
                    sp.dma_start(v_d, QKVT[:, 2, :]).then_inc(st_v, 16)
                    sp.wait_ge(st_v, 16)
                    sp.dma_start(V2[:, :, :], v_d.rearrange("(c e) (b s) -> e b c s", e=HD, s=S)
                                 .rearrange("e b c s -> (e b) c s")).then_inc(ld_v2, 16)

            for h in range(2):
                sp.wait_ge(o_act[h], 1)
                sp.wait_ge(o_dve[h], 1)
                sp.dma_start(o_d[h, :, :].rearrange("(c e) (b s) -> e b c s", e=HD, s=S)
                             .rearrange("e b c s -> (e b) c s"), OT2).then_inc(st_o[h], 16)
                sp.wait_ge(st_o[h], 16)
                sp.dma_start(OT[:, half(h)], o_d[h, :, :]).then_inc(ld_o[h], 16)
                if h == 0:
                    for s in range(2):
                        for part_h in range(2):
                            sp.wait_ge(st_qk[s][part_h], 48)
                    sp.dma_start(W1b, w["L1_ffn_W1"].rearrange("e d f -> d e f")).then_inc(ld_f1, 16)
                    for e in range(E1):
                        sp.dma_start(W2b[:, e, :, :], w["L1_ffn_W2"][e, :, :].rearrange("(k p) d -> p k d", p=P)
                                     ).then_inc(ld_f1, 16)

            for t in range(NT):
                sp.wait_ge(m_done, t + 1)
                sp.dma_start(out.rearrange("b s d -> (b s) d")[t * P:(t + 1) * P, :], X[:, t, :]
                             ).then_inc(st_out, 16)
            sp.wait_ge(st_out, 16 * NT)

        @block.gpsimd
        def _(pool):
            nc.gpsimd.memset(ident[:, :], 0.0).then_inc(c_zero, 1)
            nc.gpsimd.memset(magic[:, :], 0x5f3759df).then_inc(c_magic, 1)
            pool.wait_ge(c_zero, 1)
            nc.gpsimd.affine_select(out=ident[:, :], in_=ident[:, :], compare_op=ALU.not_equal, fill=1.0, base=0,
                                    pattern=[[-1, P]], channel_multiplier=1).then_inc(c_ident, 1)
            nc.gpsimd.memset(Apow[:, 0, 0, :], 0.0).then_inc(c_azero, 1)
            pool.wait_ge(ld_qkv, 16)
            nc.gpsimd.tensor_copy(Wp[:, :, :].rearrange("d s (c e) -> d c s e", e=HD),
                                  Wqkv[:, :].rearrange("d (c s e) -> d c s e", s=3, e=HD)).then_inc(c_wp, 1)
            pool.wait_ge(c_azero, 1)
            for q in range(BQ):
                pool.dma_start(Apow[q * NS:(q + 1) * NS, 0, 0, q * NS:(q + 1) * NS], w["L1_attn_A"]
                               ).then_inc(ld_ssm, 16)
                pool.dma_start(Cn[:, q, :], w["L1_attn_C"]).then_inc(ld_ssm, 16)
            pool.dma_start(Bn[:, :], w["L1_attn_B"]).then_inc(ld_ssm, 16)
            pool.dma_start(bv0[:, :], w["L0_xattn_bv"].partition_broadcast(P)).then_inc(ld_bv, 16)
            nc.gpsimd.memset(causal[:, :, :], 0.0).then_inc(c_fill, 1)
            nc.gpsimd.memset(trib[:, :], 1.0).then_inc(c_fill, 1)
            nc.gpsimd.memset(att[:, 0:VP], 0.0).then_inc(c_fill, 1)
            nc.gpsimd.memset(CT[:, :, :], 0.0).then_inc(c_fill, 1)
            nc.gpsimd.iota(jconst[:, :, :], pattern=[[1, NC], [0, E1]], base=1, channel_multiplier=0).then_inc(c_misc, 1)
            nc.gpsimd.memset(onesb[:, :], 1.0).then_inc(c_misc, 1)
            pool.wait_ge(c_ident, 1)
            nc.gpsimd.tensor_copy(perm[:, :].rearrange("k (g c t) -> k g c t", g=2, c=CH),
                                  ident[:, :].rearrange("k (g t c) -> k g c t", g=2, c=CH)).then_inc(c_misc, 1)
            for e in range(E0):
                nc.gpsimd.memset(em8[:, :, e], float(e - E0)).then_inc(c_misc, 1)
            nc.gpsimd.memset(comb[:, :, E0], 1.0).then_inc(c_misc, 1)
            pool.wait_ge(c_fill, 4)
            pool.wait_ge(c_wp, 1)
            for g2 in range(2):
                pool.wait_ge(c_misc, 4 + E0 + g2)
                part = causal[g2 * S:(g2 + 1) * S, :, :]
                nc.gpsimd.affine_select(out=part, in_=part, compare_op=ALU.is_ge, fill=-1.0e38, base=0,
                                        pattern=[[0, NPAIR], [-1, S]], channel_multiplier=1).then_inc(c_misc, 1)
            pool.wait_ge(c_misc, 4 + E0 + 2)
            nc.gpsimd.affine_select(out=trib[:, :], in_=trib[:, :], compare_op=ALU.is_gt, fill=0.0, base=0,
                                    pattern=[[1, P]], channel_multiplier=-1).then_inc(c_misc, 1)
            for p2 in range(2):
                pool.wait_ge(c_misc, 4 + E0 + 3 + p2)
                nc.gpsimd.memset(Vb[p2 * S:(p2 + 1) * S, :, :, p2, 2 * HD], 1.0).then_inc(c_misc, 1)
            pool.dma_start(masku[:, :], w["mask_BxS2_bk0"].rearrange("b s -> (b s)").partition_broadcast(P)
                           ).then_inc(ld_mask, 16)
            pool.dma_start(Wk1[:, :], w["L1_xattn_W_k"]).then_inc(ld_x1, 16)
            pool.dma_start(Wv1[:, :], w["L1_xattn_W_v"]).then_inc(ld_x1, 16)
            pool.dma_start(Wq1[:, :], w["L1_xattn_W_q"]).then_inc(ld_x1, 16)
            pool.dma_start(Wo1[:, :, :], w["L1_xattn_W_o"].rearrange("(h p) d -> p h d", p=P)).then_inc(ld_x1, 16)
            for dst, name, one in ((W1a, "L0_ffn_w1", "L0_ffn_sw1"), (W3a, "L0_ffn_w3", "L0_ffn_sw3"),
                                   (W2a, "L0_ffn_w2", "L0_ffn_sw2")):
                pool.dma_start(dst[:, 0:E0, :], w[name].rearrange("e d f -> d e f")).then_inc(ld_f0, 16)
                pool.dma_start(dst[:, E0, :], w[one]).then_inc(ld_f0, 16)
            pool.dma_start(b2a[0:E0, :], w["L0_ffn_b2"]).then_inc(ld_f0, 16)
            pool.dma_start(b2a[E0:E0 + 1, :], w["L0_ffn_sb2"].unsqueeze(0)).then_inc(ld_f0, 16)
            for dst, name in ((gamma, "L1_attn_gamma"), (beta, "L1_attn_beta"), (bo, "L1_xattn_b_o")):
                pool.dma_start(dst[:, :], w[name].partition_broadcast(P)).then_inc(ld_rows, 16)
            pool.dma_start(Wg[:, :], w["L1_ffn_Wg"]).then_inc(ld_rows, 16)
        C_MISC = 4 + E0 + 2 + 1 + 2

        @block.tensor
        def _(pe):
            mm = nc.tensor.matmul

            def transpose_xn(n, h, b):
                pe.wait_ge(xn_ready[h], HT * (n + 1))
                if n == 2 and h == 0:
                    pe.wait_ge(xt_ready[1], 2)
                if n == 2 and h == 1:
                    pe.wait_ge(g_combc[0], 1)
                if n == 3 and h == 0:
                    pe.wait_ge(g_combc[1], 1)
                for t in range(HT):
                    last = nc.tensor.transpose(bank[b][:, t * P:(t + 1) * P], XN[:, h * HT + t, :], ident[:, :])
                last.then_inc(xt_psum[h], 1)

            pe.wait_ge(c_ident, 1)
            pe.wait_ge(ld_vecs, 128)
            nc.tensor.transpose(bank[4][:, 0:31], vecs[:, :], ident[0:31, 0:31]).then_inc(prep_psum, 1)
            for h in range(2):
                transpose_xn(0, h, h)
            pe.wait_ge(c_wp, 1)
            for h in range(2):
                pe.wait_ge(xt_ready[h], 1)
                for s in range(2):
                    if h == 1 and s == 0:
                        pe.wait_ge(prep_act, 1)
                    mm(bank[2 + 2 * h + s][:, :], Wp[:, s, :], XT[:, half(h)].rearrange("d (g t) -> d t g", t=GT),
                       start=True, stop=True).then_inc(qk_psum, 1)
            for h in range(2):
                mm(bank[6 + h][:, :], Wp[:, 2, :], XT[:, half(h)], start=True, stop=True).then_inc(v_psum, 1)
            pe.wait_ge(ld_ctx, 16)
            for h in range(2):
                pe.wait_ge(xt_ready[h], 1)
                for t in range(HT):
                    last = nc.tensor.transpose(bank[h][0:DC, t * P:(t + 1) * P], CTX[:, HT * h + t, :], ident[:, :])
                last.then_inc(prep_psum, 1)
            pe.wait_ge(ld_ssm, 144)
            pe.wait_ge(qk_copied, 1)
            nc.tensor.transpose(bank[2][:, 0:NS], Bn[:, :], ident[0:NS, 0:NS])
            nc.tensor.transpose(bank[2][:, NS:NS + P], Cn[:, :, :].rearrange("p q n -> p (q n)"), ident[:, :])
            nc.tensor.transpose(bank[2][:, NS + P:NS + 2 * P], Apow[:, 0, 0, :], ident[:, :]).then_inc(prep_psum, 1)
            pe.wait_ge(ld_x0, 48)
            pe.wait_ge(prep_act, 3)
            for h in range(2):
                mm(bank[h][:, :], Wk0[:, :], CTXT[:, half(h)], start=True, stop=True).then_inc(prep_psum, 1)
            pe.wait_ge(v_copied, 2)
            for h in range(2):
                for t in range(HT):
                    last = mm(bank[6 + h][:, t * P:(t + 1) * P], CTXT[:, (HT * h + t) * P:(HT * h + t + 1) * P],
                              Wv0[:, :], start=True, stop=True)
                last.then_inc(v0_psum, 1)
            pe.wait_ge(qk_copied, 4)
            for r in range(1, ROUNDS):
                pe.wait_ge(pow_ready, r)
                mm(bank[3][:, 0:P], Apow[:, r - 1, 1, :], Apow[:, r - 1, 0, :], start=True, stop=True)
                mm(bank[3][:, P:2 * P], Apow[:, r - 1, 0, :], Apow[:, r - 1, 1, :], start=True, stop=True
                   ).then_inc(pow_psum, 1)
            pe.wait_ge(v_order, 4)
            pe.wait_ge(v0_ready, 2)
            for g2 in range(2):
                for p4 in range(4):
                    src = V2r[:, p4, g2, :, :, :].rearrange("p r c t -> p (r c t)")
                    last = nc.tensor.transpose(bank[6 + g2][:, p4 * P:(p4 + 1) * P], src, ident[:, :])
                last.then_inc(v2_psum, 1)

            def head_cols(t, n, pair, g2):
                head = (n % HB) * 2 * NPAIR + 2 * pair + g2
                return t[:, n // HB, :].rearrange("p (s g) -> p s g", s=S)[:, :, head]

            def scores(n):
                if n % HB == 0:
                    pe.wait_ge(ld_qk[n // HB], 128)
                if n == 0:
                    pe.wait_ge(c_misc, C_MISC)
                    pe.wait_ge(prep_act, 5)
                    pe.wait_ge(pow_ready, ROUNDS)
                if n >= 3:
                    pe.wait_ge(a_sub, n - 2)
                dst = bank[n % 3]
                mm(dst[:, :], perm[:, :], causal[:, :, :].rearrange("p a (t c) -> p a c t", c=CH), start=True,
                   stop=False, skip_group_check=True)
                for pair in range(NPAIR):
                    for g2 in range(2):
                        last = mm(dst[g2 * S:(g2 + 1) * S, pair * S:(pair + 1) * S], head_cols(Q9, n, pair, g2),
                                  head_cols(K9, n, pair, g2), start=False, stop=(pair == NPAIR - 1),
                                  skip_group_check=True)
                last.then_inc(a_scores, 1)

            def transpose_probs(n):
                pe.wait_ge(a_exp, n + 1)
                if n >= 2:
                    pe.wait_ge(a_trc, n - 1)
                for p4 in range(4):
                    last = nc.tensor.transpose(bank[3 + n % 2][:, p4 * P:(p4 + 1) * P],
                                               Es[:, n % 3, p4 * P:(p4 + 1) * P], ident[:, :])
                last.then_inc(a_tr, 1)

            def weigh_values(n):
                pe.wait_ge(a_trc, n + 1)
                if n == 0:
                    pe.wait_ge(vb_act, 2)
                    pe.wait_ge(vb_dve, 2)
                if n >= 1:
                    pe.wait_ge(a_norm, n)
                for p4 in range(4):
                    first = (4 * n + p4) * 2 * VW
                    last = mm(bank[5][:, p4 * VN:(p4 + 1) * VN],
                              PTs[:, n % 2, p4 * P:(p4 + 1) * P], att[:, first:first + VN], start=True, stop=True)
                last.then_inc(a_pv, 1)

            def outputs_by_feature(h):
                pe.wait_ge(a_norm, HB * (h + 1))
                if h == 0:
                    pe.wait_ge(vb_act, 2)
                    pe.wait_ge(vb_dve, 2)
                else:
                    pe.wait_ge(xt_ready[0], 2)
                for pair in range(NPAIR):
                    last = nc.tensor.transpose(bank[6 + pair // 4][0:S, (pair % 4) * P:(pair % 4 + 1) * P],
                                               Opos[:, h, pair, :, :].rearrange("p e b -> p (e b)"), ident[:, :])
                    if pair % 4 == 3:
                        last.then_inc(o_psum[h], 1)

            def outputs_by_token(h):
                pe.wait_ge(ld_o[h], 16)
                if h == 0:
                    pe.wait_ge(o_act[0], 1)
                else:
                    pe.wait_ge(b_added[0], 1)
                for t in range(HT):
                    last = nc.tensor.transpose(bank[6][:, t * P:(t + 1) * P],
                                               OT[:, (h * HT + t) * P:(h * HT + t + 1) * P], ident[:, :])
                last.then_inc(x_psum[h], 1)

            def cross0_q(h):
                pe.wait_ge(xt_ready[h], 2)
                if h == 0:
                    pe.wait_ge(o_act[1], 1)
                mm(bank[6][:, :], Wq0[:, :], XT[:, half(h)], start=True, stop=True).then_inc(b_q[h], 1)

            def cross0_scores(h):
                pe.wait_ge(b_qc[h], 1)
                pe.wait_ge(prep_act, 5)
                for i in range(HB):
                    u, o, r, b = i // 4, (i // 2) % 2, i % 2, h * HB + i
                    last = mm(bank[6][o * S:(o + 1) * S, (2 * u + r) * S:(2 * u + r + 1) * S],
                              Q0T[:, b * S:(b + 1) * S], K0T[:, b * S:(b + 1) * S], start=True, stop=True)
                last.then_inc(b_scores[h], 1)

            def cross0_transpose(h):
                pe.wait_ge(b_prob[h], 1)
                for u in range(2):
                    last = nc.tensor.transpose(bank[6][:, u * P:(u + 1) * P],
                                               E0s[:, h * HALF + u * P:h * HALF + (u + 1) * P], ident[:, :])
                last.then_inc(b_tr[h], 1)

            def cross0_values(h):
                pe.wait_ge(b_trc[h], 1)
                pe.wait_ge(v0_ready, 2)
                for i in range(HB):
                    u, o, r, t = i // 4, (i // 2) % 2, i % 2, i // 2
                    first = h * HALF + 2 * P + u * P + o * S
                    last = mm(bank[6][r * S:(r + 1) * S, t * P:(t + 1) * P], E0s[r * S:(r + 1) * S, first:first + S],
                              V0[r * S:(r + 1) * S, h * HT + t, :], start=True, stop=True)
                last.then_inc(b_pv[h], 1)

            def gate(h):
                pe.wait_ge(xt_ready[h], 3)
                for t in range(HT):
                    tt = h * HT + t
                    last = mm(bank[7][:, t * E0:(t + 1) * E0], XT[:, tt * P:(tt + 1) * P], cols[:, 23:31],
                              start=True, stop=True)
                last.then_inc(g_psum[h], 1)

            def gate_transpose(h):
                pe.wait_ge(g_comb[h], 1)
                for t in range(HT):
                    last = nc.tensor.transpose(bank[7][0:E0 + 1, t * P:(t + 1) * P], comb[:, h * HT + t, :],
                                               ident[:, :])
                last.then_inc(g_combt[h], 1)

            def up0(h, e):
                i = (E0 + 1) * h + e
                if i == 0:
                    pe.wait_ge(ld_f0, 128)
                    pe.wait_ge(a_norm, B)
                if i >= 2:
                    pe.wait_ge(f_silu, i - 1)
                mm(bank[i % 2][:, :], W1a[:, e, :], XT[:, half(h)], start=True, stop=True).then_inc(f_h1, 1)
                if i >= 2:
                    pe.wait_ge(f_h, i - 1)
                mm(bank[2 + i % 2][:, :], W3a[:, e, :], XT[:, half(h)], start=True, stop=True).then_inc(f_h3, 1)

            def down0(h, e):
                i = (E0 + 1) * h + e
                shared = e == E0
                pe.wait_ge(f_h, i + 1)
                if i >= 2:
                    pe.wait_ge(f_acc, i - 1)
                if shared:
                    pe.wait_ge(g_combc[h], 1)
                for t in range(HT):
                    dst = bank[4 + i % 2][:, t * P:(t + 1) * P]
                    tt = h * HT + t
                    last = mm(dst, hid0[:, i % 2, t * P:(t + 1) * P], W2a[:, e, :], start=True, stop=not shared)
                    if shared:
                        last = mm(dst, combT[:, tt * P:(tt + 1) * P], b2a[:, :], start=False, stop=True)
                last.then_inc(f_out, 1)

            def keys1(i, b):
                mm(bank[b][:, :], Wk1[:, (i // 2) * P:(i // 2 + 1) * P], CTXT[:, half(i % 2)], start=True, stop=True
                   ).then_inc(k1_psum, 1)

            def values1(i, b):
                mm(bank[b][:, :], CTXT[:, i * P:(i + 1) * P], Wv1[:, :], start=True, stop=True).then_inc(v1_psum, 1)

            def inject(h):
                pe.wait_ge(xt_ready[h], 4)
                for q in range(BQ):
                    first = h * HALF + q * 2 * S
                    last = mm(bank[7][q * NS:(q + 1) * NS, 0:2 * S], BT[:, :], XT[:, first:first + 2 * S],
                              start=True, stop=False, skip_group_check=True)
                last.then_inc(s_psum[h], 1)

            def widen(h, r):
                k = 2 ** r
                pe.wait_ge(s_state[h], r + 1)
                dst = bank[7][:, 0:2 * S].rearrange("p (b s) -> p b s", s=S)[:, :, k:S]
                mm(dst, Apow[:, r, 1, :], ST[:, h, :, 0:S - k], start=False, stop=(r == ROUNDS - 1),
                   skip_group_check=True).then_inc(s_psum[h], 1)

            def read_out(h):
                pe.wait_ge(s_state[h], ROUNDS + 1)
                if h == 1:
                    pe.wait_ge(xt_ready[0], 5)
                mm(bank[6][:, :], ST[:, h, :, :].rearrange("p b s -> p (b s)"),
                   CT[:, :, :].rearrange("p q d -> p (q d)"), start=True, stop=True).then_inc(s_y[h], 1)

            def queries1(h, i):
                if i == 0:
                    pe.wait_ge(xt_ready[h], 5)
                    pe.wait_ge(s_gelu[1], 1)
                if i >= 2:
                    pe.wait_ge(c_qc[h], i - 1)
                mm(bank[6 + i % 2][:, :], Wq1[:, i * P:(i + 1) * P], XT[:, half(h)], start=True, stop=True
                   ).then_inc(c_q[h], 1)

            def scores1(t):
                if t % HT == 0:
                    pe.wait_ge(c_qc[t // HT], 4)
                if t == 0:
                    pe.wait_ge(f_acc, 2 * (E0 + 1))
                    pe.wait_ge(mask_ready, 2)
                    pe.wait_ge(k1_ready, 8)
                if t >= 2:
                    pe.wait_ge(c_sub, t - 1)
                dst = bank[t % 2]
                bias = per_col(maskrow[0:1, t * P:(t + 1) * P], NHP)
                mm(dst[:, :], onesb[0:1, :], bias, start=True, stop=False, skip_group_check=True)
                for hp in range(NHP):
                    for b2 in range(2):
                        for h2 in range(2):
                            tok = slice(t * P + b2 * S, t * P + (b2 + 1) * S)
                            last = mm(dst[h2 * S:(h2 + 1) * S, (2 * hp + b2) * S:(2 * hp + b2 + 1) * S],
                                      Q1T[h2 * DH1:(h2 + 1) * DH1, hp, tok], K1T[h2 * DH1:(h2 + 1) * DH1, hp, tok],
                                      start=False, stop=(hp == NHP - 1), skip_group_check=True)
                last.then_inc(c_scores, 1)

            def transpose_probs1(t):
                pe.wait_ge(c_prob, t + 1)
                if t >= 1:
                    pe.wait_ge(c_trc, t)
                for hp in range(NHP):
                    last = nc.tensor.transpose(bank[2][:, hp * P:(hp + 1) * P],
                                               Es[:, t % 3, hp * P:(hp + 1) * P], ident[:, :])
                last.then_inc(c_tr, 1)

            def weigh_values1(t):
                pe.wait_ge(c_trc, t + 1)
                if t == 0:
                    pe.wait_ge(v1_ready, 8)
                if t >= 1:
                    pe.wait_ge(c_otc, 2 * t)
                for hp in range(NHP):
                    for b2 in range(2):
                        for h2 in range(2):
                            g = 2 * hp + h2
                            last = mm(bank[3 + b2][h2 * S:(h2 + 1) * S, hp * S:(hp + 1) * S],
                                      V1[b2 * S:(b2 + 1) * S, t, g * DH1:(g + 1) * DH1],
                                      PTs[b2 * S:(b2 + 1) * S, t % 2, hp * P + h2 * S:hp * P + (h2 + 1) * S],
                                      start=True, stop=True)
                last.then_inc(c_pv, 1)

            def project_out(t):
                pe.wait_ge(c_otc, 2 * t + 2)
                if t >= 1:
                    pe.wait_ge(c_added, t)
                for hp in range(NHP):
                    last = mm(bank[5][:, 0:D], OTs[:, t % 2, hp, :], Wo1[:, hp, :],
                              start=(hp == 0), stop=(hp == NHP - 1))
                last.then_inc(c_wo, 1)

            def up1(e, f, h):
                i = 4 * e + 2 * f + h
                if i == 0:
                    pe.wait_ge(c_otc, 2 * NT)
                    pe.wait_ge(ld_f1, 16 * (1 + E1))
                if i >= 4:
                    pe.wait_ge(m_gelu, i - 3)
                mm(bank[i % 4][:, :], W1b[:, e, f * P:(f + 1) * P], XT[:, half(h)], start=True, stop=True
                   ).then_inc(m_up, 1)

            def down1(e, h):
                pe.wait_ge(m_gelu, 4 * e + 2 + h + 1)
                if e >= 1:
                    pe.wait_ge(m_ys, 2 * (e - 1) + h + 1)
                for t in range(HT):
                    tile = slice((HT * h + t) * P, (HT * h + t + 1) * P)
                    for f in range(F1):
                        last = mm(bank[4 + h][:, t * P:(t + 1) * P], hid[:, e % 2, f, tile], W2b[:, e, f, :],
                                  start=(f == 0), stop=(f == F1 - 1))
                last.then_inc(m_down, 1)

            def route(h):
                pe.wait_ge(xt_ready[h], 6)
                pe.wait_ge(xt_ready[1], 6)
                for t in range(HT):
                    tt = HT * h + t
                    last = mm(bank[7][:, tt * E1:(tt + 1) * E1], XT[:, tt * P:(tt + 1) * P], Wg[:, :],
                              start=True, stop=True)
                last.then_inc(r_psum, 1)

            def count(i):
                pe.wait_ge(r_hit, i + 1)
                mm(bank[6][:, 0:NC * E1 * NT], onesb[:, :], hit[:, :, :].rearrange("p a t -> p (a t)"),
                   start=True, stop=True).then_inc(r_cnt, 1)

            def prefix():
                pe.wait_ge(r_eq, 1)
                mm(bank[7][:, 0:NT * E1], trib[:, :], eqb[:, :, :].rearrange("p t e -> p (t e)"),
                   start=True, stop=False, skip_group_check=True)
                for t in range(NT - 1):
                    last = mm(bank[7][:, (t + 1) * E1:NT * E1], onesb[:, :], per_col(eqb[:, t, :], NT - 1 - t),
                              start=False, stop=(t == NT - 2), skip_group_check=True)
                last.then_inc(r_pre, 1)

            for n in range(B + 3):
                if n < B:
                    scores(n)
                if 2 <= n < B + 2:
                    transpose_probs(n - 2)
                if n >= 3:
                    weigh_values(n - 3)
                if n == HB + 4:
                    outputs_by_feature(0)
                if n == HB + 7:
                    outputs_by_token(0)
                if n == B + 2:
                    transpose_xn(1, 0, 7)
            outputs_by_feature(1)
            cross0_q(0)
            cross0_scores(0)
            pe.wait_ge(a_norm, B)
            pe.wait_ge(ld_x1, 64)
            pe.wait_ge(mask_ready, 1)
            for i in range(2):
                keys1(i, i)
                values1(i, 3 + i)
            cross0_transpose(0)
            cross0_values(0)
            outputs_by_token(1)
            for i in range(2, 8):
                if i >= 3:
                    pe.wait_ge(k1_ready, i - 2)
                    pe.wait_ge(v1_ready, i - 2)
                keys1(i, i % 3)
                values1(i, 3 + i % 3)
                if i == 4:
                    transpose_xn(1, 1, 7)
            transpose_xn(2, 0, 7)
            cross0_q(1)
            cross0_scores(1)
            gate(0)
            pe.wait_ge(k1_ready, 8)
            pe.wait_ge(v1_ready, 8)
            up0(0, 0)
            cross0_transpose(1)
            cross0_values(1)
            gate_transpose(0)
            for e in range(E0 + 1):
                if e < E0:
                    up0(0, e + 1)
                else:
                    up0(1, 0)
                down0(0, e)
                if e == 2:
                    transpose_xn(2, 1, 7)
                if e == 3:
                    gate(1)
                if e == 5:
                    gate_transpose(1)
            for e in range(E0 + 1):
                if e < E0:
                    up0(1, e + 1)
                down0(1, e)
                if e == 2:
                    transpose_xn(3, 0, 7)
                if e == 3:
                    inject(0)
                if 4 <= e < 7:
                    widen(0, 2 * (e - 4))
                    widen(0, 2 * (e - 4) + 1)
                if e == 7:
                    read_out(0)
            transpose_xn(3, 1, 7)
            inject(1)
            for r in range(ROUNDS):
                widen(1, r)
            transpose_xn(4, 0, 6)
            read_out(1)
            for i in range(4):
                queries1(0, i)
            for t in range(NT + 3):
                if t < NT:
                    if t == HT:
                        transpose_xn(4, 1, 6)
                        for i in range(4):
                            queries1(1, i)
                    scores1(t)
                if 1 <= t < NT + 1:
                    transpose_probs1(t - 1)
                if 2 <= t < NT + 2:
                    weigh_values1(t - 2)
                if t >= 3:
                    project_out(t - 3)
            for h in range(2):
                transpose_xn(5, h, 6 + h)
            route(0)
            route(1)
            for f in range(F1):
                for h in range(2):
                    up1(0, f, h)
            done = slot = 0
            for e in range(E1):
                units = [(up1, e + 1, f, h) for f in range(F1) for h in range(2)] if e + 1 < E1 else []
                units += [(down1, e, h) for h in range(2)]
                for unit in units:
                    unit[0](*unit[1:])
                    slot += 1
                    if slot % 2 == 0 and done <= SEARCH:
                        count(done)
                        if done == SEARCH:
                            prefix()
                        done += 1
            assert done == SEARCH + 1

        @block.scalar
        def _(act):
            AF = nc.scalar.activation

            def copy_xt(n, h, b):
                act.wait_ge(xt_psum[h], n + 1)
                AF(XT[:, half(h)], bank[b][:, :], ACT.Copy).then_inc(xt_ready[h], 1)

            act.wait_ge(prep_psum, 1)
            AF(cols[:, :], bank[4][:, 0:31], ACT.Copy).then_inc(prep_act, 1)
            copy_xt(0, 0, 0)
            copy_xt(0, 1, 1)
            act.wait_ge(prep_act, 1)

            def mid_part(i):
                act.wait_ge(qk_rest, i + 1)
                AF(QS[:, i % 2, 1, half(i // 2)], OT[:, (i % 2) * HALF:(i % 2 + 1) * HALF], ACT.Copy
                   ).then_inc(qk_mid, 1)

            for i in range(4):
                h, s = i // 2, i % 2
                act.wait_ge(qk_psum, i + 1)
                AF(QKVT[:, s, half(h)], bank[2 + i][:, :], ACT.Identity, bias=cols[:, s:s + 1])
                AF(QS[:, s, 0, half(h)], bank[2 + i][:, :], ACT.Identity, bias=cols[:, s:s + 1]).then_inc(qk_copied, 1)
                if i >= 1:
                    mid_part(i - 1)
            mid_part(3)
            for h in range(2):
                act.wait_ge(prep_psum, 2 + h)
                AF(CTXT[:, half(h)], bank[h][0:DC, :], ACT.Copy).then_inc(prep_act, 1)
            act.wait_ge(prep_psum, 4)
            act.wait_ge(c_fill, 4)
            AF(BT[:, :], bank[2][:, 0:NS], ACT.Copy)
            for q in range(BQ):
                rows = slice(q * NS, (q + 1) * NS)
                AF(CT[rows, q, :], bank[2][rows, NS:NS + P], ACT.Copy)
            AF(Apow[:, 0, 1, :], bank[2][:, NS + P:NS + 2 * P], ACT.Copy).then_inc(pow_ready, 1)
            for h in range(2):
                act.wait_ge(prep_psum, 5 + h)
                AF(K0T[:, half(h)], bank[h][:, :], ACT.Identity, bias=cols[:, 4:5]).then_inc(prep_act, 1)
            for r in range(1, ROUNDS):
                act.wait_ge(pow_psum, r)
                AF(Apow[:, r, :, :], bank[3][:, 0:2 * P].rearrange("p (a n) -> p a n", a=2), ACT.Copy
                   ).then_inc(pow_ready, 1)
            act.wait_ge(v2_psum, 1)
            act.wait_ge(c_misc, C_MISC)
            for p2 in range(2):
                AF(Vb[p2 * S:(p2 + 1) * S, :, :, p2, 0:HD].rearrange("p b q e -> p q e b"),
                   bank[6][p2 * S:(p2 + 1) * S, :].rearrange("p (q e b) -> p q e b", q=4, e=HD), ACT.Copy
                   ).then_inc(vb_act, 1)

            def exponentials(n):
                act.wait_ge(a_sub, n + 1)
                AF(Es[:, n % 3, :], Es[:, n % 3, :], ACT.Exp, scale=ATTN_SCALE).then_inc(a_exp, 1)

            def copy_probs(n):
                act.wait_ge(a_tr, n + 1)
                if n >= 2:
                    act.wait_ge(a_pv, n - 1)
                AF(PTs[:, n % 2, :], bank[3 + n % 2][:, :], ACT.Copy).then_inc(a_trc, 1)

            def outputs_by_feature(h):
                act.wait_ge(o_psum[h], 1)
                if h == 1:
                    act.wait_ge(st_o[0], 16)
                AF(OT2[:, :, 0:S // 2].rearrange("p c (q g t) -> p q g c t", q=4, g=2)[:, :, 0, :, :],
                   bank[6][0:S, :].rearrange("p (q g c t) -> p q g c t", q=4, g=2, c=CH)[:, :, 0, :, :], ACT.Copy)
                AF(OT2[:, :, 0:S // 2].rearrange("p c (q g t) -> p q g c t", q=4, g=2)[:, :, 1, :, :],
                   bank[6][0:S, :].rearrange("p (q g c t) -> p q g c t", q=4, g=2, c=CH)[:, :, 1, :, :], ACT.Copy
                   ).then_inc(o_act[h], 1)

            def cross0_q(h):
                act.wait_ge(b_q[h], 1)
                AF(Q0T[:, half(h)], bank[6][:, :], ACT.Identity, bias=cols[:, 3:4]).then_inc(b_qc[h], 1)

            def cross0_exp(h):
                act.wait_ge(b_sub[h], 1)
                e = E0s[:, h * HALF:h * HALF + 2 * P]
                AF(e, e, ACT.Exp, scale=XATTN0_SCALE).then_inc(b_exp[h], 1)

            def cross0_copy(h):
                act.wait_ge(b_tr[h], 1)
                AF(E0s[:, h * HALF + 2 * P:(h + 1) * HALF], bank[6][:, 0:2 * P], ACT.Copy).then_inc(b_trc[h], 1)

            def gate_exp(h):
                act.wait_ge(g_sub[h], 1)
                AF(rt[:, 1, tiles(h), :], rt[:, 1, tiles(h), :], ACT.Exp).then_inc(g_exp[h], 1)

            def gate_copy(h):
                act.wait_ge(g_combt[h], 1)
                AF(combT[:, half(h)], bank[7][0:E0 + 1, :], ACT.Copy).then_inc(g_combc[h], 1)

            def silu(h, e):
                i = (E0 + 1) * h + e
                act.wait_ge(f_h1, i + 1)
                if i >= 1:
                    act.wait_ge(f_h, i)
                AF(sil0[:, :], bank[i % 2][:, :], ACT.Silu, bias=cols[:, 5 + e:6 + e]).then_inc(f_silu, 1)

            def values1(i, b):
                act.wait_ge(v1_psum, i + 1)
                AF(V1[:, i, :], bank[b][:, :], ACT.Copy).then_inc(v1_ready, 1)

            def gelu_states(h):
                act.wait_ge(s_y[h], 1)
                AF(GA[:, tiles(h), :], bank[6][:, :].rearrange("p (t d) -> p t d", d=D), ACT.Gelu
                   ).then_inc(s_gelu[h], 1)

            def queries1(h, i):
                act.wait_ge(c_q[h], i + 1)
                AF(Q1T[:, i, half(h)], bank[6 + i % 2][:, :], ACT.Copy).then_inc(c_qc[h], 1)

            def exponentials1(t):
                act.wait_ge(c_sub, t + 1)
                AF(Es[:, t % 3, :], Es[:, t % 3, :], ACT.Exp, scale=XATTN1_SCALE).then_inc(c_exp, 1)

            def copy_probs1(t):
                act.wait_ge(c_tr, t + 1)
                if t >= 2:
                    act.wait_ge(c_pv, t - 1)
                AF(PTs[:, t % 2, :], bank[2][:, :], ACT.Copy).then_inc(c_trc, 1)

            def copy_values1(t):
                act.wait_ge(c_pv, t + 1)
                if t >= 2:
                    act.wait_ge(c_wo, t - 1)
                for b2 in range(2):
                    AF(OTs[:, t % 2, :, b2 * S:(b2 + 1) * S],
                       bank[3 + b2][:, 0:NHP * S].rearrange("p (h n) -> p h n", n=S), ACT.Copy).then_inc(c_otc, 1)

            def gelu(e, f, h):
                i = 4 * e + 2 * f + h
                act.wait_ge(m_up, i + 1)
                if e >= 2:
                    act.wait_ge(m_down, 2 * (e - 2) + h + 1)
                AF(hid[:, e % 2, f, half(h)], bank[i % 4][:, :], ACT.Gelu).then_inc(m_gelu, 1)

            def copy_ys(e, h):
                act.wait_ge(m_down, 2 * e + h + 1)
                AF(ys[:, e, tiles(h), :], bank[4 + h][:, :].rearrange("p (t d) -> p t d", d=D), ACT.Copy
                   ).then_inc(m_ys, 1)

            for n in range(B + 2):
                if n < B:
                    exponentials(n)
                if n >= 1 and n - 1 < B:
                    copy_probs(n - 1)
                if n == HB + 5:
                    outputs_by_feature(0)
            copy_xt(1, 0, 7)
            outputs_by_feature(1)
            cross0_q(0)
            cross0_exp(0)
            values1(0, 3)
            values1(1, 4)
            cross0_copy(0)
            for i in range(2, 5):
                values1(i, 3 + i % 3)
            copy_xt(1, 1, 7)
            for i in range(5, 8):
                values1(i, 3 + i % 3)
            copy_xt(2, 0, 7)
            cross0_q(1)
            gate_exp(0)
            cross0_exp(1)
            cross0_copy(1)
            gate_copy(0)
            silu(0, 0)
            for e in range(1, E0 + 1):
                silu(0, e)
                if e == 3:
                    copy_xt(2, 1, 7)
                if e == 4:
                    gate_exp(1)
                if e == 6:
                    gate_copy(1)
            for e in range(E0 + 1):
                silu(1, e)
                if e == 3:
                    copy_xt(3, 0, 7)
            gelu_states(0)
            copy_xt(3, 1, 7)
            copy_xt(4, 0, 6)
            gelu_states(1)
            for i in range(4):
                queries1(0, i)
            for t in range(NT + 2):
                if t == HT:
                    copy_xt(4, 1, 6)
                    for i in range(4):
                        queries1(1, i)
                if t < NT:
                    exponentials1(t)
                if 1 <= t < NT + 1:
                    copy_probs1(t - 1)
                if t >= 2:
                    copy_values1(t - 2)
            for h in range(2):
                copy_xt(5, h, 6 + h)
            act.wait_ge(r_sub, 1)
            AF(rt[:, 1, :, :], rt[:, 1, :, :], ACT.Exp).then_inc(r_exp, 1)
            for f in range(F1):
                for h in range(2):
                    gelu(0, f, h)
            for e in range(E1):
                if e + 1 < E1:
                    for f in range(F1):
                        for h in range(2):
                            gelu(e + 1, f, h)
                for h in range(2):
                    copy_ys(e, h)

        @block.vector
        def _(dve):
            V = nc.vector
            steps = [0]

            def then(ins):
                steps[0] += 1
                ins.then_inc(v_step, 1)
                dve.wait_ge(v_step, steps[0])

            def moments(src, h):
                for t in range(h * HT, (h + 1) * HT):
                    last = V.bn_stats(stats[:, t, :], src[:, t, :])
                then(last)
                for t in range(h * HT, (h + 1) * HT):
                    last = V.bn_aggr(mv[:, t, :], stats[:, t, :])
                then(last)
                r, var, y2, p, bits = (rs[:, i, tiles(h)] for i in range(5))
                then(V.tensor_scalar(var, mv[:, tiles(h), 1], EPS, None, ALU.add))
                then(V.tensor_scalar(bits.bitcast(int32), var.bitcast(int32), 1, None, ALU.logical_shift_right))
                then(V.tensor_tensor(r.bitcast(int32), magic[:, :], bits.bitcast(int32), ALU.subtract))
                then(V.tensor_tensor(y2, r, r, ALU.mult))
                then(V.tensor_tensor(y2, y2, var, ALU.mult))
                then(V.tensor_scalar(p, y2, 0.375, -1.25, ALU.mult, ALU.add))
                then(V.tensor_tensor(p, p, y2, ALU.mult))
                then(V.scalar_tensor_tensor(r, p, 1.875, r, ALU.add, ALU.mult))
                then(V.tensor_tensor(y2, r, r, ALU.mult))
                then(V.tensor_tensor(y2, y2, var, ALU.mult))
                then(V.tensor_scalar(p, y2, -0.5, 1.5, ALU.mult, ALU.add))
                then(V.tensor_tensor(r, p, r, ALU.mult))

            def layernorm(n, h):
                if n >= 1:
                    dve.wait_ge(xt_ready[h], n)
                moments(X, h)
                for t in range(h * HT, (h + 1) * HT):
                    V.tensor_scalar(XN[:, t, :], X[:, t, :], mv[:, t, 0:1], rs[:, 0, t:t + 1], ALU.subtract, ALU.mult
                                    ).then_inc(xn_ready[h], 1)

            def softmax_small(logits, cut, sub_done, exp_done):
                then(V.tensor_reduce(rv[:, 0, cut], logits, AX.X, ALU.max))
                V.tensor_tensor(rt[:, 1, cut, :], logits, per_row(rv[:, 0, cut], E0), ALU.subtract).then_inc(sub_done, 1)
                dve.wait_ge(exp_done, 1)
                then(V.tensor_reduce(rv[:, 1, cut], rt[:, 1, cut, :], AX.X, ALU.add))
                then(V.reciprocal(rv[:, 2, cut], rv[:, 1, cut]))
                then(V.tensor_tensor(rt[:, 0, cut, :], rt[:, 1, cut, :], per_row(rv[:, 2, cut], E0), ALU.mult))

            def first_max(src, one_hot, cut):
                then(V.tensor_reduce(rv[:, 3, cut], src, AX.X, ALU.max))
                then(V.tensor_tensor(rt[:, 2, cut, :], src, per_row(rv[:, 3, cut], E0), ALU.is_equal))
                then(V.tensor_tensor(rt[:, 2, cut, :], rt[:, 2, cut, :], em8[:, cut, :], ALU.mult))
                then(V.tensor_reduce(rv[:, 4, cut], rt[:, 2, cut, :], AX.X, ALU.min))
                then(V.tensor_tensor(one_hot, em8[:, cut, :], per_row(rv[:, 4, cut], E0), ALU.is_equal))

            dve.wait_ge(c_magic, 1)
            for h in range(2):
                dve.wait_ge(ld_x[h], 16)
                layernorm(0, h)
            for i in range(4):
                h, s = i // 2, i % 2
                dve.wait_ge(qk_copied, i + 1)
                rest = OT[:, s * HALF:(s + 1) * HALF]
                if i >= 2:
                    dve.wait_ge(qk_low, i - 1)
                V.tensor_tensor(rest, QKVT[:, s, half(h)], QS[:, s, 0, half(h)], ALU.subtract).then_inc(qk_rest, 1)
                dve.wait_ge(qk_mid, i + 1)
                V.tensor_tensor(QS[:, s, 2, half(h)], rest, QS[:, s, 1, half(h)], ALU.subtract).then_inc(qk_low, 1)
            for h in range(2):
                dve.wait_ge(v_psum, h + 1)
                V.tensor_scalar(QKVT[:, 2, half(h)], bank[6 + h][:, :], cols[:, 2:3], None, ALU.add
                                ).then_inc(v_copied, 1)
            dve.wait_ge(ld_bv, 16)
            for h in range(2):
                dve.wait_ge(v0_psum, h + 1)
                V.tensor_tensor(V0[:, tiles(h), :], bank[6 + h][:, :].rearrange("p (t d) -> p t d", d=D),
                                per_col(bv0[:, :], HT), ALU.add).then_inc(v0_ready, 1)
            dve.wait_ge(ld_v2, 16)
            for g2 in range(2):
                for p2 in range(2):
                    src = V2[:, :, :].rearrange("p c (q r g t) -> p q r g c t", r=2, g=2, t=GT)[:, :, p2, g2, :, :]
                    V.tensor_copy(V2r[:, :, g2, p2, :, :], src).then_inc(v_order, 1)
            dve.wait_ge(v2_psum, 2)
            dve.wait_ge(c_misc, C_MISC)
            for p2 in range(2):
                V.tensor_copy(Vb[p2 * S:(p2 + 1) * S, :, :, p2, HD:2 * HD].rearrange("p b q e -> p q e b"),
                              bank[7][p2 * S:(p2 + 1) * S, :].rearrange("p (q e b) -> p q e b", q=4, e=HD)
                              ).then_inc(vb_dve, 1)

            def normalise(n):
                dve.wait_ge(a_pv, n + 1)
                o = bank[5][:, 0:4 * VN].rearrange("p (q v) -> p q v", q=4)[:, :, 0:2 * VW]
                o = o.rearrange("p q (r v) -> p q r v", r=2)
                then(V.reciprocal(rO[:, n, :].rearrange("p (q r) -> p q r", r=2), o[:, :, :, 2 * HD]))
                inv = rO[:, n, :].rearrange("p (q r) -> p q r", r=2)
                for g2 in range(2):
                    rows = slice(g2 * S, (g2 + 1) * S)
                    last = V.tensor_tensor(
                        Opos[rows, n // HB, :, :, n % HB].rearrange("p (q r) e -> p q r e", r=2),
                        o[rows, :, :, g2 * HD:(g2 + 1) * HD],
                        inv[rows, :, :].unsqueeze(3).broadcast_to([S, 4, 2, HD]), ALU.mult)
                last.then_inc(a_norm, 1)

            def subtract_max(n):
                dve.wait_ge(a_scores, n + 1)
                s = bank[n % 3][:, :].rearrange("p (a s) -> p a s", s=S)
                then(V.tensor_reduce(mx0[:, n, :], s, AX.X, ALU.max))
                if n >= 3:
                    dve.wait_ge(a_tr, n - 2)
                V.tensor_tensor(Es[:, n % 3, :].rearrange("p (a s) -> p a s", s=S), s, per_row(mx0[:, n, :], S),
                                ALU.subtract).then_inc(a_sub, 1)

            def outputs_by_feature(h):
                dve.wait_ge(o_psum[h], 2)
                if h == 1:
                    dve.wait_ge(st_o[0], 16)
                for g2 in range(2):
                    last = V.tensor_copy(
                        OT2[:, :, S // 2:S].rearrange("p c (q g t) -> p q g c t", q=4, g=2)[:, :, g2, :, :],
                        bank[7][0:S, :].rearrange("p (q g c t) -> p q g c t", q=4, g=2, c=CH)[:, :, g2, :, :])
                last.then_inc(o_dve[h], 1)

            def add_attention(h):
                dve.wait_ge(x_psum[h], 1)
                then(V.tensor_tensor(X[:, tiles(h), :], bank[6][:, :].rearrange("p (t d) -> p t d", d=D),
                                     X[:, tiles(h), :], ALU.add))

            def cross0_sub(h):
                dve.wait_ge(b_scores[h], 1)
                s = bank[6][:, 0:2 * P].rearrange("p (a s) -> p a s", s=S)
                e = E0s[:, h * HALF:h * HALF + 2 * P].rearrange("p (a s) -> p a s", s=S)
                then(V.tensor_reduce(sm[:, NT + h, 0, 0:4], s, AX.X, ALU.max))
                V.tensor_tensor(e, s, per_row(sm[:, NT + h, 0, 0:4], S), ALU.subtract).then_inc(b_sub[h], 1)

            def cross0_prob(h):
                dve.wait_ge(b_exp[h], 1)
                e = E0s[:, h * HALF:h * HALF + 2 * P].rearrange("p (a s) -> p a s", s=S)
                then(V.tensor_reduce(sm[:, NT + h, 1, 0:4], e, AX.X, ALU.add))
                then(V.reciprocal(sm[:, NT + h, 2, 0:4], sm[:, NT + h, 1, 0:4]))
                V.tensor_tensor(e, e, per_row(sm[:, NT + h, 2, 0:4], S), ALU.mult).then_inc(b_prob[h], 1)

            def cross0_add(h):
                dve.wait_ge(b_pv[h], 1)
                V.tensor_tensor(X[:, tiles(h), :], bank[6][:, :].rearrange("p (t d) -> p t d", d=D),
                                X[:, tiles(h), :], ALU.add).then_inc(b_added[h], 1)
                dve.wait_ge(b_added[h], 1)

            def gate(h):
                cut = tiles(h)
                dve.wait_ge(g_psum[h], 1)
                softmax_small(bank[7][:, 0:HT * E0].rearrange("p (t e) -> p t e", e=E0), cut, g_sub[h], g_exp[h])
                first_max(rt[:, 0, cut, :], rt[:, 3, cut, :], cut)
                then(V.scalar_tensor_tensor(rt[:, 4, cut, :], rt[:, 3, cut, :], -2.0, rt[:, 0, cut, :], ALU.mult, ALU.add))
                first_max(rt[:, 4, cut, :], rt[:, 5, cut, :], cut)
                then(V.tensor_tensor(rt[:, 3, cut, :], rt[:, 3, cut, :], rt[:, 5, cut, :], ALU.add))
                V.tensor_tensor(comb[:, cut, 0:E0], rt[:, 3, cut, :], rt[:, 0, cut, :], ALU.mult).then_inc(g_comb[h], 1)
                dve.wait_ge(g_comb[h], 1)

            def gate0(h, e):
                i = (E0 + 1) * h + e
                dve.wait_ge(f_silu, i + 1)
                dve.wait_ge(f_h3, i + 1)
                if i >= 2:
                    dve.wait_ge(f_out, i - 1)
                V.scalar_tensor_tensor(hid0[:, i % 2, :], bank[2 + i % 2][:, :], cols[:, 14 + e:15 + e],
                                       sil0[:, :], ALU.add, ALU.mult).then_inc(f_h, 1)

            def add0(h, e):
                i = (E0 + 1) * h + e
                dve.wait_ge(f_out, i + 1)
                if i >= 1:
                    dve.wait_ge(f_acc, i)
                for t in range(HT):
                    tt = HT * h + t
                    last = V.scalar_tensor_tensor(X[:, tt, :], bank[4 + i % 2][:, t * P:(t + 1) * P],
                                                  comb[:, tt, e:e + 1], X[:, tt, :], ALU.mult, ALU.add)
                last.then_inc(f_acc, 1)
                if e == E0:
                    dve.wait_ge(f_acc, i + 1)

            def mask_rows():
                dve.wait_ge(ld_mask, 16)
                V.tensor_copy(maskf[:, :], masku[:, :]).then_inc(mask_ready, 1)
                dve.wait_ge(mask_ready, 1)
                V.tensor_scalar(maskrow[:, :], maskf[0:1, :], 1.0, 2.0 ** 127, ALU.subtract, ALU.mult
                                ).then_inc(mask_ready, 1)

            def keys1(i, b):
                dve.wait_ge(k1_psum, i + 1)
                V.tensor_tensor(K1T[:, i // 2, half(i % 2)], bank[b][:, :], maskf[:, half(i % 2)], ALU.mult
                                ).then_inc(k1_ready, 1)

            def state(h, r):
                dve.wait_ge(s_psum[h], r + 1)
                V.tensor_copy(ST[:, h, :, :], bank[7][:, 0:2 * S].rearrange("p (b s) -> p b s", s=S)
                              ).then_inc(s_state[h], 1)

            def add_states(h):
                cut = tiles(h)
                wide = HT
                dve.wait_ge(s_gelu[h], 1)
                moments(GA, h)
                for t in range(h * HT, (h + 1) * HT):
                    last = V.tensor_scalar(GB[:, t, :], GA[:, t, :], mv[:, t, 0:1], rs[:, 0, t:t + 1], ALU.subtract,
                                           ALU.mult)
                then(last)
                dve.wait_ge(ld_rows, 64)
                ga, gb, mask = GA[:, cut, :], GB[:, cut, :], nanm[:, cut, :]
                then(V.tensor_tensor(gb, gb, per_col(gamma[:, :], wide), ALU.mult))
                then(V.tensor_tensor(gb, gb, per_col(beta[:, :], wide), ALU.add))
                then(V.tensor_tensor(mask, gb, gb, ALU.is_equal))
                then(V.tensor_scalar(ga, gb, CLAMP, -CLAMP, ALU.min, ALU.max))
                then(V.tensor_tensor(ga, ga, mask, ALU.mult))
                then(V.tensor_scalar(mask, gb, 0.0, 0.0, ALU.mult, ALU.is_equal))
                then(V.copy_predicated(ga, mask, gb))
                then(V.tensor_tensor(X[:, cut, :], ga, X[:, cut, :], ALU.add))

            def add_bo(h):
                dve.wait_ge(xn_ready[h], 5 * HT)
                then(V.tensor_tensor(X[:, tiles(h), :], X[:, tiles(h), :], per_col(bo[:, :], HT), ALU.add))

            def subtract_max1(t):
                dve.wait_ge(c_scores, t + 1)
                s = bank[t % 2][:, :].rearrange("p (a s) -> p a s", s=S)
                then(V.tensor_reduce(sm[:, t, 0, :], s, AX.X, ALU.max))
                if t >= 3:
                    dve.wait_ge(c_tr, t - 2)
                V.tensor_tensor(Es[:, t % 3, :].rearrange("p (a s) -> p a s", s=S), s,
                                per_row(sm[:, t, 0, :], S), ALU.subtract).then_inc(c_sub, 1)

            def probs1(t):
                dve.wait_ge(c_exp, t + 1)
                e = Es[:, t % 3, :].rearrange("p (a s) -> p a s", s=S)
                then(V.tensor_reduce(sm[:, t, 1, :], e, AX.X, ALU.add))
                then(V.reciprocal(sm[:, t, 2, :], sm[:, t, 1, :]))
                V.tensor_tensor(e, e, per_row(sm[:, t, 2, :], S), ALU.mult).then_inc(c_prob, 1)

            def add1(t):
                dve.wait_ge(c_wo, t + 1)
                V.tensor_tensor(X[:, t, :], bank[5][:, 0:D], X[:, t, :], ALU.add).then_inc(c_added, 1)
                if t % HT == HT - 1:
                    dve.wait_ge(c_added, t + 1)

            def candidates(shift):
                then(V.tensor_scalar(cand[:, :, :], jconst[:, :, :], shift, None, ALU.logical_shift_left))
                then(V.tensor_tensor(cand[:, :, :], cand[:, :, :], per_col(thr[:, :], NC), ALU.bitwise_or))

            def route():
                dve.wait_ge(r_psum, 2)
                softmax_small(bank[7][:, 0:NT * E1].rearrange("p (t e) -> p t e", e=E1), slice(0, NT), r_sub, r_exp)
                prob = rt[:, 0, :, :]
                prob_et = rt[:, 0, :, :].rearrange("p t e -> p e t")
                then(V.memset(thr[:, :], 0))
                for i in range(SEARCH):
                    shift = BITS - STEP * (i + 1)
                    candidates(shift)
                    V.tensor_tensor(hit[:, :, :].rearrange("p (j e) t -> p j e t", e=E1),
                                    prob_et.unsqueeze(1).broadcast_to([P, NC, E1, NT]),
                                    cand[:, :, :].bitcast(fp32).unsqueeze(3).broadcast_to([P, NC, E1, NT]), ALU.is_ge
                                    ).then_inc(r_hit, 1)
                    dve.wait_ge(r_cnt, i + 1)
                    then(V.tensor_reduce(cnt[:, :, :].rearrange("p j e -> p (j e)"),
                                         bank[6][:, 0:NC * E1 * NT].rearrange("p (a t) -> p a t", t=NT), AX.X, ALU.add))
                    then(V.tensor_scalar(acc[:, :, :], cnt[:, :, :], CAP - 0.5, float(2 ** shift), ALU.is_ge, ALU.mult))
                    with nc.allow_low_precision(reason="up to NC times one power of two: exact"):
                        then(V.tensor_reduce(add[:, :], acc[:, :, :].rearrange("p j e -> p e j"), AX.X, ALU.add))
                    then(V.tensor_tensor(thr[:, :], thr[:, :], add[:, :], ALU.bitwise_or))
                level = per_col(thr[:, :].bitcast(fp32), NT)
                above, tie, ahead = rt[:, 6, :, :], rt[:, 7, :, :], rt[:, 8, :, :]
                then(V.memset(hit[:, :, :], 0.0))
                then(V.tensor_tensor(above, prob, level, ALU.is_gt))
                V.tensor_copy(hit[:, 0:E1, :], above.rearrange("p t e -> p e t")).then_inc(r_hit, 1)
                V.tensor_tensor(tie, prob, level, ALU.is_equal)
                V.tensor_tensor(eqb[:, :, :], prob, level, ALU.is_equal).then_inc(r_eq, 1)
                dve.wait_ge(r_cnt, SEARCH + 1)
                then(V.tensor_reduce(cnt[:, 0, :], bank[6][:, 0:E1 * NT].rearrange("p (a t) -> p a t", t=NT), AX.X, ALU.add))
                then(V.tensor_scalar(acc[:, 0, :], cnt[:, 0, :], -1.0, float(CAP), ALU.mult, ALU.add))
                dve.wait_ge(r_pre, 1)
                then(V.tensor_tensor(ahead, bank[7][:, 0:NT * E1].rearrange("p (t e) -> p t e", e=E1),
                                     per_col(acc[:, 0, :], NT), ALU.is_lt))
                then(V.tensor_tensor(ahead, ahead, tie, ALU.mult))
                then(V.tensor_tensor(above, above, ahead, ALU.add))
                then(V.tensor_reduce(rv[:, 5, :], above, AX.X, ALU.max))
                then(V.tensor_tensor(tie, above, per_row(rv[:, 5, :], E1), ALU.subtract))
                then(V.scalar_tensor_tensor(tie, tie, 4.0, prob, ALU.mult, ALU.add))
                first_max(tie, ahead, slice(0, NT))
                then(V.tensor_tensor(rt[:, 9, :, :], ahead, prob, ALU.mult))

            def add_expert(e):
                for t in range(NT):
                    if t % HT == 0:
                        dve.wait_ge(m_ys, 2 * e + t // HT + 1)
                    last = V.scalar_tensor_tensor(X[:, t, :], ys[:, e, t, :], rt[:, 9, t, e:e + 1], X[:, t, :],
                                                  ALU.mult, ALU.add)
                    if e == E1 - 1:
                        last.then_inc(m_done, 1)
                if e < E1 - 1:
                    then(last)

            for n in range(B + 4):
                if n >= 4:
                    normalise(n - 4)
                if n < B:
                    subtract_max(n)
                if n == HB + 5:
                    outputs_by_feature(0)
                if n == B:
                    add_attention(0)
                    layernorm(1, 0)
            mask_rows()
            outputs_by_feature(1)
            cross0_sub(0)
            cross0_prob(0)
            keys1(0, 0)
            keys1(1, 1)
            cross0_add(0)
            layernorm(2, 0)
            add_attention(1)
            layernorm(1, 1)
            for i in range(2, 8):
                keys1(i, i % 3)
            gate(0)
            cross0_sub(1)
            cross0_prob(1)
            gate0(0, 0)
            cross0_add(1)
            for e in range(E0 + 1):
                if e < E0:
                    gate0(0, e + 1)
                else:
                    gate0(1, 0)
                add0(0, e)
                if e == 0:
                    layernorm(2, 1)
                if e == 3:
                    gate(1)
            for e in range(E0 + 1):
                if e < E0:
                    gate0(1, e + 1)
                add0(1, e)
                if e == 0:
                    layernorm(3, 0)
                if e == 3:
                    state(0, 0)
                if 4 <= e < 7:
                    state(0, 2 * (e - 4) + 1)
                    state(0, 2 * (e - 4) + 2)
            layernorm(3, 1)
            add_states(0)
            state(1, 0)
            for r in range(ROUNDS):
                state(1, r + 1)
            layernorm(4, 0)
            add_bo(0)
            add_states(1)
            layernorm(4, 1)
            add_bo(1)
            for t in range(NT + 4):
                if t < NT:
                    subtract_max1(t)
                if t >= 1 and t - 1 < NT:
                    probs1(t - 1)
                if t >= 4:
                    add1(t - 4)
            layernorm(5, 0)
            layernorm(5, 1)
            route()
            for e in range(E1):
                add_expert(e)


_NAMES = ["x", "ctx_768", "mask_BxS2_bk0", "L0_attn_qkv_kernel", "L0_attn_qkv_bias", "L0_xattn_Wq", "L0_xattn_bq",
          "L0_xattn_Wk", "L0_xattn_bk", "L0_xattn_Wv", "L0_xattn_bv", "L0_ffn_gate_w", "L0_ffn_w1", "L0_ffn_b1",
          "L0_ffn_w2", "L0_ffn_b2", "L0_ffn_w3", "L0_ffn_b3", "L0_ffn_sw1", "L0_ffn_sb1", "L0_ffn_sw2", "L0_ffn_sb2",
          "L0_ffn_sw3", "L0_ffn_sb3", "L1_attn_A", "L1_attn_B", "L1_attn_C", "L1_attn_gamma", "L1_attn_beta",
          "L1_xattn_W_q", "L1_xattn_W_k", "L1_xattn_W_v", "L1_xattn_W_o", "L1_xattn_b_o", "L1_ffn_Wg", "L1_ffn_W1",
          "L1_ffn_W2"]


def kernel(**inputs):
    import numpy as np
    import concourse.bacc as bacc
    from concourse import mybir as _mybir
    from concourse.bass_utils import run_bass_kernel_spmd

    nc = bacc.Bacc("TRN2", target_bir_lowering=False, num_devices=1)
    arrays, w = {}, {}
    for name in _NAMES:
        a = np.ascontiguousarray(inputs[name])
        arrays[f"in_{name}"] = a
        w[name] = nc.dram_tensor(f"in_{name}", a.shape, _mybir.dt.from_np(a.dtype), kind="ExternalInput").ap()
    out = nc.dram_tensor("out", arrays["in_x"].shape, _mybir.dt.float32, kind="ExternalOutput").ap()
    decoder_kernel(nc, w, out)
    r = run_bass_kernel_spmd(nc, [arrays], core_ids=[0])
    return r.results[0]["out"]
```

```python
import concourse.bass as bass
from concourse import mybir
from contextlib import ExitStack


def decoder_kernel(nc: bass.Bass, w, out):
    fp32 = mybir.dt.float32
    bf16 = mybir.dt.bfloat16
    int32 = mybir.dt.int32
    uint8 = mybir.dt.uint8
    ALU = mybir.AluOpType
    ACT = mybir.ActivationFunctionType
    AX = mybir.AxisListType

    B, S, D = w["x"].shape
    DC = w["ctx_768"].shape[2]
    P = 128
    NT = B * S // P
    N = B * S
    HALF = N // 2
    EPS = 1e-5

    CH, HD = 16, 8
    GT = S // CH
    NPAIR = S // (2 * GT)
    VW = 2 * HD + 1
    VN = 6 * VW
    TERMS = 9
    ATTN_SCALE = 1.0 / (2.0 * D) ** 0.5
    XATTN0_SCALE = 1.0 / float(D) ** 0.5
    H1, DH1 = 8, 64
    XATTN1_SCALE = DH1 ** -0.5
    NHP = H1 // 2
    E0 = 8
    E1 = 8
    F1 = w["L1_ffn_W1"].shape[2] // P
    CAP = N // E1
    NS = 32
    BQ = P // NS
    ROUNDS = 6
    CLAMP = 1.0e6
    BITS, STEP = 30, 2
    NC = 2 ** STEP - 1
    HT = NT // 2
    HB = B // 2

    ctx = ExitStack()
    with ctx:
        def sb(name, shape, dt=fp32):
            return ctx.enter_context(nc.sbuf_tensor(name, shape, dt))

        def sem(name):
            return ctx.enter_context(nc.semaphore(name))

        def per_row(ap, n):
            return ap.unsqueeze(2).broadcast_to([ap.shape[0], ap.shape[1], n])

        def per_col(ap, n):
            return ap.unsqueeze(1).broadcast_to([ap.shape[0], n, ap.shape[1]])

        bank = [ctx.enter_context(nc.psum_tensor(f"bank{i}", [P, 512], fp32)) for i in range(8)]


        X = sb("X", [P, NT, D])
        XN = sb("XN", [P, NT, D])
        XT = sb("XT", [P, N])
        stats = sb("stats", [P, NT, 6])
        mv = sb("mv", [P, NT, 2])
        rs = sb("rs", [P, 5, NT])
        CTX = sb("CTX", [P, NT, DC])
        CTXT = sb("CTXT", [DC, N])
        ident = sb("ident", [P, P])
        perm = sb("perm", [P, P], bf16)
        causal = sb("causal", [P, NPAIR, S], bf16)
        onesb = sb("onesb", [P, P], bf16)
        trib = sb("trib", [P, P], bf16)
        em8 = sb("em8", [P, NT, E0])
        jconst = sb("jconst", [P, NC, E1], int32)
        magic = sb("magic", [P, HT], int32)
        vecs = sb("vecs", [31, P])
        cols = sb("cols", [P, 31])
        Wp = sb("Wp", [P, 3, D])
        Wq0 = sb("Wq0", [P, D])
        Wk0 = sb("Wk0", [DC, D])
        Wv0 = sb("Wv0", [DC, D])
        bv0 = sb("bv0", [P, D])
        W1a = sb("W1a", [P, E0 + 1, D])
        W3a = sb("W3a", [P, E0 + 1, D])
        W2a = sb("W2a", [P, E0 + 1, D])
        b2a = sb("b2a", [E0 + 1, D])
        Bn = sb("Bn", [NS, D])
        Cn = sb("Cn", [P, BQ, NS])
        BT = sb("BT", [P, NS])
        CT = sb("CT", [P, BQ, D])
        Apow = sb("Apow", [P, ROUNDS, 2, P])
        gamma = sb("gamma", [P, D])
        beta = sb("beta", [P, D])
        bo = sb("bo", [P, D])
        Wq1 = sb("Wq1", [P, H1 * DH1])
        Wk1 = sb("Wk1", [DC, H1 * DH1])
        Wv1 = sb("Wv1", [DC, H1 * DH1])
        Wo1 = sb("Wo1", [P, NHP, D])
        Wqkv = Wo1[:, 0:3, :].rearrange("p a d -> p (a d)")
        Wg = sb("Wg", [P, E1])
        Wb = sb("Wb", [P, 2 * E1 * F1 * P])
        W1b = Wb[:, 0:E1 * F1 * P].rearrange("p (e f) -> p e f", e=E1)
        W2b = Wb[:, E1 * F1 * P:].rearrange("p (e k d) -> p e k d", e=E1, d=D)
        QS = Wb[:, 0:3 * N].bitcast(bf16).rearrange("p (s a n) -> p s a n", s=2, a=3)
        masku = sb("masku", [P, N], uint8)
        maskf = sb("maskf", [P, N])
        maskrow = sb("maskrow", [1, N], bf16)
        CTXTM = maskf[0:DC, :]
        QKVT = sb("QKVT", [P, 3, N])
        big = sb("big", [P, 16 * N])
        Q9 = big[0:TERMS * HD, 0:8 * N].bitcast(bf16).rearrange("p (h n) -> p h n", h=2)
        K9 = big[0:TERMS * HD, 8 * N:].bitcast(bf16).rearrange("p (h n) -> p h n", h=2)
        K1T = big[:, 0:4 * N].rearrange("p (a n) -> p a n", n=N)
        V1 = big[:, 4 * N:8 * N].rearrange("p (t n) -> p t n", t=NT)
        ys = big[:, 8 * N:].rearrange("p (e t d) -> p e t d", e=E1, d=D)
        V2 = sb("V2", [P, CH, S])
        VB = B * NPAIR * VW
        VP = VB + VN - 2 * VW
        att = sb("att", [P, VP + 2 * N])
        Vb = att[:, 0:VB].rearrange("p (b q r v) -> p b q r v", b=B, r=2, v=VW)
        Opos = att[:, VP:VP + N].rearrange("p (h a e b) -> p h a e b", h=2, a=NPAIR, e=HD)
        V2r = att[:, VP + N:VP + 2 * N].rearrange("p (q g r c t) -> p q g r c t", g=2, r=2, t=GT, c=CH)
        OT2 = att[0:S, VP + N:VP + 2 * N].rearrange("p (c s) -> p c s", s=S)
        OT = sb("OT", [P, N])
        mx0 = sb("mx0", [P, B, NPAIR])
        Es = sb("Es", [P, 3, 512])
        PTs = sb("PTs", [P, 2, 512])
        rO = sb("rO", [P, B, NPAIR])
        K0T = sb("K0T", [P, N])
        V0 = sb("V0", [P, NT, D])
        Q0T = QKVT[:, 0, :]
        E0s = QKVT[:, 1, :]
        hid = att[:, 0:4 * N].rearrange("p (a b n) -> p a b n", a=2, b=2)
        Q1T = att[:, 0:4 * N].rearrange("p (a n) -> p a n", a=4)
        sm = sb("sm", [P, NT + 2, 3, 8])
        OTs = V2[:, :, :].rearrange("p c s -> p (c s)").rearrange("p (a h n) -> p a h n", a=2, n=P)
        rt = sb("rt", [P, 10, NT, E0])
        rv = sb("rv", [P, 6, NT])
        comb = sb("comb", [P, NT, E0 + 1])
        combT = OT[0:E0 + 1, :]
        hid0 = att[:, 0:N].rearrange("p (a n) -> p a n", a=2)
        sil0 = att[:, N:N + HALF]
        part0 = att[:, 3 * N:4 * N].rearrange("p (a t d) -> p a t d", a=2, d=D)
        thr = sb("thr", [P, E1], int32)
        jshift = PTs[:, 0, 0:BITS // STEP * NC * E1].bitcast(int32).rearrange(
            "p (r a) -> p r a", a=NC * E1)
        base = sb("base", [P, NC, E1], int32)
        cand = sb("cand", [P, NC, E1], int32)
        hit = sb("hit", [P, NC * E1, NT], bf16)
        cnt = sb("cnt", [P, NC, E1])
        acc = sb("acc", [P, NC, E1])
        add = sb("add", [P, E1], int32)
        eqb = sb("eqb", [P, NT, E1], bf16)
        ST = sb("ST", [P, 2, 2, S])
        GA = QKVT[:, 2, :].rearrange("p (t d) -> p t d", d=D)
        GB = XN[:, :, :]
        nanm = QKVT[:, 1, :].bitcast(int32).rearrange("p (t d) -> p t d", d=D)

        qk_d = nc.dram_tensor("qk_scratch", [2, 2, 3, HD, CH, HALF], bf16).ap()
        v_d = nc.dram_tensor("v_scratch", [P, N], fp32).ap()
        o_d = nc.dram_tensor("o_scratch", [2, P, HALF], fp32).ap()

        def pair_of(name):
            return [sem(f"{name}_a"), sem(f"{name}_b")]

        ld_x = pair_of("ld_x")
        ld_ctx = sem("ld_ctx")
        ld_vecs = sem("ld_vecs")
        ld_qkv = sem("ld_qkv")
        ld_x0 = sem("ld_x0")
        ld_bv = sem("ld_bv")
        ld_mask = sem("ld_mask")
        ld_ssm = sem("ld_ssm")
        ld_x1 = sem("ld_x1")
        ld_f0 = sem("ld_f0")
        ld_f1 = sem("ld_f1")
        ld_rows = sem("ld_rows")
        c_zero = sem("c_zero")
        c_ident = sem("c_ident")
        c_magic = sem("c_magic")
        c_azero = sem("c_azero")
        c_fill = sem("c_fill")
        c_wp = sem("c_wp")
        c_misc = sem("c_misc")
        v_step = sem("v_step")
        xn_ready = pair_of("xn_ready")
        xt_psum = pair_of("xt_psum")
        xt_ready = pair_of("xt_ready")
        prep_psum = sem("prep_psum")
        prep_act = sem("prep_act")
        v0_psum = sem("v0_psum")
        v0_ready = sem("v0_ready")
        mask_ready = sem("mask_ready")
        kv_psum = sem("kv_psum")
        kv_ready = sem("kv_ready")
        pow_psum = sem("pow_psum")
        pow_ready = sem("pow_ready")
        qk_psum = sem("qk_psum")
        qk_copied = sem("qk_copied")
        qk_rest = sem("qk_rest")
        qk_mid = sem("qk_mid")
        qk_low = sem("qk_low")
        v_psum = sem("v_psum")
        v_copied = sem("v_copied")
        st_qk = [pair_of("st_q"), pair_of("st_k")]
        ld_qk = pair_of("ld_qk")
        st_v = sem("st_v")
        ld_v2 = sem("ld_v2")
        v_order = sem("v_order")
        v2_psum = sem("v2_psum")
        vb_act = sem("vb_act")
        vb_dve = sem("vb_dve")
        a_scores = sem("a_scores")
        a_sub = sem("a_sub")
        a_exp = sem("a_exp")
        a_tr = sem("a_tr")
        a_trc = sem("a_trc")
        a_pv = sem("a_pv")
        a_norm = sem("a_norm")
        o_psum = pair_of("o_psum")
        o_act = pair_of("o_act")
        o_dve = pair_of("o_dve")
        st_o = pair_of("st_o")
        ld_o = pair_of("ld_o")
        x_psum = pair_of("x_psum")
        b_q = pair_of("b_q")
        b_qc = pair_of("b_qc")
        b_scores = pair_of("b_scores")
        b_sub = pair_of("b_sub")
        b_exp = pair_of("b_exp")
        b_prob = pair_of("b_prob")
        b_tr = pair_of("b_tr")
        b_trc = pair_of("b_trc")
        b_pv = pair_of("b_pv")
        b_added = pair_of("b_added")
        g_psum = pair_of("g_psum")
        g_sub = pair_of("g_sub")
        g_exp = pair_of("g_exp")
        g_comb = pair_of("g_comb")
        g_combt = pair_of("g_combt")
        g_combc = pair_of("g_combc")
        f_h1 = sem("f_h1")
        f_h3 = sem("f_h3")
        f_silu = sem("f_silu")
        f_h = sem("f_h")
        f_out = sem("f_out")
        f_part = sem("f_part")
        f_acc = sem("f_acc")
        s_psum = pair_of("s_psum")
        s_state = pair_of("s_state")
        s_y = pair_of("s_y")
        s_gelu = pair_of("s_gelu")
        c_q = pair_of("c_q")
        c_qc = pair_of("c_qc")
        c_scores = sem("c_scores")
        c_sub = sem("c_sub")
        c_exp = sem("c_exp")
        bo_added = sem("bo_added")
        c_sum = sem("c_sum")
        c_prob = sem("c_prob")
        c_tr = sem("c_tr")
        c_trc = sem("c_trc")
        c_pv = sem("c_pv")
        c_otc = sem("c_otc")
        c_wo = sem("c_wo")
        c_added = sem("c_added")
        r_psum = sem("r_psum")
        r_sub = sem("r_sub")
        r_exp = sem("r_exp")
        r_hit = sem("r_hit")
        r_cnt = sem("r_cnt")
        r_eq = sem("r_eq")
        r_pre = sem("r_pre")
        m_up = sem("m_up")
        m_gelu = sem("m_gelu")
        m_down = sem("m_down")
        m_ys = sem("m_ys")
        m_done = sem("m_done")
        st_out = sem("st_out")

        block = ctx.enter_context(nc.Block())

        def half(h):
            return slice(h * HALF, (h + 1) * HALF)

        def tiles(h):
            return slice(h * HT, (h + 1) * HT)

        def kv_bank(j):
            return j % 4 if j < 13 else 6 + j % 2

        SEARCH = BITS // STEP

        @block.sync
        def _(sp):
            def tokens(ap):
                return ap.rearrange("b s d -> (b s) d").rearrange("(t p) d -> p t d", p=P)

            for h in range(2):
                sp.dma_start(X[:, tiles(h), :], tokens(w["x"])[:, tiles(h), :]).then_inc(ld_x[h], 16)
            sp.dma_start(Wqkv[:, :], w["L0_attn_qkv_kernel"]).then_inc(ld_qkv, 16)
            sp.dma_start(vecs[0:3, :].rearrange("s (c e) -> s c e", e=HD),
                         w["L0_attn_qkv_bias"].rearrange("o (c s e) -> (o s) c e", s=3, e=HD)).then_inc(ld_vecs, 16)
            for row, name in ((3, "L0_xattn_bq"), (4, "L0_xattn_bk"), (13, "L0_ffn_sb1"), (22, "L0_ffn_sb3")):
                sp.dma_start(vecs[row:row + 1, :], w[name].unsqueeze(0)).then_inc(ld_vecs, 16)
            for row, name in ((5, "L0_ffn_b1"), (14, "L0_ffn_b3"), (23, "L0_ffn_gate_w")):
                sp.dma_start(vecs[row:row + 8, :], w[name]).then_inc(ld_vecs, 16)
            sp.dma_start(CTX[:, :, :], tokens(w["ctx_768"])).then_inc(ld_ctx, 16)
            sp.dma_start(Wk0[:, :], w["L0_xattn_Wk"]).then_inc(ld_x0, 16)
            sp.dma_start(Wv0[:, :], w["L0_xattn_Wv"]).then_inc(ld_x0, 16)
            sp.dma_start(Wq0[:, :], w["L0_xattn_Wq"]).then_inc(ld_x0, 16)

            for h in range(2):
                for s in range(2):
                    sp.wait_ge(qk_low, 2 * h + s + 1)
                    for a in range(3):
                        sp.dma_start(qk_d[s, h, a, :, :, :].rearrange("e c n -> c e n"),
                                     QS[:, s, a, half(h)]).then_inc(st_qk[s][h], 16)
                if h == 0:
                    sp.wait_ge(v_copied, 2)
                    sp.dma_start(v_d, QKVT[:, 2, :]).then_inc(st_v, 16)
                for s in range(2):
                    sp.wait_ge(st_qk[s][h], 48)
                    parts = qk_d[s, h, :, :, :, :].rearrange("a e c n -> a e (c n)")
                    for j in range(3):
                        for first, last, at in (((0, 3, 0),) if s == 0 or j == 0 else ((j, 3, 0), (0, j, 3 - j))):
                            rows = slice((3 * j + at) * HD, (3 * j + at + last - first) * HD)
                            dst = (Q9, K9)[s][rows, h, :]
                            sp.dma_start(dst, parts[first:last, :, :].rearrange("a e n -> (a e) n")
                                         ).then_inc(ld_qk[h], 16)
                    if h == 0 and s == 0:
                        sp.wait_ge(st_v, 16)
                        sp.dma_start(V2[:, :, :], v_d.rearrange("(c e) (b s) -> e b c s", e=HD, s=S)
                                     .rearrange("e b c s -> (e b) c s")).then_inc(ld_v2, 16)

            for h in range(2):
                sp.wait_ge(o_act[h], 1)
                sp.wait_ge(o_dve[h], 1)
                sp.dma_start(o_d[h, :, :].rearrange("(c e) (b s) -> e b c s", e=HD, s=S)
                             .rearrange("e b c s -> (e b) c s"), OT2).then_inc(st_o[h], 16)
                sp.wait_ge(st_o[h], 16)
                sp.dma_start(OT[:, half(h)], o_d[h, :, :]).then_inc(ld_o[h], 16)
                if h == 0:
                    for s in range(2):
                        for part_h in range(2):
                            sp.wait_ge(st_qk[s][part_h], 48)
                    sp.dma_start(W1b, w["L1_ffn_W1"].rearrange("e d f -> d e f")).then_inc(ld_f1, 16)
                    for e in range(E1):
                        sp.dma_start(W2b[:, e, :, :], w["L1_ffn_W2"][e, :, :].rearrange("(k p) d -> p k d", p=P)
                                     ).then_inc(ld_f1, 16)

            for t in range(NT):
                sp.wait_ge(m_done, t + 1)
                sp.dma_start(out.rearrange("b s d -> (b s) d")[t * P:(t + 1) * P, :], X[:, t, :]
                             ).then_inc(st_out, 16)
            sp.wait_ge(st_out, 16 * NT)

        @block.gpsimd
        def _(pool):
            nc.gpsimd.memset(ident[:, :], 0.0).then_inc(c_zero, 1)
            nc.gpsimd.memset(magic[:, :], 0x5f3759df).then_inc(c_magic, 1)
            pool.wait_ge(c_zero, 1)
            nc.gpsimd.affine_select(out=ident[:, :], in_=ident[:, :], compare_op=ALU.not_equal, fill=1.0, base=0,
                                    pattern=[[-1, P]], channel_multiplier=1).then_inc(c_ident, 1)
            nc.gpsimd.memset(Apow[:, 0, 0, :], 0.0).then_inc(c_azero, 1)
            pool.wait_ge(ld_qkv, 16)
            nc.gpsimd.tensor_copy(Wp[:, :, :].rearrange("d s (c e) -> d c s e", e=HD),
                                  Wqkv[:, :].rearrange("d (c s e) -> d c s e", s=3, e=HD)).then_inc(c_wp, 1)
            pool.wait_ge(c_azero, 1)
            for q in range(BQ):
                pool.dma_start(Apow[q * NS:(q + 1) * NS, 0, 0, q * NS:(q + 1) * NS], w["L1_attn_A"]
                               ).then_inc(ld_ssm, 16)
                pool.dma_start(Cn[:, q, :], w["L1_attn_C"]).then_inc(ld_ssm, 16)
            pool.dma_start(Bn[:, :], w["L1_attn_B"]).then_inc(ld_ssm, 16)
            pool.dma_start(bv0[:, :], w["L0_xattn_bv"].partition_broadcast(P)).then_inc(ld_bv, 16)
            nc.gpsimd.memset(causal[:, :, :], 0.0).then_inc(c_fill, 1)
            nc.gpsimd.memset(trib[:, :], 1.0).then_inc(c_fill, 1)
            nc.gpsimd.memset(att[:, 0:VP], 0.0).then_inc(c_fill, 1)
            nc.gpsimd.memset(CT[:, :, :], 0.0).then_inc(c_fill, 1)
            nc.gpsimd.iota(jconst[:, :, :], pattern=[[1, NC], [0, E1]], base=1, channel_multiplier=0).then_inc(c_misc, 1)
            nc.gpsimd.memset(onesb[:, :], 1.0).then_inc(c_misc, 1)
            pool.wait_ge(c_ident, 1)
            nc.gpsimd.tensor_copy(perm[:, :].rearrange("k (g c t) -> k g c t", g=2, c=CH),
                                  ident[:, :].rearrange("k (g t c) -> k g c t", g=2, c=CH)).then_inc(c_misc, 1)
            for e in range(E0):
                nc.gpsimd.memset(em8[:, :, e], float(e - E0)).then_inc(c_misc, 1)
            nc.gpsimd.memset(comb[:, :, E0], 1.0).then_inc(c_misc, 1)
            pool.wait_ge(c_fill, 4)
            pool.wait_ge(c_wp, 1)
            for g2 in range(2):
                pool.wait_ge(c_misc, 4 + E0 + g2)
                part = causal[g2 * S:(g2 + 1) * S, :, :]
                nc.gpsimd.affine_select(out=part, in_=part, compare_op=ALU.is_ge, fill=-1.0e38, base=0,
                                        pattern=[[0, NPAIR], [-1, S]], channel_multiplier=1).then_inc(c_misc, 1)
            pool.wait_ge(c_misc, 4 + E0 + 2)
            nc.gpsimd.affine_select(out=trib[:, :], in_=trib[:, :], compare_op=ALU.is_gt, fill=0.0, base=0,
                                    pattern=[[1, P]], channel_multiplier=-1).then_inc(c_misc, 1)
            for p2 in range(2):
                pool.wait_ge(c_misc, 4 + E0 + 3 + p2)
                nc.gpsimd.memset(Vb[p2 * S:(p2 + 1) * S, :, :, p2, 2 * HD], 1.0).then_inc(c_misc, 1)
            pool.wait_ge(ld_qk[1], 128)
            pool.dma_start(masku[:, :], w["mask_BxS2_bk0"].rearrange("b s -> (b s)").partition_broadcast(P)
                           ).then_inc(ld_mask, 16)
            for dst, name, one in ((W1a, "L0_ffn_w1", "L0_ffn_sw1"), (W3a, "L0_ffn_w3", "L0_ffn_sw3"),
                                   (W2a, "L0_ffn_w2", "L0_ffn_sw2")):
                pool.dma_start(dst[:, 0:E0, :], w[name].rearrange("e d f -> d e f")).then_inc(ld_f0, 16)
                pool.dma_start(dst[:, E0, :], w[one]).then_inc(ld_f0, 16)
            pool.dma_start(b2a[0:E0, :], w["L0_ffn_b2"]).then_inc(ld_f0, 16)
            pool.dma_start(b2a[E0:E0 + 1, :], w["L0_ffn_sb2"].unsqueeze(0)).then_inc(ld_f0, 16)
            pool.dma_start(Wk1[:, :], w["L1_xattn_W_k"]).then_inc(ld_x1, 16)
            pool.dma_start(Wv1[:, :], w["L1_xattn_W_v"]).then_inc(ld_x1, 16)
            pool.dma_start(Wq1[:, :], w["L1_xattn_W_q"]).then_inc(ld_x1, 16)
            pool.dma_start(Wo1[:, :, :], w["L1_xattn_W_o"].rearrange("(h p) d -> p h d", p=P)).then_inc(ld_x1, 16)
            for dst, name in ((gamma, "L1_attn_gamma"), (beta, "L1_attn_beta"), (bo, "L1_xattn_b_o")):
                pool.dma_start(dst[:, :], w[name].partition_broadcast(P)).then_inc(ld_rows, 16)
            pool.dma_start(Wg[:, :], w["L1_ffn_Wg"]).then_inc(ld_rows, 16)
            for h in range(2):
                pool.wait_ge(b_added[h], 1)
                pool.wait_ge(xn_ready[h], 3 * HT)
                for e in range(E0 + 1):
                    i = (E0 + 1) * h + e
                    pool.wait_ge(f_part, i + 1)
                    if i >= 1:
                        pool.wait_ge(f_acc, i)
                    nc.gpsimd.tensor_tensor(X[:, h * HT:(h + 1) * HT, :], X[:, h * HT:(h + 1) * HT, :],
                                            part0[:, i % 2, :, :], ALU.add).then_inc(f_acc, 1)
            pool.wait_ge(ld_rows, 64)
            for t in range(NT):
                if t % HT == 0:
                    h = t // HT
                    pool.wait_ge(xn_ready[h], 5 * HT)
                    rows = X[:, h * HT:(h + 1) * HT, :]
                    nc.gpsimd.tensor_tensor(rows, rows, per_col(bo[:, :], HT), ALU.add).then_inc(bo_added, 1)
                pool.wait_ge(c_sum, t + 1)
                e = Es[:, t % 3, :].rearrange("p (a s) -> p a s", s=S)
                nc.gpsimd.tensor_tensor(e, e, per_row(sm[:, t, 2, :], S), ALU.mult).then_inc(c_prob, 1)
        C_MISC = 4 + E0 + 2 + 1 + 2

        @block.tensor
        def _(pe):
            mm = nc.tensor.matmul

            def transpose_xn(n, h, b):
                pe.wait_ge(xn_ready[h], HT * (n + 1))
                if n == 2 and h == 1:
                    pe.wait_ge(g_combc[0], 1)
                if n == 3 and h == 0:
                    pe.wait_ge(g_combc[1], 1)
                for t in range(HT):
                    last = nc.tensor.transpose(bank[b][:, t * P:(t + 1) * P], XN[:, h * HT + t, :], ident[:, :])
                last.then_inc(xt_psum[h], 1)

            pe.wait_ge(c_ident, 1)
            pe.wait_ge(ld_vecs, 128)
            nc.tensor.transpose(bank[4][:, 0:31], vecs[:, :], ident[0:31, 0:31]).then_inc(prep_psum, 1)
            pe.wait_ge(c_wp, 1)
            pe.wait_ge(prep_act, 1)
            for h in range(2):
                transpose_xn(0, h, h)
                pe.wait_ge(xt_ready[h], 1)
                if h == 1:
                    for g in range(2):
                        mm(bank[6 + g][:, :], Wp[:, 2, :], XT[:, half(g)], start=True, stop=True).then_inc(v_psum, 1)
                for s in range(2):
                    mm(bank[2 + 2 * h + s][:, :], Wp[:, s, :], XT[:, half(h)].rearrange("d (g t) -> d t g", t=GT),
                       start=True, stop=True).then_inc(qk_psum, 1)
            pe.wait_ge(ld_ctx, 16)
            for h in range(2):
                pe.wait_ge(xt_ready[h], 1)
                for t in range(HT):
                    last = nc.tensor.transpose(bank[h][0:DC, t * P:(t + 1) * P], CTX[:, HT * h + t, :], ident[:, :])
                last.then_inc(prep_psum, 1)
            pe.wait_ge(ld_ssm, 144)
            pe.wait_ge(qk_copied, 1)
            nc.tensor.transpose(bank[2][:, 0:NS], Bn[:, :], ident[0:NS, 0:NS])
            nc.tensor.transpose(bank[2][:, NS:NS + P], Cn[:, :, :].rearrange("p q n -> p (q n)"), ident[:, :])
            nc.tensor.transpose(bank[2][:, NS + P:NS + 2 * P], Apow[:, 0, 0, :], ident[:, :]).then_inc(prep_psum, 1)
            pe.wait_ge(ld_x0, 48)
            pe.wait_ge(prep_act, 3)
            for h in range(2):
                mm(bank[h][:, :], Wk0[:, :], CTXT[:, half(h)], start=True, stop=True).then_inc(prep_psum, 1)
            pe.wait_ge(v_copied, 2)
            for h in range(2):
                for t in range(HT):
                    last = mm(bank[6 + h][:, t * P:(t + 1) * P], CTXT[:, (HT * h + t) * P:(HT * h + t + 1) * P],
                              Wv0[:, :], start=True, stop=True)
                last.then_inc(v0_psum, 1)
            pe.wait_ge(v_order, 4)
            pe.wait_ge(v0_ready, 2)
            for g2 in range(2):
                for p4 in range(4):
                    src = V2r[:, p4, g2, :, :, :].rearrange("p r c t -> p (r c t)")
                    last = nc.tensor.transpose(bank[6 + g2][:, p4 * P:(p4 + 1) * P], src, ident[:, :])
                last.then_inc(v2_psum, 1)

            def head_cols(t, n, pair, g2):
                head = (n % HB) * 2 * NPAIR + 2 * pair + g2
                return t[:, n // HB, :].rearrange("p (s g) -> p s g", s=S)[:, :, head]

            def scores(n):
                if n % HB == 0:
                    pe.wait_ge(ld_qk[n // HB], 128)
                if n == 0:
                    pe.wait_ge(c_misc, C_MISC)
                    pe.wait_ge(prep_act, 5)
                    pe.wait_ge(pow_ready, 1)
                if n >= 3:
                    pe.wait_ge(a_sub, n - 2)
                dst = bank[n % 3]
                mm(dst[:, :], perm[:, :], causal[:, :, :].rearrange("p a (t c) -> p a c t", c=CH), start=True,
                   stop=False, skip_group_check=True)
                for pair in range(NPAIR):
                    for g2 in range(2):
                        last = mm(dst[g2 * S:(g2 + 1) * S, pair * S:(pair + 1) * S], head_cols(Q9, n, pair, g2),
                                  head_cols(K9, n, pair, g2), start=False, stop=(pair == NPAIR - 1),
                                  skip_group_check=True)
                last.then_inc(a_scores, 1)

            def transpose_probs(n):
                pe.wait_ge(a_exp, n + 1)
                if n >= 2:
                    pe.wait_ge(a_trc, n - 1)
                for p4 in range(4):
                    last = nc.tensor.transpose(bank[3 + n % 2][:, p4 * P:(p4 + 1) * P],
                                               Es[:, n % 3, p4 * P:(p4 + 1) * P], ident[:, :])
                last.then_inc(a_tr, 1)

            def weigh_values(n):
                pe.wait_ge(a_trc, n + 1)
                if n == 0:
                    pe.wait_ge(vb_act, 2)
                    pe.wait_ge(vb_dve, 2)
                if n >= 1:
                    pe.wait_ge(a_norm, n)
                for p4 in range(4):
                    first = (4 * n + p4) * 2 * VW
                    last = mm(bank[5][:, p4 * VN:(p4 + 1) * VN],
                              PTs[:, n % 2, p4 * P:(p4 + 1) * P], att[:, first:first + VN], start=True, stop=True)
                last.then_inc(a_pv, 1)

            def outputs_by_feature(h):
                pe.wait_ge(a_norm, HB * (h + 1))
                if h == 0:
                    pe.wait_ge(vb_act, 2)
                    pe.wait_ge(vb_dve, 2)
                for pair in range(NPAIR):
                    last = nc.tensor.transpose(bank[(6, 0)[h] + pair // 4][0:S, (pair % 4) * P:(pair % 4 + 1) * P],
                                               Opos[:, h, pair, :, :].rearrange("p e b -> p (e b)"), ident[:, :])
                    if pair % 4 == 3:
                        last.then_inc(o_psum[h], 1)

            def power(r):
                pe.wait_ge(pow_ready, r)
                mm(bank[3][:, 0:P], Apow[:, r - 1, 1, :], Apow[:, r - 1, 0, :], start=True, stop=True)
                mm(bank[3][:, P:2 * P], Apow[:, r - 1, 0, :], Apow[:, r - 1, 1, :], start=True, stop=True
                   ).then_inc(pow_psum, 1)

            def outputs_by_token(h):
                pe.wait_ge(ld_o[h], 16)
                if h == 0:
                    pe.wait_ge(o_act[0], 1)
                else:
                    pe.wait_ge(b_added[0], 1)
                for t in range(HT):
                    last = nc.tensor.transpose(bank[6][:, t * P:(t + 1) * P],
                                               OT[:, (h * HT + t) * P:(h * HT + t + 1) * P], ident[:, :])
                last.then_inc(x_psum[h], 1)

            def cross0_q(h):
                pe.wait_ge(xt_ready[h], 2)
                mm(bank[6][:, :], Wq0[:, :], XT[:, half(h)], start=True, stop=True).then_inc(b_q[h], 1)

            def cross0_scores(h):
                pe.wait_ge(b_qc[h], 1)
                pe.wait_ge(prep_act, 5)
                for i in range(HB):
                    u, o, r, b = i // 4, (i // 2) % 2, i % 2, h * HB + i
                    last = mm(bank[6][o * S:(o + 1) * S, (2 * u + r) * S:(2 * u + r + 1) * S],
                              Q0T[:, b * S:(b + 1) * S], K0T[:, b * S:(b + 1) * S], start=True, stop=True)
                last.then_inc(b_scores[h], 1)

            def cross0_transpose(h):
                pe.wait_ge(b_prob[h], 1)
                for u in range(2):
                    last = nc.tensor.transpose(bank[6][:, u * P:(u + 1) * P],
                                               E0s[:, h * HALF + u * P:h * HALF + (u + 1) * P], ident[:, :])
                last.then_inc(b_tr[h], 1)

            def cross0_values(h):
                pe.wait_ge(b_trc[h], 1)
                pe.wait_ge(v0_ready, 2)
                for i in range(HB):
                    u, o, r, t = i // 4, (i // 2) % 2, i % 2, i // 2
                    first = h * HALF + 2 * P + u * P + o * S
                    last = mm(bank[6][r * S:(r + 1) * S, t * P:(t + 1) * P], E0s[r * S:(r + 1) * S, first:first + S],
                              V0[r * S:(r + 1) * S, h * HT + t, :], start=True, stop=True)
                last.then_inc(b_pv[h], 1)

            def gate(h):
                pe.wait_ge(xt_ready[h], 3)
                for t in range(HT):
                    tt = h * HT + t
                    last = mm(bank[7][:, t * E0:(t + 1) * E0], XT[:, tt * P:(tt + 1) * P], cols[:, 23:31],
                              start=True, stop=True)
                last.then_inc(g_psum[h], 1)

            def gate_transpose(h):
                pe.wait_ge(g_comb[h], 1)
                for t in range(HT):
                    last = nc.tensor.transpose(bank[7][0:E0 + 1, t * P:(t + 1) * P], comb[:, h * HT + t, :],
                                               ident[:, :])
                last.then_inc(g_combt[h], 1)

            def up0_first(h, e):
                i = (E0 + 1) * h + e
                if i == 0:
                    pe.wait_ge(ld_f0, 128)
                    pe.wait_ge(a_norm, B)
                if e == 0:
                    pe.wait_ge(xt_ready[h], 3)
                if i >= 2:
                    pe.wait_ge(f_silu, i - 1)
                mm(bank[i % 2][:, :], W1a[:, e, :], XT[:, half(h)], start=True, stop=True).then_inc(f_h1, 1)

            def up0_third(h, e):
                i = (E0 + 1) * h + e
                if i >= 2:
                    pe.wait_ge(f_h, i - 1)
                mm(bank[2 + i % 2][:, :], W3a[:, e, :], XT[:, half(h)], start=True, stop=True).then_inc(f_h3, 1)

            def up0(h, e):
                up0_first(h, e)
                up0_third(h, e)

            def down0(h, e):
                i = (E0 + 1) * h + e
                shared = e == E0
                pe.wait_ge(f_h, i + 1)
                if i >= 2:
                    pe.wait_ge(f_part, i - 1)
                if shared:
                    pe.wait_ge(g_combc[h], 1)
                for t in range(HT):
                    dst = bank[4 + i % 2][:, t * P:(t + 1) * P]
                    tt = h * HT + t
                    last = mm(dst, hid0[:, i % 2, t * P:(t + 1) * P], W2a[:, e, :], start=True, stop=not shared)
                    if shared:
                        last = mm(dst, combT[:, tt * P:(tt + 1) * P], b2a[:, :], start=False, stop=True)
                last.then_inc(f_out, 1)

            def keys_values1(j):
                h, i = j // 8, (j % 8) // 2
                if j == 0:
                    pe.wait_ge(f_h, 2 * (E0 + 1))
                    pe.wait_ge(ld_x1, 64)
                    pe.wait_ge(mask_ready, 3)
                if 4 <= j < 13:
                    pe.wait_ge(kv_ready, j - 3)
                if j == 14:
                    pe.wait_ge(s_gelu[1], 1)
                if j == 15:
                    pe.wait_ge(kv_ready, 14)
                if j % 2 == 0:
                    last = mm(bank[kv_bank(j)][:, :], Wk1[:, i * P:(i + 1) * P], CTXTM[:, half(h)], start=True, stop=True)
                else:
                    tile = HT * h + i
                    last = mm(bank[kv_bank(j)][:, :], CTXT[:, tile * P:(tile + 1) * P], Wv1[:, :], start=True, stop=True)
                last.then_inc(kv_psum, 1)

            def inject(h):
                pe.wait_ge(xt_ready[h], 4)
                for q in range(BQ):
                    first = h * HALF + q * 2 * S
                    last = mm(bank[7][q * NS:(q + 1) * NS, 0:2 * S], BT[:, :], XT[:, first:first + 2 * S],
                              start=True, stop=False, skip_group_check=True)
                last.then_inc(s_psum[h], 1)

            def widen(h, r):
                k = 2 ** r
                pe.wait_ge(s_state[h], r + 1)
                dst = bank[7][:, 0:2 * S].rearrange("p (b s) -> p b s", s=S)[:, :, k:S]
                mm(dst, Apow[:, r, 1, :], ST[:, h, :, 0:S - k], start=False, stop=(r == ROUNDS - 1),
                   skip_group_check=True).then_inc(s_psum[h], 1)

            def read_out(h):
                pe.wait_ge(s_state[h], ROUNDS + 1)
                if h == 1:
                    pe.wait_ge(s_gelu[0], 1)
                mm(bank[6][:, :], ST[:, h, :, :].rearrange("p b s -> p (b s)"),
                   CT[:, :, :].rearrange("p q d -> p (q d)"), start=True, stop=True).then_inc(s_y[h], 1)

            def queries1(h, i):
                if i == 0:
                    pe.wait_ge(xt_ready[h], 5)
                    pe.wait_ge(f_part, 2 * (E0 + 1))
                if i >= 2:
                    pe.wait_ge(c_qc[h], i - 1)
                mm(bank[4 + 2 * h + i % 2][:, :], Wq1[:, i * P:(i + 1) * P], XT[:, half(h)], start=True, stop=True
                   ).then_inc(c_q[h], 1)

            def scores1(t):
                if t % HT == 0:
                    pe.wait_ge(c_qc[t // HT], 4)
                    pe.wait_ge(kv_ready, 13 if t == 0 else 16)
                if t >= 2:
                    pe.wait_ge(c_sub, t - 1)
                dst = bank[t % 2]
                bias = per_col(maskrow[0:1, t * P:(t + 1) * P], NHP)
                mm(dst[:, :], onesb[0:1, :], bias, start=True, stop=False, skip_group_check=True)
                for hp in range(NHP):
                    for b2 in range(2):
                        for h2 in range(2):
                            tok = slice(t * P + b2 * S, t * P + (b2 + 1) * S)
                            last = mm(dst[h2 * S:(h2 + 1) * S, (2 * hp + b2) * S:(2 * hp + b2 + 1) * S],
                                      Q1T[h2 * DH1:(h2 + 1) * DH1, hp, tok], K1T[h2 * DH1:(h2 + 1) * DH1, hp, tok],
                                      start=False, stop=(hp == NHP - 1), skip_group_check=True)
                last.then_inc(c_scores, 1)

            def transpose_probs1(t):
                pe.wait_ge(c_prob, t + 1)
                if t >= 1:
                    pe.wait_ge(c_trc, t)
                for hp in range(NHP):
                    last = nc.tensor.transpose(bank[2][:, hp * P:(hp + 1) * P],
                                               Es[:, t % 3, hp * P:(hp + 1) * P], ident[:, :])
                last.then_inc(c_tr, 1)

            def weigh_values1(t):
                pe.wait_ge(c_trc, t + 1)
                if t >= 1:
                    pe.wait_ge(c_otc, 2 * t)
                for hp in range(NHP):
                    for b2 in range(2):
                        for h2 in range(2):
                            g = 2 * hp + h2
                            last = mm(bank[3 + b2][h2 * S:(h2 + 1) * S, hp * S:(hp + 1) * S],
                                      V1[b2 * S:(b2 + 1) * S, t, g * DH1:(g + 1) * DH1],
                                      PTs[b2 * S:(b2 + 1) * S, t % 2, hp * P + h2 * S:hp * P + (h2 + 1) * S],
                                      start=True, stop=True)
                last.then_inc(c_pv, 1)

            def project_out(t):
                pe.wait_ge(c_otc, 2 * t + 2)
                if t >= 1:
                    pe.wait_ge(c_added, t)
                for hp in range(NHP):
                    last = mm(bank[5][:, 0:D], OTs[:, t % 2, hp, :], Wo1[:, hp, :],
                              start=(hp == 0), stop=(hp == NHP - 1))
                last.then_inc(c_wo, 1)

            def up1(e, f, h):
                i = 4 * e + 2 * h + f
                if e == 0 and f == 0:
                    pe.wait_ge(xt_ready[h], 6)
                if i == 0:
                    pe.wait_ge(c_otc, 2 * NT)
                    pe.wait_ge(ld_f1, 16 * (1 + E1))
                if i >= 4:
                    pe.wait_ge(m_gelu, i - 3)
                mm(bank[i % 4][:, :], W1b[:, e, f * P:(f + 1) * P], XT[:, half(h)], start=True, stop=True
                   ).then_inc(m_up, 1)

            def down1(e, h):
                pe.wait_ge(m_gelu, 4 * e + 2 * h + 2)
                if e == 0:
                    pe.wait_ge(c_added, NT)
                else:
                    pe.wait_ge(m_ys, 2 * (e - 1) + h + 1)
                for t in range(HT):
                    tile = slice((HT * h + t) * P, (HT * h + t + 1) * P)
                    for f in range(F1):
                        last = mm(bank[4 + h][:, t * P:(t + 1) * P], hid[:, e % 2, f, tile], W2b[:, e, f, :],
                                  start=(f == 0), stop=(f == F1 - 1))
                last.then_inc(m_down, 1)

            def route(h):
                pe.wait_ge(xt_ready[h], 6)
                for t in range(HT):
                    tt = HT * h + t
                    last = mm(bank[7][:, tt * E1:(tt + 1) * E1], XT[:, tt * P:(tt + 1) * P], Wg[:, :],
                              start=True, stop=True)
                last.then_inc(r_psum, 1)

            def count(i):
                pe.wait_ge(r_hit, i + 1)
                mm(bank[6][:, 0:NC * E1 * NT], onesb[:, :], hit[:, :, :].rearrange("p a t -> p (a t)"),
                   start=True, stop=True).then_inc(r_cnt, 1)

            def count_next(rounds):
                i = next(rounds, None)
                if i is not None:
                    count(i)
                if i == SEARCH:
                    prefix()

            def prefix():
                pe.wait_ge(r_eq, 1)
                mm(bank[7][:, 0:NT * E1], trib[:, :], eqb[:, :, :].rearrange("p t e -> p (t e)"),
                   start=True, stop=False, skip_group_check=True)
                for t in range(NT - 1):
                    last = mm(bank[7][:, (t + 1) * E1:NT * E1], onesb[:, :], per_col(eqb[:, t, :], NT - 1 - t),
                              start=False, stop=(t == NT - 2), skip_group_check=True)
                last.then_inc(r_pre, 1)

            for n in range(B + 3):
                if n < B:
                    scores(n)
                if 2 <= n < B + 2:
                    transpose_probs(n - 2)
                if n >= 3:
                    weigh_values(n - 3)
                if n == HB + 3:
                    outputs_by_feature(0)
                if n == B + 1:
                    outputs_by_token(0)
            outputs_by_feature(1)
            power(1)
            transpose_xn(1, 0, 7)
            power(2)
            cross0_q(0)
            cross0_scores(0)
            power(3)
            cross0_transpose(0)
            power(4)
            cross0_values(0)
            power(5)
            outputs_by_token(1)
            transpose_xn(2, 0, 7)
            up0(0, 0)
            gate(0)
            for e in range(E0 + 1):
                if e == 1:
                    cross0_q(1)
                if e == 7:
                    gate(1)
                up0_first((0, 1)[e == E0], (e + 1) % (E0 + 1))
                if e == 1:
                    cross0_scores(1)
                if e == 2:
                    gate_transpose(0)
                up0_third((0, 1)[e == E0], (e + 1) % (E0 + 1))
                if e == 0:
                    transpose_xn(1, 1, 6)
                down0(0, e)
                if e == 2:
                    cross0_transpose(1)
                if e == 3:
                    cross0_values(1)
                if e == 6:
                    transpose_xn(2, 1, 7)
            for e in range(E0 + 1):
                if e == 5:
                    widen(0, 1)
                if e == 6:
                    widen(0, 4)
                if e < E0:
                    up0_first(1, e + 1)
                if e == 2:
                    gate_transpose(1)
                if e == 4:
                    inject(0)
                if e == 5:
                    widen(0, 2)
                if e == 6:
                    widen(0, 5)
                if e < E0:
                    up0_third(1, e + 1)
                if e == 3:
                    transpose_xn(3, 0, 7)
                if e == 4:
                    widen(0, 0)
                if e == 5:
                    widen(0, 3)
                if e == 6:
                    read_out(0)
                down0(1, e)
            for j in range(8):
                keys_values1(j)
            transpose_xn(3, 1, 7)
            inject(1)
            for r in range(ROUNDS):
                widen(1, r)
                if r < 5:
                    keys_values1(8 + r)
            read_out(1)
            transpose_xn(4, 0, 7)
            for i in range(4):
                queries1(0, i)
            for t in range(NT + 3):
                if t < NT:
                    scores1(t)
                if t == 1:
                    for j in range(13, 15):
                        keys_values1(j)
                if t == 2:
                    keys_values1(15)
                if 2 <= t < NT + 2:
                    weigh_values1(t - 2)
                if 1 <= t < NT + 1:
                    transpose_probs1(t - 1)
                if t >= 3:
                    project_out(t - 3)
                if t == HT - 1:
                    pe.wait_ge(kv_ready, 16)
                    transpose_xn(4, 1, 6)
                    for i in range(4):
                        queries1(1, i)
                if t == NT + 1:
                    transpose_xn(5, 0, 6)
            route(0)
            for f in range(F1):
                up1(0, f, 0)
            down1(0, 0)
            transpose_xn(5, 1, 6)
            route(1)
            for f in range(F1):
                up1(0, f, 1)
            rounds = iter(range(SEARCH + 1))
            for e in range(E1):
                for h in range(2):
                    if e + 1 < E1:
                        for f in range(F1):
                            up1(e + 1, f, h)
                        count_next(rounds)
                for h in range(2):
                    if e + h > 0:
                        down1(e, h)
                        count_next(rounds)

        @block.scalar
        def _(act):
            AF = nc.scalar.activation

            def copy_xt(n, h, b):
                act.wait_ge(xt_psum[h], n + 1)
                AF(XT[:, half(h)], bank[b][:, :], ACT.Copy).then_inc(xt_ready[h], 1)

            act.wait_ge(prep_psum, 1)
            AF(cols[:, :], bank[4][:, 0:31], ACT.Copy).then_inc(prep_act, 1)
            copy_xt(0, 0, 0)
            act.wait_ge(prep_act, 1)

            def mid_part(i):
                act.wait_ge(qk_rest, i + 1)
                AF(QS[:, i % 2, 1, half(i // 2)], OT[:, (i % 2) * HALF:(i % 2 + 1) * HALF], ACT.Copy
                   ).then_inc(qk_mid, 1)

            for i in range(4):
                h, s = i // 2, i % 2
                act.wait_ge(qk_psum, i + 1)
                AF(QKVT[:, s, half(h)], bank[2 + i][:, :], ACT.Identity, bias=cols[:, s:s + 1])
                AF(QS[:, s, 0, half(h)], bank[2 + i][:, :], ACT.Identity, bias=cols[:, s:s + 1]).then_inc(qk_copied, 1)
                if i == 1:
                    copy_xt(0, 1, 1)
                if i in (1, 3):
                    mid_part(i - 1)
                    mid_part(i)
            for h in range(2):
                act.wait_ge(prep_psum, 2 + h)
                AF(CTXT[:, half(h)], bank[h][0:DC, :], ACT.Copy).then_inc(prep_act, 1)
            act.wait_ge(prep_psum, 4)
            act.wait_ge(c_fill, 4)
            AF(BT[:, :], bank[2][:, 0:NS], ACT.Copy)
            for q in range(BQ):
                rows = slice(q * NS, (q + 1) * NS)
                AF(CT[rows, q, :], bank[2][rows, NS:NS + P], ACT.Copy)
            AF(Apow[:, 0, 1, :], bank[2][:, NS + P:NS + 2 * P], ACT.Copy).then_inc(pow_ready, 1)
            for h in range(2):
                act.wait_ge(prep_psum, 5 + h)
                AF(K0T[:, half(h)], bank[h][:, :], ACT.Identity, bias=cols[:, 4:5]).then_inc(prep_act, 1)
            act.wait_ge(v2_psum, 1)
            act.wait_ge(c_misc, C_MISC)
            for p2 in range(2):
                AF(Vb[p2 * S:(p2 + 1) * S, :, :, p2, 0:HD].rearrange("p b q e -> p q e b"),
                   bank[6][p2 * S:(p2 + 1) * S, :].rearrange("p (q e b) -> p q e b", q=4, e=HD), ACT.Copy
                   ).then_inc(vb_act, 1)

            def power(r):
                act.wait_ge(pow_psum, r)
                AF(Apow[:, r, :, :], bank[3][:, 0:2 * P].rearrange("p (a n) -> p a n", a=2), ACT.Copy
                   ).then_inc(pow_ready, 1)

            def exponentials(n):
                act.wait_ge(a_sub, n + 1)
                AF(Es[:, n % 3, :], Es[:, n % 3, :], ACT.Exp, scale=ATTN_SCALE).then_inc(a_exp, 1)

            def copy_probs(n):
                act.wait_ge(a_tr, n + 1)
                if n >= 2:
                    act.wait_ge(a_pv, n - 1)
                AF(PTs[:, n % 2, :], bank[3 + n % 2][:, :], ACT.Copy).then_inc(a_trc, 1)

            def outputs_by_feature(h):
                act.wait_ge(o_psum[h], 1)
                if h == 1:
                    act.wait_ge(st_o[0], 16)
                AF(OT2[:, :, 0:S // 2].rearrange("p c (q g t) -> p q g c t", q=4, g=2)[:, :, 0, :, :],
                   bank[(6, 0)[h]][0:S, :].rearrange("p (q g c t) -> p q g c t", q=4, g=2, c=CH)[:, :, 0, :, :], ACT.Copy)
                AF(OT2[:, :, 0:S // 2].rearrange("p c (q g t) -> p q g c t", q=4, g=2)[:, :, 1, :, :],
                   bank[(6, 0)[h]][0:S, :].rearrange("p (q g c t) -> p q g c t", q=4, g=2, c=CH)[:, :, 1, :, :], ACT.Copy
                   ).then_inc(o_act[h], 1)

            def cross0_q(h):
                act.wait_ge(b_q[h], 1)
                AF(Q0T[:, half(h)], bank[6][:, :], ACT.Identity, bias=cols[:, 3:4]).then_inc(b_qc[h], 1)

            def cross0_exp(h):
                act.wait_ge(b_sub[h], 1)
                e = E0s[:, h * HALF:h * HALF + 2 * P]
                AF(e, e, ACT.Exp, scale=XATTN0_SCALE).then_inc(b_exp[h], 1)

            def cross0_copy(h):
                act.wait_ge(b_tr[h], 1)
                AF(E0s[:, h * HALF + 2 * P:(h + 1) * HALF], bank[6][:, 0:2 * P], ACT.Copy).then_inc(b_trc[h], 1)

            def gate_exp(h):
                act.wait_ge(g_sub[h], 1)
                AF(rt[:, 1, tiles(h), :], rt[:, 1, tiles(h), :], ACT.Exp).then_inc(g_exp[h], 1)

            def gate_copy(h):
                act.wait_ge(g_combt[h], 1)
                AF(combT[:, half(h)], bank[7][0:E0 + 1, :], ACT.Copy).then_inc(g_combc[h], 1)

            def silu(h, e):
                i = (E0 + 1) * h + e
                act.wait_ge(f_h1, i + 1)
                if i >= 1:
                    act.wait_ge(f_h, i)
                AF(sil0[:, :], bank[i % 2][:, :], ACT.Silu, bias=cols[:, 5 + e:6 + e]).then_inc(f_silu, 1)

            def weigh0(h, e):
                i = (E0 + 1) * h + e
                act.wait_ge(f_out, i + 1)
                act.wait_ge(g_comb[h], 1)
                if i >= 2:
                    act.wait_ge(f_acc, i - 1)
                for t in range(HT):
                    tt = HT * h + t
                    last = AF(part0[:, i % 2, t, :], bank[4 + i % 2][:, t * P:(t + 1) * P], ACT.Copy,
                              scale=comb[:, tt, e:e + 1])
                last.then_inc(f_part, 1)

            def keys_values1(j):
                h, i = j // 8, (j % 8) // 2
                act.wait_ge(kv_psum, j + 1)
                dst = K1T[:, i, half(h)] if j % 2 == 0 else V1[:, HT * h + i, :]
                AF(dst, bank[kv_bank(j)][:, :], ACT.Copy).then_inc(kv_ready, 1)

            def gelu_states(h):
                act.wait_ge(s_y[h], 1)
                AF(GA[:, tiles(h), :], bank[6][:, :].rearrange("p (t d) -> p t d", d=D), ACT.Gelu
                   ).then_inc(s_gelu[h], 1)

            def queries1(h, i):
                act.wait_ge(c_q[h], i + 1)
                AF(Q1T[:, i, half(h)], bank[4 + 2 * h + i % 2][:, :], ACT.Copy).then_inc(c_qc[h], 1)

            def exponentials1(t):
                act.wait_ge(c_sub, t + 1)
                AF(Es[:, t % 3, :], Es[:, t % 3, :], ACT.Exp, scale=XATTN1_SCALE).then_inc(c_exp, 1)

            def copy_probs1(t):
                act.wait_ge(c_tr, t + 1)
                if t >= 2:
                    act.wait_ge(c_pv, t - 1)
                AF(PTs[:, t % 2, :], bank[2][:, :], ACT.Copy).then_inc(c_trc, 1)

            def copy_values1(t):
                act.wait_ge(c_pv, t + 1)
                if t >= 2:
                    act.wait_ge(c_wo, t - 1)
                for b2 in range(2):
                    AF(OTs[:, t % 2, :, b2 * S:(b2 + 1) * S],
                       bank[3 + b2][:, 0:NHP * S].rearrange("p (h n) -> p h n", n=S), ACT.Copy).then_inc(c_otc, 1)

            def gelu(e, f, h):
                i = 4 * e + 2 * h + f
                act.wait_ge(m_up, i + 1)
                if e >= 2:
                    act.wait_ge(m_down, 2 * (e - 2) + h + 1)
                AF(hid[:, e % 2, f, half(h)], bank[i % 4][:, :], ACT.Gelu).then_inc(m_gelu, 1)

            def copy_ys(e, h):
                act.wait_ge(m_down, 2 * e + h + 1)
                AF(ys[:, e, tiles(h), :], bank[4 + h][:, :].rearrange("p (t d) -> p t d", d=D), ACT.Copy
                   ).then_inc(m_ys, 1)

            for n in range(B + 2):
                if n < B:
                    exponentials(n)
                if n >= 1 and n - 1 < B:
                    copy_probs(n - 1)
                if n == HB + 4:
                    outputs_by_feature(0)
            outputs_by_feature(1)
            power(1)
            copy_xt(1, 0, 7)
            cross0_q(0)
            power(2)
            power(3)
            cross0_exp(0)
            cross0_copy(0)
            power(4)
            power(5)
            copy_xt(2, 0, 7)
            gate_exp(0)
            silu(0, 0)
            for e in range(1, E0 + 1):
                silu(0, e)
                if e == 1:
                    copy_xt(1, 1, 6)
                    cross0_q(1)
                if e == 3:
                    gate_copy(0)
                if e == 7:
                    copy_xt(2, 1, 7)
                weigh0(0, e - 1)
                if e == 2:
                    cross0_exp(1)
                if e == 3:
                    cross0_copy(1)
                if e == 8:
                    gate_exp(1)
            for e in range(E0 + 1):
                silu(1, e)
                if e == 4:
                    copy_xt(3, 0, 7)
                if e == E0:
                    gelu_states(0)
                weigh0((0, 1)[e > 0], (e - 1) % (E0 + 1))
                if e == 3:
                    gate_copy(1)
            weigh0(1, E0)
            for j in range(8):
                keys_values1(j)
            copy_xt(3, 1, 7)
            for j in range(8, 13):
                keys_values1(j)
            gelu_states(1)
            copy_xt(4, 0, 7)
            for i in range(4):
                queries1(0, i)
            for t in range(NT + 2):
                if t == 1:
                    for j in range(13, 15):
                        keys_values1(j)
                if t < NT:
                    exponentials1(t)
                if t == 2:
                    keys_values1(15)
                if t >= 2:
                    copy_values1(t - 2)
                if 1 <= t < NT + 1:
                    copy_probs1(t - 1)
                if t == HT - 1:
                    copy_xt(4, 1, 6)
                    for i in range(4):
                        queries1(1, i)
            copy_xt(5, 0, 6)
            for f in range(F1):
                gelu(0, f, 0)
            copy_ys(0, 0)
            copy_xt(5, 1, 6)
            act.wait_ge(r_sub, 1)
            AF(rt[:, 1, :, :], rt[:, 1, :, :], ACT.Exp).then_inc(r_exp, 1)
            for f in range(F1):
                gelu(0, f, 1)
            for e in range(E1):
                for h in range(2):
                    for f in range(F1):
                        if e + 1 < E1:
                            gelu(e + 1, f, h)
                for h in range(2):
                    if e + h > 0:
                        copy_ys(e, h)

        @block.vector
        def _(dve):
            V = nc.vector
            steps = [0]

            def then(ins):
                steps[0] += 1
                ins.then_inc(v_step, 1)
                dve.wait_ge(v_step, steps[0])

            def moments(src, h):
                for t in range(h * HT, (h + 1) * HT):
                    last = V.bn_stats(stats[:, t, :], src[:, t, :])
                then(last)
                for t in range(h * HT, (h + 1) * HT):
                    last = V.bn_aggr(mv[:, t, :], stats[:, t, :])
                then(last)

            def root_guess(h):
                r, var, bits = rs[:, 0, tiles(h)], rs[:, 1, tiles(h)], rs[:, 4, tiles(h)]
                then(V.tensor_scalar(var, mv[:, tiles(h), 1], EPS, None, ALU.add))
                then(V.tensor_scalar(bits.bitcast(int32), var.bitcast(int32), 1, None, ALU.logical_shift_right))
                then(V.tensor_tensor(r.bitcast(int32), magic[:, :], bits.bitcast(int32), ALU.subtract))

            def root_third(h):
                r, var, y2, p = (rs[:, i, tiles(h)] for i in range(4))
                then(V.tensor_tensor(y2, r, r, ALU.mult))
                then(V.tensor_tensor(y2, y2, var, ALU.mult))
                then(V.tensor_scalar(p, y2, 0.375, -1.25, ALU.mult, ALU.add))
                then(V.tensor_tensor(p, p, y2, ALU.mult))
                then(V.scalar_tensor_tensor(r, p, 1.875, r, ALU.add, ALU.mult))

            def root_second(h):
                r, var, y2, p = (rs[:, i, tiles(h)] for i in range(4))
                then(V.tensor_tensor(y2, r, r, ALU.mult))
                then(V.scalar_tensor_tensor(p, y2, -0.5, var, ALU.mult, ALU.mult))
                then(V.scalar_tensor_tensor(r, p, 1.5, r, ALU.add, ALU.mult))

            def root(h):
                root_guess(h)
                root_third(h)
                root_second(h)

            def ln_moments(n, h):
                if n == 3:
                    dve.wait_ge(f_acc, (E0 + 1) * (h + 1))
                moments(X, h)

            def ln_apply(n, h):
                if n >= 1:
                    dve.wait_ge(xt_ready[h], n)
                for t in range(h * HT, (h + 1) * HT):
                    V.tensor_scalar(XN[:, t, :], X[:, t, :], mv[:, t, 0:1], rs[:, 0, t:t + 1], ALU.subtract, ALU.mult
                                    ).then_inc(xn_ready[h], 1)

            def layernorm(n, h):
                ln_moments(n, h)
                root(h)
                ln_apply(n, h)

            def less_max(logits, cut, sub_done):
                then(V.tensor_reduce(rv[:, 0, cut], logits, AX.X, ALU.max))
                V.tensor_tensor(rt[:, 1, cut, :], logits, per_row(rv[:, 0, cut], E0), ALU.subtract).then_inc(sub_done, 1)

            def over_sum(cut, exp_done):
                dve.wait_ge(exp_done, 1)
                then(V.tensor_reduce(rv[:, 1, cut], rt[:, 1, cut, :], AX.X, ALU.add))
                then(V.reciprocal(rv[:, 2, cut], rv[:, 1, cut]))
                then(V.tensor_tensor(rt[:, 0, cut, :], rt[:, 1, cut, :], per_row(rv[:, 2, cut], E0), ALU.mult))

            def first_max(src, one_hot, cut):
                then(V.tensor_reduce(rv[:, 3, cut], src, AX.X, ALU.max))
                then(V.tensor_tensor(rt[:, 2, cut, :], src, per_row(rv[:, 3, cut], E0), ALU.is_equal))
                then(V.tensor_tensor(rt[:, 2, cut, :], rt[:, 2, cut, :], em8[:, cut, :], ALU.mult))
                then(V.tensor_reduce(rv[:, 4, cut], rt[:, 2, cut, :], AX.X, ALU.min))
                then(V.tensor_tensor(one_hot, em8[:, cut, :], per_row(rv[:, 4, cut], E0), ALU.is_equal))

            dve.wait_ge(c_magic, 1)
            for h in range(2):
                dve.wait_ge(ld_x[h], 16)
                layernorm(0, h)
            for i in range(4):
                h, s = i // 2, i % 2
                dve.wait_ge(qk_copied, i + 1)
                rest = OT[:, s * HALF:(s + 1) * HALF]
                if i >= 2:
                    dve.wait_ge(qk_low, i - 1)
                V.tensor_tensor(rest, QKVT[:, s, half(h)], QS[:, s, 0, half(h)], ALU.subtract).then_inc(qk_rest, 1)
                dve.wait_ge(qk_mid, i + 1)
                V.tensor_tensor(QS[:, s, 2, half(h)], rest, QS[:, s, 1, half(h)], ALU.subtract).then_inc(qk_low, 1)
                if i == 1:
                    for g in range(2):
                        dve.wait_ge(v_psum, g + 1)
                        V.tensor_scalar(QKVT[:, 2, half(g)], bank[6 + g][:, :], cols[:, 2:3], None, ALU.add
                                        ).then_inc(v_copied, 1)
            dve.wait_ge(ld_bv, 16)
            for h in range(2):
                dve.wait_ge(v0_psum, h + 1)
                V.tensor_tensor(V0[:, tiles(h), :], bank[6 + h][:, :].rearrange("p (t d) -> p t d", d=D),
                                per_col(bv0[:, :], HT), ALU.add).then_inc(v0_ready, 1)
            dve.wait_ge(ld_v2, 16)
            for g2 in range(2):
                for p2 in range(2):
                    src = V2[:, :, :].rearrange("p c (q r g t) -> p q r g c t", r=2, g=2, t=GT)[:, :, p2, g2, :, :]
                    V.tensor_copy(V2r[:, :, g2, p2, :, :], src).then_inc(v_order, 1)
            dve.wait_ge(v2_psum, 2)
            dve.wait_ge(c_misc, C_MISC)
            for p2 in range(2):
                V.tensor_copy(Vb[p2 * S:(p2 + 1) * S, :, :, p2, HD:2 * HD].rearrange("p b q e -> p q e b"),
                              bank[7][p2 * S:(p2 + 1) * S, :].rearrange("p (q e b) -> p q e b", q=4, e=HD)
                              ).then_inc(vb_dve, 1)

            def normalise(n):
                dve.wait_ge(a_pv, n + 1)
                o = bank[5][:, 0:4 * VN].rearrange("p (q v) -> p q v", q=4)[:, :, 0:2 * VW]
                o = o.rearrange("p q (r v) -> p q r v", r=2)
                then(V.reciprocal(rO[:, n, :].rearrange("p (q r) -> p q r", r=2), o[:, :, :, 2 * HD]))
                inv = rO[:, n, :].rearrange("p (q r) -> p q r", r=2)
                for g2 in range(2):
                    rows = slice(g2 * S, (g2 + 1) * S)
                    last = V.tensor_tensor(
                        Opos[rows, n // HB, :, :, n % HB].rearrange("p (q r) e -> p q r e", r=2),
                        o[rows, :, :, g2 * HD:(g2 + 1) * HD],
                        inv[rows, :, :].unsqueeze(3).broadcast_to([S, 4, 2, HD]), ALU.mult)
                last.then_inc(a_norm, 1)

            def subtract_max(n):
                dve.wait_ge(a_scores, n + 1)
                s = bank[n % 3][:, :].rearrange("p (a s) -> p a s", s=S)
                then(V.tensor_reduce(mx0[:, n, :], s, AX.X, ALU.max))
                if n >= 3:
                    dve.wait_ge(a_tr, n - 2)
                V.tensor_tensor(Es[:, n % 3, :].rearrange("p (a s) -> p a s", s=S), s, per_row(mx0[:, n, :], S),
                                ALU.subtract).then_inc(a_sub, 1)

            def outputs_by_feature(h):
                dve.wait_ge(o_psum[h], 2)
                if h == 1:
                    dve.wait_ge(st_o[0], 16)
                for g2 in range(2):
                    last = V.tensor_copy(
                        OT2[:, :, S // 2:S].rearrange("p c (q g t) -> p q g c t", q=4, g=2)[:, :, g2, :, :],
                        bank[(7, 1)[h]][0:S, :].rearrange("p (q g c t) -> p q g c t", q=4, g=2, c=CH)[:, :, g2, :, :])
                last.then_inc(o_dve[h], 1)

            def add_attention(h):
                dve.wait_ge(x_psum[h], 1)
                then(V.tensor_tensor(X[:, tiles(h), :], bank[6][:, :].rearrange("p (t d) -> p t d", d=D),
                                     X[:, tiles(h), :], ALU.add))

            def mask_context():
                dve.wait_ge(ld_mask, 16)
                V.tensor_copy(maskf[:, :], masku[:, :]).then_inc(mask_ready, 1)
                dve.wait_ge(mask_ready, 1)
                V.tensor_scalar(maskrow[:, :], maskf[0:1, :], 1.0, 2.0 ** 127, ALU.subtract, ALU.mult
                                ).then_inc(mask_ready, 1)
                dve.wait_ge(mask_ready, 2)
                dve.wait_ge(prep_act, 3)
                V.tensor_tensor(CTXTM, CTXT[:, :], CTXTM, ALU.mult).then_inc(mask_ready, 1)

            def cross0_sub(h):
                dve.wait_ge(b_scores[h], 1)
                s = bank[6][:, 0:2 * P].rearrange("p (a s) -> p a s", s=S)
                e = E0s[:, h * HALF:h * HALF + 2 * P].rearrange("p (a s) -> p a s", s=S)
                then(V.tensor_reduce(sm[:, NT + h, 0, 0:4], s, AX.X, ALU.max))
                V.tensor_tensor(e, s, per_row(sm[:, NT + h, 0, 0:4], S), ALU.subtract).then_inc(b_sub[h], 1)

            def cross0_prob(h):
                dve.wait_ge(b_exp[h], 1)
                e = E0s[:, h * HALF:h * HALF + 2 * P].rearrange("p (a s) -> p a s", s=S)
                then(V.tensor_reduce(sm[:, NT + h, 1, 0:4], e, AX.X, ALU.add))
                then(V.reciprocal(sm[:, NT + h, 2, 0:4], sm[:, NT + h, 1, 0:4]))
                V.tensor_tensor(e, e, per_row(sm[:, NT + h, 2, 0:4], S), ALU.mult).then_inc(b_prob[h], 1)

            def cross0_add(h):
                dve.wait_ge(b_pv[h], 1)
                V.tensor_tensor(X[:, tiles(h), :], bank[6][:, :].rearrange("p (t d) -> p t d", d=D),
                                X[:, tiles(h), :], ALU.add).then_inc(b_added[h], 1)
                dve.wait_ge(b_added[h], 1)

            def gate_sub(h):
                dve.wait_ge(g_psum[h], 1)
                less_max(bank[7][:, 0:HT * E0].rearrange("p (t e) -> p t e", e=E0), tiles(h), g_sub[h])

            def gate_first(h):
                cut = tiles(h)
                over_sum(cut, g_exp[h])
                first_max(rt[:, 0, cut, :], rt[:, 3, cut, :], cut)

            def gate_second(h):
                cut = tiles(h)
                then(V.scalar_tensor_tensor(rt[:, 4, cut, :], rt[:, 3, cut, :], -2.0, rt[:, 0, cut, :], ALU.mult, ALU.add))
                first_max(rt[:, 4, cut, :], rt[:, 5, cut, :], cut)
                then(V.tensor_tensor(rt[:, 3, cut, :], rt[:, 3, cut, :], rt[:, 5, cut, :], ALU.add))
                V.tensor_tensor(comb[:, cut, 0:E0], rt[:, 3, cut, :], rt[:, 0, cut, :], ALU.mult).then_inc(g_comb[h], 1)
                dve.wait_ge(g_comb[h], 1)

            def gate0(h, e):
                i = (E0 + 1) * h + e
                dve.wait_ge(f_silu, i + 1)
                dve.wait_ge(f_h3, i + 1)
                if i >= 2:
                    dve.wait_ge(f_out, i - 1)
                V.scalar_tensor_tensor(hid0[:, i % 2, :], bank[2 + i % 2][:, :], cols[:, 14 + e:15 + e],
                                       sil0[:, :], ALU.add, ALU.mult).then_inc(f_h, 1)

            def state(h, r):
                dve.wait_ge(s_psum[h], r + 1)
                V.tensor_copy(ST[:, h, :, :], bank[7][:, 0:2 * S].rearrange("p (b s) -> p b s", s=S)
                              ).then_inc(s_state[h], 1)

            def states_moments(h):
                dve.wait_ge(s_gelu[h], 1)
                moments(GA, h)

            def states_apply(h):
                for t in range(h * HT, (h + 1) * HT):
                    last = V.tensor_scalar(GB[:, t, :], GA[:, t, :], mv[:, t, 0:1], rs[:, 0, t:t + 1], ALU.subtract,
                                           ALU.mult)
                then(last)

            def norm_states(h):
                states_moments(h)
                root(h)
                states_apply(h)

            def affine_states(h):
                cut = tiles(h)
                dve.wait_ge(ld_rows, 64)
                then(V.tensor_tensor(GB[:, cut, :], GB[:, cut, :], per_col(gamma[:, :], HT), ALU.mult))
                then(V.tensor_tensor(GB[:, cut, :], GB[:, cut, :], per_col(beta[:, :], HT), ALU.add))

            def add_states(h, step):
                cut = tiles(h)
                ga, gb, mask = GA[:, cut, :], GB[:, cut, :], nanm[:, cut, :]
                if step == 0:
                    then(V.tensor_tensor(mask, gb, gb, ALU.is_equal))
                if step == 1:
                    then(V.tensor_scalar(ga, gb, CLAMP, -CLAMP, ALU.min, ALU.max))
                if step == 2:
                    then(V.tensor_tensor(ga, ga, mask, ALU.mult))
                if step == 3:
                    then(V.tensor_scalar(mask, gb, 0.0, 0.0, ALU.mult, ALU.is_equal))
                if step == 4:
                    then(V.copy_predicated(ga, mask, gb))
                if step == 5:
                    then(V.tensor_tensor(X[:, cut, :], ga, X[:, cut, :], ALU.add))

            def subtract_max1(t):
                dve.wait_ge(c_scores, t + 1)
                s = bank[t % 2][:, :].rearrange("p (a s) -> p a s", s=S)
                then(V.tensor_reduce(sm[:, t, 0, :], s, AX.X, ALU.max))
                if t >= 3:
                    dve.wait_ge(c_tr, t - 2)
                V.tensor_tensor(Es[:, t % 3, :].rearrange("p (a s) -> p a s", s=S), s,
                                per_row(sm[:, t, 0, :], S), ALU.subtract).then_inc(c_sub, 1)

            def probs1(t):
                dve.wait_ge(c_exp, t + 1)
                e = Es[:, t % 3, :].rearrange("p (a s) -> p a s", s=S)
                then(V.tensor_reduce(sm[:, t, 1, :], e, AX.X, ALU.add))
                V.reciprocal(sm[:, t, 2, :], sm[:, t, 1, :]).then_inc(c_sum, 1)

            def add1(t):
                dve.wait_ge(bo_added, t // HT + 1)
                dve.wait_ge(c_wo, t + 1)
                V.tensor_tensor(X[:, t, :], bank[5][:, 0:D], X[:, t, :], ALU.add).then_inc(c_added, 1)
                if t % HT == HT - 1:
                    dve.wait_ge(c_added, t + 1)

            def search_bits():
                dve.wait_ge(c_misc, C_MISC)
                for i in range(SEARCH):
                    last = V.tensor_scalar(jshift[:, i, :], jconst[:, :, :].rearrange("p j e -> p (j e)"),
                                           BITS - STEP * (i + 1), None, ALU.logical_shift_left)
                then(last)

            def route():
                dve.wait_ge(r_psum, 2)
                less_max(bank[7][:, 0:NT * E1].rearrange("p (t e) -> p t e", e=E1), slice(0, NT), r_sub)
                over_sum(slice(0, NT), r_exp)
                prob = rt[:, 0, :, :]
                prob_et = rt[:, 0, :, :].rearrange("p t e -> p e t")
                then(V.memset(thr[:, :], 0))
                for i in range(SEARCH):
                    shift = BITS - STEP * (i + 1)
                    bits = jshift[:, i, :].rearrange("p (j e) -> p j e", e=E1)
                    if i > 0:
                        then(V.tensor_tensor(cand[:, :, :], base[:, :, :], per_col(add[:, :], NC), ALU.bitwise_or))
                    levels = bits if i == 0 else cand[:, :, :]
                    V.tensor_tensor(hit[:, :, :].rearrange("p (j e) t -> p j e t", e=E1),
                                    prob_et.unsqueeze(1).broadcast_to([P, NC, E1, NT]),
                                    levels.bitcast(fp32).unsqueeze(3).broadcast_to([P, NC, E1, NT]), ALU.is_ge
                                    ).then_inc(r_hit, 1)
                    if i > 0:
                        then(V.tensor_tensor(thr[:, :], thr[:, :], add[:, :], ALU.bitwise_or))
                    if i + 1 < SEARCH:
                        then(V.tensor_tensor(base[:, :, :], jshift[:, i + 1, :].rearrange("p (j e) -> p j e", e=E1),
                                             per_col(thr[:, :], NC), ALU.bitwise_or))
                    dve.wait_ge(r_cnt, i + 1)
                    then(V.tensor_reduce(cnt[:, :, :].rearrange("p j e -> p (j e)"),
                                         bank[6][:, 0:NC * E1 * NT].rearrange("p (a t) -> p a t", t=NT), AX.X, ALU.add))
                    then(V.tensor_scalar(acc[:, :, :], cnt[:, :, :], CAP - 0.5, float(2 ** shift), ALU.is_ge, ALU.mult))
                    with nc.allow_low_precision(reason="up to NC times one power of two: exact"):
                        then(V.tensor_reduce(add[:, :], acc[:, :, :].rearrange("p j e -> p e j"), AX.X, ALU.add))
                then(V.tensor_tensor(thr[:, :], thr[:, :], add[:, :], ALU.bitwise_or))
                level = per_col(thr[:, :].bitcast(fp32), NT)
                above, tie, ahead = rt[:, 6, :, :], rt[:, 7, :, :], rt[:, 8, :, :]
                then(V.memset(hit[:, :, :], 0.0))
                then(V.tensor_tensor(above, prob, level, ALU.is_gt))
                V.tensor_copy(hit[:, 0:E1, :], above.rearrange("p t e -> p e t")).then_inc(r_hit, 1)
                V.tensor_tensor(tie, prob, level, ALU.is_equal)
                V.tensor_tensor(eqb[:, :, :], prob, level, ALU.is_equal).then_inc(r_eq, 1)
                dve.wait_ge(r_cnt, SEARCH + 1)
                then(V.tensor_reduce(cnt[:, 0, :], bank[6][:, 0:E1 * NT].rearrange("p (a t) -> p a t", t=NT), AX.X, ALU.add))
                then(V.tensor_scalar(acc[:, 0, :], cnt[:, 0, :], -1.0, float(CAP), ALU.mult, ALU.add))
                dve.wait_ge(r_pre, 1)
                then(V.tensor_tensor(ahead, bank[7][:, 0:NT * E1].rearrange("p (t e) -> p t e", e=E1),
                                     per_col(acc[:, 0, :], NT), ALU.is_lt))
                then(V.tensor_tensor(ahead, ahead, tie, ALU.mult))
                then(V.tensor_tensor(above, above, ahead, ALU.add))
                then(V.tensor_reduce(rv[:, 5, :], above, AX.X, ALU.max))
                then(V.tensor_tensor(tie, above, per_row(rv[:, 5, :], E1), ALU.subtract))
                then(V.scalar_tensor_tensor(tie, tie, 4.0, prob, ALU.mult, ALU.add))
                first_max(tie, ahead, slice(0, NT))
                then(V.tensor_tensor(rt[:, 9, :, :], ahead, prob, ALU.mult))

            def add_expert(e):
                for t in range(NT):
                    if t % HT == 0:
                        dve.wait_ge(m_ys, 2 * e + t // HT + 1)
                    last = V.scalar_tensor_tensor(X[:, t, :], ys[:, e, t, :], rt[:, 9, t, e:e + 1], X[:, t, :],
                                                  ALU.mult, ALU.add)
                    if e == E1 - 1:
                        last.then_inc(m_done, 1)
                if e < E1 - 1:
                    then(last)

            for n in range(B + 4):
                if n >= 4:
                    normalise(n - 4)
                if n < B:
                    subtract_max(n)
                if n == HB + 4:
                    outputs_by_feature(0)
                if n == B + 1:
                    add_attention(0)
                    ln_moments(1, 0)
                if n == B + 2:
                    root_guess(0)
                    root_third(0)
                if n == B + 3:
                    root_second(0)
            ln_apply(1, 0)
            outputs_by_feature(1)
            cross0_sub(0)
            cross0_prob(0)
            mask_context()
            cross0_add(0)
            layernorm(2, 0)
            add_attention(1)
            ln_moments(1, 1)
            root(1)
            ln_apply(1, 1)
            gate_sub(0)
            gate0(0, 0)
            gate_first(0)
            for e in range(E0 + 1):
                if e == 2:
                    cross0_prob(1)
                if e == 4:
                    cross0_add(1)
                gate0((0, 1)[e == E0], (e + 1) % (E0 + 1))
                if e == 0:
                    gate_second(0)
                if e == 1:
                    cross0_sub(1)
                if e == 4:
                    ln_moments(2, 1)
                    root_guess(1)
                if e == 5:
                    root_third(1)
                    root_second(1)
                if e == 6:
                    ln_apply(2, 1)
                if e == 7:
                    gate_sub(1)
                if e == 8:
                    gate_first(1)
            for e in range(E0 + 1):
                if e == 4:
                    state(0, 0)
                if e == 5:
                    state(0, 2)
                    state(0, 3)
                if e == 6:
                    state(0, 5)
                    state(0, 6)
                if e < E0:
                    gate0(1, e + 1)
                if e == 0:
                    gate_second(1)
                if e == 1:
                    ln_moments(3, 0)
                    root_guess(0)
                if e == 2:
                    root_third(0)
                    root_second(0)
                    ln_apply(3, 0)
                if e == 4:
                    state(0, 1)
                if e == 5:
                    state(0, 4)
                if e == 7:
                    states_moments(0)
                    root_guess(0)
            root_third(0)
            root_second(0)
            states_apply(0)
            layernorm(3, 1)
            affine_states(0)
            for step in range(6):
                if step == 1:
                    state(1, 0)
                if step == 3:
                    state(1, 1)
                if step == 5:
                    state(1, 2)
                add_states(0, step)
            ln_moments(4, 0)
            state(1, 3)
            root_guess(0)
            state(1, 4)
            root_third(0)
            state(1, 5)
            root_second(0)
            state(1, 6)
            ln_apply(4, 0)
            norm_states(1)
            affine_states(1)
            subtract_max1(0)
            for step in range(3):
                add_states(1, step)
            probs1(0)
            subtract_max1(1)
            for step in range(3, 6):
                add_states(1, step)
            probs1(1)
            subtract_max1(2)
            ln_moments(4, 1)
            root(1)
            probs1(2)
            subtract_max1(3)
            ln_apply(4, 1)
            for t in range(HT, NT + 4):
                if t - 1 < NT:
                    probs1(t - 1)
                if t < NT:
                    subtract_max1(t)
                if t >= 4:
                    add1(t - 4)
                if t == NT - 1:
                    ln_moments(5, 0)
                if t == NT:
                    root(0)
                if t == NT + 1:
                    ln_apply(5, 0)
            layernorm(5, 1)
            search_bits()
            route()
            for e in range(E1):
                add_expert(e)


_NAMES = ["x", "ctx_768", "mask_BxS2_bk0", "L0_attn_qkv_kernel", "L0_attn_qkv_bias", "L0_xattn_Wq", "L0_xattn_bq",
          "L0_xattn_Wk", "L0_xattn_bk", "L0_xattn_Wv", "L0_xattn_bv", "L0_ffn_gate_w", "L0_ffn_w1", "L0_ffn_b1",
          "L0_ffn_w2", "L0_ffn_b2", "L0_ffn_w3", "L0_ffn_b3", "L0_ffn_sw1", "L0_ffn_sb1", "L0_ffn_sw2", "L0_ffn_sb2",
          "L0_ffn_sw3", "L0_ffn_sb3", "L1_attn_A", "L1_attn_B", "L1_attn_C", "L1_attn_gamma", "L1_attn_beta",
          "L1_xattn_W_q", "L1_xattn_W_k", "L1_xattn_W_v", "L1_xattn_W_o", "L1_xattn_b_o", "L1_ffn_Wg", "L1_ffn_W1",
          "L1_ffn_W2"]


def kernel(**inputs):
    import numpy as np
    import concourse.bacc as bacc
    from concourse import mybir as _mybir
    from concourse.bass_utils import run_bass_kernel_spmd

    nc = bacc.Bacc("TRN2", target_bir_lowering=False, num_devices=1)
    arrays, w = {}, {}
    for name in _NAMES:
        a = np.ascontiguousarray(inputs[name])
        arrays[f"in_{name}"] = a
        w[name] = nc.dram_tensor(f"in_{name}", a.shape, _mybir.dt.from_np(a.dtype), kind="ExternalInput").ap()
    out = nc.dram_tensor("out", arrays["in_x"].shape, _mybir.dt.float32, kind="ExternalOutput").ap()
    decoder_kernel(nc, w, out)
    r = run_bass_kernel_spmd(nc, [arrays], core_ids=[0])
    return r.results[0]["out"]
```
